# Optimizing a Trainium2 kernel written in Bass

```python
import numpy as np
import jax
import jax.numpy as jnp

def _softmax(x, axis=-1):
    return jax.nn.softmax(x, axis=axis)

def _gelu(x):
    return jax.nn.gelu(x, approximate=True)

def _silu(x):
    return jax.nn.silu(x)

def _sigmoid(x):
    return jax.nn.sigmoid(x)

def _layernorm(x, axis=-1, eps=1e-05):
    m = jnp.mean(x, axis=axis, keepdims=True)
    v = jnp.var(x, axis=axis, keepdims=True)
    return (x - m) / jnp.sqrt(v + eps)

def _scatter_add(tgt, idx, src, axis=0):
    return tgt.at[idx].add(src)

def _segment_sum(src, seg, n):
    return jax.ops.segment_sum(src, seg, n)
kernel_name = 'mk_gnn_resnorm_d2_gnn_r64_54256d'

def setup_inputs(seed: int=0):
    np.random.seed(seed)
    _w = jnp.asarray

    def _rec_inputs():
        import jax
        import jax.numpy as jnp
        _gk = jax.random.key(seed)
        x = -0.0003713 + 1 * jax.random.normal(jax.random.fold_in(_gk, 1), (100000, 128), jnp.float32)
        src = jax.random.randint(jax.random.fold_in(_gk, 2), (25000,), 0, 100000, jnp.int32)
        dst = jnp.minimum((100000 * jax.random.uniform(jax.random.fold_in(_gk, 3), (25000,)) ** 2.0).astype(jnp.int32), 99999)
        _o = jnp.argsort(dst, stable=True)
        src = src[_o]
        dst = dst[_o]
        edge_weight = jax.random.uniform(jax.random.fold_in(_gk, 13), (25000,), jnp.float32, 0.0, 0.999998)
        return (x, src, dst, edge_weight)
    x, src, dst, edge_weight = _rec_inputs()

    def _L0_gnn_setup():
        import jax, jax.numpy as jnp
        import numpy as np
        N, E = (100000, 25000)
        NFEAT, NHID, HEADS = (128, 128, 2)
        FOUT = NHID // 2
        NEG_SLOPE = 0.2
        LN_EPS = 1e-05
        key = jax.random.key(seed)
        ks = jax.random.split(key, 10)
        h = jax.random.normal(ks[0], (N, NFEAT), dtype=jnp.float32)
        src = jax.random.randint(ks[1], (E,), 0, N, dtype=jnp.int32)
        dst = jax.random.randint(ks[2], (E,), 0, N, dtype=jnp.int32)
        W = jax.random.normal(ks[3], (NFEAT, HEADS * FOUT), dtype=jnp.float32) / np.sqrt(NFEAT)
        attn_l = jax.random.normal(ks[4], (HEADS, FOUT), dtype=jnp.float32) * 0.1
        attn_r = jax.random.normal(ks[5], (HEADS, FOUT), dtype=jnp.float32) * 0.1
        bias = jnp.zeros((HEADS * FOUT,), dtype=jnp.float32)
        gamma = jnp.ones((NHID,), dtype=jnp.float32)
        beta = jnp.zeros((NHID,), dtype=jnp.float32)
        return {'h': h, 'src': src, 'dst': dst, 'W': W, 'attn_l': attn_l, 'attn_r': attn_r, 'bias': bias, 'gamma': gamma, 'beta': beta}
    _L0_gnn_all = _L0_gnn_setup()
    _L0_gnn_in = {k: v for k, v in _L0_gnn_all.items() if k in ('W', 'attn_l', 'attn_r', 'bias', 'gamma', 'beta')}
    del _L0_gnn_all

    def _L1_gnn_setup():
        import jax, jax.numpy as jnp
        import numpy as np
        N, E, H = (50000, 12500, 128)
        LN_EPS = 1e-05

        def layer_norm(x, gamma, beta):
            mu = jnp.mean(x, axis=-1, keepdims=True)
            var = jnp.mean((x - mu) ** 2, axis=-1, keepdims=True)
            return (x - mu) * jax.lax.rsqrt(var + LN_EPS) * gamma + beta
        key = jax.random.key(seed)
        ks = jax.random.split(key, 8)
        sc = 1.0 / np.sqrt(2 * H)
        return {'x': jax.random.normal(ks[0], (N, H), dtype=jnp.float32), 'edge_index': jax.random.randint(ks[1], (2, E), 0, N, dtype=jnp.int64), 'edge_weights': jax.random.uniform(ks[2], (E,), dtype=jnp.float32), 'msg_w': jax.random.normal(ks[3], (2 * H, H), dtype=jnp.float32) * sc, 'msg_b': jnp.zeros((H,), jnp.float32), 'msg_g': jnp.ones((H,), jnp.float32), 'msg_beta': jnp.zeros((H,), jnp.float32), 'upd_w': jax.random.normal(ks[4], (2 * H, H), dtype=jnp.float32) * sc, 'upd_b': jnp.zeros((H,), jnp.float32), 'upd_g': jnp.ones((H,), jnp.float32), 'upd_beta': jnp.zeros((H,), jnp.float32), 'gate_w': jax.random.normal(ks[5], (H, 1), dtype=jnp.float32) / np.sqrt(H), 'gate_b': jnp.zeros((1,), jnp.float32)}
    _L1_gnn_all = _L1_gnn_setup()
    _L1_gnn_in = {k: v for k, v in _L1_gnn_all.items() if k in ('msg_w', 'msg_b', 'msg_g', 'msg_beta', 'upd_w', 'upd_b', 'upd_g', 'upd_beta', 'gate_w', 'gate_b')}
    del _L1_gnn_all
    return {'x': x, 'src': src, 'dst': dst, 'edge_weight': edge_weight, 'L0_gnn_W': _L0_gnn_in['W'], 'L0_gnn_attn_l': _L0_gnn_in['attn_l'], 'L0_gnn_attn_r': _L0_gnn_in['attn_r'], 'L0_gnn_bias': _L0_gnn_in['bias'], 'L0_gnn_gamma': _L0_gnn_in['gamma'], 'L0_gnn_beta': _L0_gnn_in['beta'], 'L1_gnn_msg_w': _L1_gnn_in['msg_w'], 'L1_gnn_msg_b': _L1_gnn_in['msg_b'], 'L1_gnn_msg_g': _L1_gnn_in['msg_g'], 'L1_gnn_msg_beta': _L1_gnn_in['msg_beta'], 'L1_gnn_upd_w': _L1_gnn_in['upd_w'], 'L1_gnn_upd_b': _L1_gnn_in['upd_b'], 'L1_gnn_upd_g': _L1_gnn_in['upd_g'], 'L1_gnn_upd_beta': _L1_gnn_in['upd_beta'], 'L1_gnn_gate_w': _L1_gnn_in['gate_w'], 'L1_gnn_gate_b': _L1_gnn_in['gate_b']}

def reference(x, src, dst, edge_weight, L0_gnn_W, L0_gnn_attn_l, L0_gnn_attn_r, L0_gnn_bias, L0_gnn_gamma, L0_gnn_beta, L1_gnn_msg_w, L1_gnn_msg_b, L1_gnn_msg_g, L1_gnn_msg_beta, L1_gnn_upd_w, L1_gnn_upd_b, L1_gnn_upd_g, L1_gnn_upd_beta, L1_gnn_gate_w, L1_gnn_gate_b):
    import jax
    import jax.numpy as jnp

    def _L0_gnn_ref(h, src, dst, W, attn_l, attn_r, bias, gamma, beta):
        import jax, jax.numpy as jnp
        import numpy as np
        N, E = (100000, 25000)
        NFEAT, NHID, HEADS = (128, 128, 2)
        FOUT = NHID // 2
        NEG_SLOPE = 0.2
        LN_EPS = 1e-05
        feat = (h @ W).reshape(N, HEADS, FOUT)
        el = jnp.einsum('nhf,hf->nh', feat, attn_l)
        er = jnp.einsum('nhf,hf->nh', feat, attn_r)
        e = jax.nn.leaky_relu(el[src] + er[dst], NEG_SLOPE)
        emax = jax.ops.segment_max(e, dst, num_segments=N)
        expe = jnp.exp(e - emax[dst])
        denom = jax.ops.segment_sum(expe, dst, num_segments=N)
        alpha = expe / denom[dst]
        msg = feat[src] * alpha[:, :, None]
        out = jax.ops.segment_sum(msg, dst, num_segments=N)
        x = out.reshape(N, HEADS * FOUT) + bias
        mu = jnp.mean(x, axis=-1, keepdims=True)
        var = jnp.mean(jnp.square(x - mu), axis=-1, keepdims=True)
        return gamma * (x - mu) * jax.lax.rsqrt(var + LN_EPS) + beta

    def _L1_gnn_ref(x, edge_index, edge_weights, msg_w, msg_b, msg_g, msg_beta, upd_w, upd_b, upd_g, upd_beta, gate_w, gate_b):
        import jax, jax.numpy as jnp
        import numpy as np
        N, E, H = (50000, 12500, 128)
        LN_EPS = 1e-05

        def layer_norm(x, gamma, beta):
            mu = jnp.mean(x, axis=-1, keepdims=True)
            var = jnp.mean((x - mu) ** 2, axis=-1, keepdims=True)
            return (x - mu) * jax.lax.rsqrt(var + LN_EPS) * gamma + beta
        num_nodes = x.shape[0]
        src, dst = (edge_index[0], edge_index[1])
        em = jnp.concatenate([x[src], x[dst]], axis=-1)
        em = jax.nn.relu(layer_norm(em @ msg_w + msg_b, msg_g, msg_beta))
        em = em * edge_weights[:, None]
        msgs = jax.ops.segment_sum(em, dst, num_segments=num_nodes)
        counts = jax.ops.segment_sum(jnp.ones((src.shape[0], 1), x.dtype), dst, num_segments=num_nodes)
        valid = (counts > 0).astype(x.dtype)
        messages = msgs / (counts + 1e-08) * valid
        gate = jax.nn.sigmoid(x @ gate_w + gate_b)
        combined = jnp.concatenate([x, messages], axis=-1)
        h_new = jax.nn.relu(layer_norm(combined @ upd_w + upd_b, upd_g, upd_beta))
        return gate * h_new + (1.0 - gate) * x
    edge_index = jnp.stack([src, dst])
    x = _layernorm(x + _L0_gnn_ref(x, src, dst, L0_gnn_W, L0_gnn_attn_l, L0_gnn_attn_r, L0_gnn_bias, L0_gnn_gamma, L0_gnn_beta), axis=-1)
    x = _layernorm(x + _L1_gnn_ref(x, edge_index, edge_weight, L1_gnn_msg_w, L1_gnn_msg_b, L1_gnn_msg_g, L1_gnn_msg_beta, L1_gnn_upd_w, L1_gnn_upd_b, L1_gnn_upd_g, L1_gnn_upd_beta, L1_gnn_gate_w, L1_gnn_gate_b), axis=-1)
    return x

_drawn_inputs = setup_inputs


def setup_inputs(seed=0):
    import zlib

    import numpy as np

    out = dict(_drawn_inputs(seed))
    spreads = {'L0_gnn_bias': (0.0, 0.1),
     'L0_gnn_gamma': (1.0, 0.2),
     'L0_gnn_beta': (0.0, 0.1),
     'L1_gnn_msg_b': (0.0, 0.8),
     'L1_gnn_msg_g': (1.0, 0.6),
     'L1_gnn_msg_beta': (0.0, 0.8),
     'L1_gnn_upd_b': (0.0, 0.375),
     'L1_gnn_upd_g': (1.0, 0.2),
     'L1_gnn_upd_beta': (0.0, 0.56)}
    factors = {'edge_weight': 3.018, 'L0_gnn_attn_r': 3.356}
    for name, (base, spread) in spreads.items():
        noise = np.random.default_rng([zlib.crc32(name.encode()), seed]).standard_normal(out[name].shape)
        drawn = base * np.exp(spread * noise) if base else spread * noise
        out[name] = jnp.asarray(drawn.astype(out[name].dtype))
    for name, factor in factors.items():
        out[name] = (out[name] * factor).astype(out[name].dtype)
    return out
```

```python
import concourse.bass as bass
from concourse import mybir
from contextlib import ExitStack


def gnn_resnorm_kernel(nc, x, src, dst, edge_weight, gat_w, attn_l, attn_r, gat_bias, gat_gamma, gat_beta,
                       msg_w, msg_b, msg_g, msg_beta, upd_w, upd_b, upd_g, upd_beta, gate_w, gate_b, out):
    f32 = mybir.dt.float32
    i32 = mybir.dt.int32
    bf16 = mybir.dt.bfloat16
    ALU = mybir.AluOpType
    ACT = mybir.ActivationFunctionType
    X = mybir.AxisListType.X

    N, F = x.shape
    E = src.shape[0]
    HEADS, FO = attn_l.shape
    EP = 125
    EJ = E // EP
    assert E == EP * EJ and EJ % 8 == 0 and F == 128 and HEADS * FO == F
    NP = 128
    T = 8
    CHUNK = NP * T
    CHUNKS = -(-N // CHUNK)
    LAST_START = N - CHUNK
    QT = 4
    EG = EJ // QT
    EPS = 1e-5
    BIG = 1e30
    GATE_CAP = 1e8
    SKIP = 1 << 20
    UNROLL = 4

    xs_dram = nc.dram_tensor("xs_rows", (E, F), f32, kind="Internal").ap()
    xd_dram = nc.dram_tensor("xd_rows", (E, F), f32, kind="Internal").ap()
    g_dram = nc.dram_tensor("g_rows", (E + 1, F), f32, kind="Internal").ap()
    x1_dram = nc.dram_tensor("x1_rows", (E, F), f32, kind="Internal").ap()

    def edge_rows(table, j, k):
        return table[0:E, :].rearrange("(p j) f -> p j f", j=EJ)[:, bass.ds(j, k), :]

    def node_rows(table, start):
        return table[bass.ds(start, CHUNK), :].rearrange("(p k) f -> p k f", k=T)

    ctx = ExitStack()
    with ctx:
        def sb(name, shape, dt=f32):
            return ctx.enter_context(nc.sbuf_tensor(name, shape, dt))

        def pb(name, shape, dt=f32):
            return ctx.enter_context(nc.psum_tensor(name, shape, dt))

        def sem(name):
            return ctx.enter_context(nc.semaphore(name))

        edge_feat = sb("edge_feat", [EP, EJ * F])
        arena = sb("arena", [128, 12800])
        ident = sb("ident", [128, 128])
        ones = sb("ones", [128, 128])
        ones_bf = sb("ones_bf", [128, 1], bf16)
        eps_col = sb("eps_col", [128, 1])
        w_gat = sb("w_gat", [F, F])
        w_ma, w_mb, w_ut, w_ub = (sb(n, [F, F]) for n in ("w_ma", "w_mb", "w_ut", "w_ub"))
        w_mag, w_mbg, w_utg, w_ubg = (sb(n, [F, F]) for n in ("w_mag", "w_mbg", "w_utg", "w_ubg"))
        v_el, v_er = sb("v_el", [F, HEADS]), sb("v_er", [F, HEADS])
        bc = {n: sb("bc_" + n, [128, F]) for n in ("al", "ar", "bias", "gamma", "beta", "mb", "mg", "mbeta",
                                                   "ub", "ug", "ubeta", "c")}
        mb_col, ub_col, gw_col = sb("mb_col", [F, 1]), sb("ub_col", [F, 1]), sb("gw_col", [F, 1])
        gb_bc, ngb = sb("gb_bc", [128, 1]), sb("ngb", [128, 1])
        src_i, dst_i = sb("src_i", [EP, EJ], i32), sb("dst_i", [EP, EJ], i32)
        src_f, dst_f = sb("src_f", [EP, EJ]), sb("dst_f", [EP, EJ])
        w_edge = sb("w_edge", [EP, EJ])
        same = sb("same", [EP, EJ])
        first = sb("first", [EP, EJ])
        pen_f, pen_b = sb("pen_f", [EP, EJ]), sb("pen_b", [EP, EJ])
        same_n = sb("same_n", [EP, EJ])
        pen_first, pen_last = sb("pen_first", [EP, EJ]), sb("pen_last", [EP, EJ])
        in_last = sb("in_last", [EP, EJ])
        cross = sb("cross", [EP, 4, EP])
        cross_pen = sb("cross_pen", [EP, 4, EP])
        cross_sum = sb("cross_sum", [EP, 2, EP])
        carry_lhs = sb("carry_lhs", [EP, EP])
        nz = sb("nz", [EP, 1])
        alpha = sb("alpha", [EP, EJ * HEADS])
        rcnt = sb("rcnt", [EP, EJ])
        g_idx, x1_idx, out_idx = (sb(n, [EP, EJ], i32) for n in ("g_idx", "x1_idx", "out_idx"))
        carry = sb("carry", [EP, F])
        sc = [sb(f"sc{n}", [EP, EJ]) for n in range(6)]
        small = sb("small", [128, 16])

        bank = [pb(f"bank{n}", [128, 512]) for n in range(8)]

        class Chain:

            def __init__(self, eng, s, per_run, run, already=0):
                self.eng, self.s, self.per_run, self.base, self.k = eng, s, per_run, run * per_run, already

            def __call__(self, ins):
                self.k += 1
                ins.then_inc(self.s, 1)
                self.eng.wait_ge(self.s, self.base + self.k)

            def end(self):
                assert self.k == self.per_run, (self.k, self.per_run)

        s_line = sem("vector_line")
        s_go = sem("rows_may_move")
        line = [0]

        def link(ins):
            line[0] += 1
            ins.then_inc(s_line, 1)
            nc.vector.wait_ge(s_line, line[0])

        def after(eng, s, count):
            if isinstance(count, int) and count <= 0:
                return
            eng.wait_ge(s, count)

        block_no = [None]

        def run_steps(eng, body, steps, full):
            blocks = full // UNROLL
            for i in range(UNROLL):
                body(i, i % UNROLL)
            with eng.Fori(1, blocks) as b:
                block_no[0] = b
                for u in range(UNROLL):
                    body(b * UNROLL + u, u)
            for i in range(blocks * UNROLL, steps):
                body(i, i % UNROLL)

        def steps2(eng, body):
            run_steps(eng, body, STEPS, 96)

        def half(i, slot):
            if isinstance(i, int):
                return i // 2 + 1
            return block_no[0] * 2 + slot // 2 + 1

        def quarter_of(i, slot):
            if isinstance(i, int):
                return i // UNROLL + 1
            return block_no[0] + 1

        def on(i, count, lag=0):
            return not isinstance(i, int) or 0 <= i - lag < count

        def bcast(row, parts, k):
            return row[0:parts, :].rearrange("p (a f) -> p a f", a=1).to_broadcast([parts, k, F])

        def stats_to_var(dve, link, st, sm, parts, k):
            s, d, v, v128 = (sm[0:parts, q, 0:k] for q in range(4))
            st = st[0:parts, 0:k, :]
            nc.vector.tensor_tensor(s, st[:, :, 1], st[:, :, 4], ALU.add)
            nc.vector.tensor_tensor(d, st[:, :, 1], st[:, :, 4], ALU.subtract)
            link(nc.vector.tensor_tensor(v, st[:, :, 2], st[:, :, 5], ALU.add))
            link(nc.vector.tensor_tensor(d, d, d, ALU.mult))
            return nc.vector.scalar_tensor_tensor(out=v128, in0=d, scalar=float(F // 4), in1=v,
                                                  op0=ALU.mult, op1=ALU.add)

        s_ld, s_nx, s_pool0, s_p0, s_st, s_row0 = (sem(n) for n in (
            "setup_loaded", "next_cleared", "ident_ready", "setup_rows", "c_row_stored", "rows_read"))
        src_all = edge_feat[:, 0:E].bitcast(i32)
        dprev = sc[0][:, :].bitcast(i32)
        dnext = small[:, 8:9].bitcast(i32)
        dgT = arena[0:EP, 0:EP]
        n_loads = [0]
        with nc.Block() as block:
            @block.sync
            def _(sp):
                def load(dst_ap, src_ap):
                    n_loads[0] += 1
                    sp.dma_start(dst_ap, src_ap, allow_slow_non_contiguous=True).then_inc(s_ld, 16)

                load(dst_i[:, :], dst.rearrange("(p j) -> p j", j=EJ))
                load(src_i[:, :], src.rearrange("(p j) -> p j", j=EJ))
                for w, d in ((gat_w, w_gat), (msg_w[0:F, :], w_ma), (msg_w[F:2 * F, :], w_mb),
                             (upd_w[0:F, :], w_ut), (upd_w[F:2 * F, :], w_ub)):
                    load(d[:, :], w)
                rows = (("al", attn_l.rearrange("h f -> (h f)")), ("ar", attn_r.rearrange("h f -> (h f)")),
                        ("bias", gat_bias), ("gamma", gat_gamma), ("beta", gat_beta), ("mb", msg_b), ("mg", msg_g),
                        ("mbeta", msg_beta), ("ub", upd_b), ("ug", upd_g), ("ubeta", upd_beta))
                for name, v in rows:
                    load(bc[name][:, :], v.partition_broadcast(128))
                load(mb_col[:, :], msg_b.rearrange("(f a) -> f a", a=1))
                load(ub_col[:, :], upd_b.rearrange("(f a) -> f a", a=1))
                load(gw_col[:, :], gate_w)
                load(gb_bc[:, :], gate_b.partition_broadcast(128))
                load(w_edge[:, :], edge_weight.rearrange("(p j) -> p j", j=EJ))
                load(dprev[1:EP, :], dst[0:E - EJ].rearrange("(p j) -> p j", j=EJ))
                quarter = E // 4
                for q in range(4):
                    load(src_all[:, q * quarter:(q + 1) * quarter],
                         src[q * quarter:(q + 1) * quarter].partition_broadcast(EP))
                sp.wait_ge(s_nx, 1)
                load(dnext[0:EP - 1, :], dst[EJ:E].rearrange("(p j) -> p j", j=EJ)[:, 0:1])
            LOADED = 16 * n_loads[0]

            @block.gpsimd
            def _(pool):
                nc.gpsimd.memset(ident[:, :], 0.0).then_inc(s_pool0, 1)
                pool.wait_ge(s_pool0, 1)
                nc.gpsimd.affine_select(out=ident[:, :], in_=ident[:, :], compare_op=ALU.not_equal, fill=1.0,
                                        base=0, pattern=[[-1, 128]], channel_multiplier=1).then_inc(s_pool0, 1)
                nc.gpsimd.iota(sc[1][:, :].bitcast(i32), pattern=[[1, EJ]], base=0,
                               channel_multiplier=EJ).then_inc(s_pool0, 1)
                pool.wait_ge(s_p0, 3)
                nc.gpsimd.affine_select(out=carry_lhs[:, :], in_=carry_lhs[:, :], compare_op=ALU.is_gt, fill=0.0,
                                        base=0, pattern=[[1, EP]], channel_multiplier=-1).then_inc(s_pool0, 1)

            @block.tensor
            def _(pe):
                pe.wait_ge(s_p0, 1)
                nc.tensor.matmul(bank[0][0:EP, 0:EP], ones[0:EP, 0:EP], arena[0:EP, 0:EP], start=True,
                                 stop=True).then_inc(s_row0, 1)
                pe.wait_ge(s_p0, 2)
                nc.tensor.matmul(bank[1][0:EP, 0:EP], ones[0:EP, 0:EP], arena[0:EP, 128:128 + EP], start=True,
                                 stop=True).then_inc(s_row0, 1)

            @block.scalar
            def _(act):
                act.preload_act_table_set("natural_log_exp_and_others")
                act.wait_ge(s_p0, 4)
                nc.scalar.activation(small[:, 4:5], small[:, 3:4], ACT.Ln, bias=eps_col[:, :],
                                     scale=1.0 / F).then_inc(s_st, 1)
                act.wait_ge(s_st, 1)
                nc.scalar.activation(small[:, 5:6], small[:, 4:5], ACT.Exp, scale=-0.5).then_inc(s_st, 1)

            @block.vector
            def _(dve):
                V = nc.vector
                V.memset(ones[:, :], 1.0)
                V.memset(ones_bf[:, :], 1.0)
                V.memset(eps_col[:, :], EPS)
                link(V.memset(dprev[0:1, :], 0))
                V.memset(small[:, 8:9], -1.0).then_inc(s_nx, 1)
                dve.wait_ge(s_ld, LOADED)
                dve.wait_ge(s_pool0, 3)
                link(V.tensor_copy(src_f[:, :], src_i[:, :]))
                link(V.tensor_copy(dst_f[:, :], dst_i[:, :]))
                link(V.tensor_copy(sc[1][:, :], sc[1][:, :].bitcast(i32)))
                fd, ld = dst_f[:, 0:1], dst_f[:, EJ - 1:EJ]
                V.tensor_scalar(arena[0:EP, 0:EP], ident[0:EP, 0:EP], fd, None, ALU.mult).then_inc(s_p0, 1)
                V.tensor_scalar(arena[0:EP, 128:128 + EP], ident[0:EP, 0:EP], ld, None, ALU.mult).then_inc(s_p0, 1)
                for row, v in (("al", v_el), ("ar", v_er)):
                    tmp = arena[:, 256:256 + F]
                    link(V.tensor_tensor(tmp, w_gat[:, :], bc[row][:, :], ALU.mult))
                    link(V.tensor_reduce(v[:, :], tmp.rearrange("p (h f) -> p h f", h=HEADS), X, ALU.add))
                for w, wg, gain in ((w_ma, w_mag, "mg"), (w_mb, w_mbg, "mg"), (w_ut, w_utg, "ug"), (w_ub, w_ubg, "ug")):
                    link(V.tensor_reduce(small[:, 0:1], w[:, :], X, ALU.add))
                    link(V.tensor_scalar(small[:, 1:2], small[:, 0:1], 1.0 / F, None, ALU.mult))
                    link(V.tensor_scalar(w[:, :], w[:, :], small[:, 1:2], None, ALU.subtract))
                    link(V.tensor_tensor(wg[:, :], w[:, :], bc[gain][:, :], ALU.mult))
                for row, col, gain in (("mb", mb_col, "mg"), ("ub", ub_col, "ug")):
                    link(V.tensor_reduce(small[:, 0:1], bc[row][:, :], X, ALU.add))
                    link(V.tensor_scalar(small[:, 1:2], small[:, 0:1], 1.0 / F, None, ALU.mult))
                    link(V.tensor_scalar(col[:, :], col[:, :], small[:, 1:2], None, ALU.subtract))
                    link(V.tensor_scalar(bc[row][:, :], bc[row][:, :], small[:, 1:2], None, ALU.subtract))
                    link(V.tensor_tensor(bc[row][:, :], bc[row][:, :], bc[gain][:, :], ALU.mult))
                V.tensor_scalar(ngb[:, :], gb_bc[:, :], -1.0, None, ALU.mult)
                link(V.bn_stats(small[:, 9:15], bc["bias"][:, :]))
                st = small[:, 9:15]
                V.tensor_tensor(small[:, 0:1], st[:, 1:2], st[:, 4:5], ALU.add)
                V.tensor_tensor(small[:, 1:2], st[:, 1:2], st[:, 4:5], ALU.subtract)
                link(V.tensor_tensor(small[:, 2:3], st[:, 2:3], st[:, 5:6], ALU.add))
                link(V.tensor_tensor(small[:, 1:2], small[:, 1:2], small[:, 1:2], ALU.mult))
                dve.wait_ge(s_row0, 2)
                for n, (rows_, key) in enumerate(((0, fd), (1, fd), (0, ld), (1, ld))):
                    link(V.tensor_scalar(cross[:, n, :], bank[rows_][0:EP, 0:EP], key, None, ALU.is_equal))
                V.tensor_copy(carry_lhs[:, :], cross[:, 2, :]).then_inc(s_p0, 1)
                V.scalar_tensor_tensor(out=small[:, 3:4], in0=small[:, 1:2], scalar=float(F // 4),
                                       in1=small[:, 2:3], op0=ALU.mult, op1=ALU.add).then_inc(s_p0, 1)
                link(V.tensor_tensor(nz[:, :], fd, ld, ALU.not_equal))
                link(V.tensor_scalar(cross_pen[:, :, :], cross[:, :, :], -1.0, BIG, ALU.add, ALU.mult))
                link(V.tensor_scalar(cross_sum[:, 0, :], cross[:, 2, :], nz[:, :], None, ALU.mult))
                link(V.tensor_scalar(cross_sum[:, 1, :], cross[:, 3, :], nz[:, :], None, ALU.mult))
                link(V.memset(same[:, :], 0.0))
                link(V.memset(same_n[:, :], 0.0))
                link(V.tensor_tensor(same[:, 1:EJ], dst_f[:, 1:EJ], dst_f[:, 0:EJ - 1], ALU.is_equal))
                link(V.tensor_copy(same_n[:, 0:EJ - 1], same[:, 1:EJ]))
                link(V.tensor_scalar(first[:, :], dst_f[:, :], fd, None, ALU.is_equal))
                link(V.tensor_scalar(in_last[:, :], dst_f[:, :], ld, None, ALU.is_equal))
                for a, b in ((same, pen_f), (same_n, pen_b), (first, pen_first), (in_last, pen_last)):
                    link(V.tensor_scalar(b[:, :], a[:, :], -1.0, BIG, ALU.add, ALU.mult))
                last = sc[2]
                link(V.tensor_scalar(last[:, :], same_n[:, :], -1.0, 1.0, ALU.mult, ALU.add))
                link(V.tensor_copy(small[0:EP, 6:7], dnext[0:EP, :]))
                link(V.tensor_tensor(last[:, EJ - 1:EJ], small[0:EP, 6:7], ld, ALU.not_equal))
                link(V.scalar_tensor_tensor(out=sc[3][:, :], in0=dst_f[:, :], scalar=float(-SKIP), in1=last[:, :],
                                            op0=ALU.add, op1=ALU.mult))
                link(V.tensor_scalar(out_idx[:, :], sc[3][:, :], float(SKIP), None, ALU.add))
                dve.wait_ge(s_st, 2)
                link(V.scalar_tensor_tensor(out=small[:, 2:3], in0=small[:, 0:1], scalar=-0.5, in1=small[:, 5:6],
                                            op0=ALU.mult, op1=ALU.mult))
                link(V.tensor_scalar(bc["c"][:, :], bc["bias"][:, :], small[:, 5:6], small[:, 2:3], ALU.mult, ALU.add))
                link(V.tensor_tensor(bc["c"][:, :], bc["c"][:, :], bc["gamma"][:, :], ALU.mult))
                link(V.tensor_tensor(bc["c"][:, :], bc["c"][:, :], bc["beta"][:, :], ALU.add))

        above = arena[:, :].bitcast(bf16)[0:EP, 0:E].rearrange("k (j p) -> k j p", p=EP)
        step_hi, step_lo = (sb(n, [EP, EJ], bf16) for n in ("step_hi", "step_lo"))
        s_sp, s_sr, s_sc, s_ss, s_sb, s_cst = (sem(n) for n in (
            "search_ready", "row_fetched", "row_counted", "row_signed", "search_done",
            "c_stored"))
        junk_d, junk_a = (sb(n, [EP, 4, EJ], bf16) for n in ("junk_d", "junk_a"))
        qm = sc[4]
        cle, sgn = sc[2], sc[3]
        with nc.Block() as block:
            @block.vector
            def _(dve):
                V = nc.vector
                link(V.tensor_copy(sc[5][:, :], dprev[:, :]))
                link(V.tensor_tensor(sc[2][:, :], dst_f[:, :], sc[5][:, :], ALU.subtract))
                link(V.tensor_scalar(sc[3][:, :], sc[2][:, :], 1.0 / 512, float(3 << 22), ALU.mult, ALU.add))
                link(V.tensor_scalar(sc[3][:, :], sc[3][:, :], float(-(3 << 22)), 512.0, ALU.add, ALU.mult))
                link(V.tensor_copy(step_hi[:, :], sc[3][:, :]))
                link(V.tensor_tensor(step_lo[:, :], sc[2][:, :], sc[3][:, :], ALU.subtract))
                link(V.tensor_scalar(qm[:, :], src_f[:, :], -0.5, None, ALU.add))
                part = EJ // 5
                for q in range(5):
                    view = src_all.rearrange("k (p j) -> k j p", j=EJ)[:, q * part:(q + 1) * part, :]
                    ins = V.tensor_scalar(above[:, q * part:(q + 1) * part, :], view, dst_f[:, 0:1], None, ALU.is_ge)
                    ins.then_inc(s_sp, 1)
                def count(b, u):
                    i = b * 4 + u
                    dve.wait_ge(s_sr, i + 1)
                    V.tensor_scalar(junk_d[:, u, :], bank[u][0:EP, 0:EJ], src_f[:, bass.ds(i, 1)],
                                    None, ALU.is_le, ALU.add, accum_out=cle[:, bass.ds(i, 1)]).then_inc(s_sc, 1)
                with dve.Fori(0, EJ // 4) as b:
                    for u in range(4):
                        count(b, u)
                dve.wait_ge(s_sc, EJ)
                dve.wait_ge(s_ss, EJ)
                dve.wait_ge(s_sb, EJ)
                part_no = sc[5]
                V.tensor_copy(part_no[:, :], bank[4][0:EP, 0:EJ])
                link(V.tensor_scalar(cle[:, :], cle[:, :], 1.0, None, ALU.mult))
                link(V.scalar_tensor_tensor(out=qm[:, :], in0=cle[:, :], scalar=2.0, in1=sgn[:, :], op0=ALU.mult,
                                            op1=ALU.subtract))
                link(V.tensor_scalar(qm[:, :], qm[:, :], float(EJ) + 0.5, None, ALU.is_gt))
                link(V.scalar_tensor_tensor(out=qm[:, :], in0=part_no[:, :], scalar=0.5, in1=qm[:, :], op0=ALU.is_gt,
                                            op1=ALU.mult))
                link(V.scalar_tensor_tensor(out=cle[:, :], in0=part_no[:, :], scalar=float(EJ), in1=cle[:, :],
                                            op0=ALU.mult, op1=ALU.add))
                link(V.scalar_tensor_tensor(out=cle[:, :], in0=cle[:, :], scalar=float(-EJ - 1 - E), in1=qm[:, :],
                                            op0=ALU.add, op1=ALU.mult))
                link(V.tensor_scalar(g_idx[:, :], cle[:, :], float(E), None, ALU.add))

            @block.scalar
            def _(act):
                act.preload_act_table_set("natural_log_exp_and_others")
                def signs(b, u):
                    i = b * 4 + u
                    act.wait_ge(s_sc, i + 1)
                    nc.scalar.activation(junk_a[:, u, :], bank[u][0:EP, 0:EJ], ACT.Sign, bias=qm[:, bass.ds(i, 1)], scale=-1.0,
                                         accum_out=sgn[:, bass.ds(i, 1)]).then_inc(s_ss, 1)
                act.wait_ge(s_sp, 5)
                with act.Fori(0, EJ // 4) as b:
                    for u in range(4):
                        signs(b, u)

            @block.tensor
            def _(pe):
                pe.wait_ge(s_sp, 5)

                def fetch(b, u, head):
                    i = b * 4 + u
                    if not head:
                        pe.wait_ge(s_ss, i - 3)
                    nc.tensor.matmul(bank[u][0:EP, 0:EJ], above[:, bass.ds(i, 1), :].rearrange("k a p -> k (a p)"),
                                     step_hi[:, :], start=True, stop=False)
                    nc.tensor.matmul(bank[u][0:EP, 0:EJ], above[:, bass.ds(i, 1), :].rearrange("k a p -> k (a p)"),
                                     step_lo[:, :], start=False, stop=True).then_inc(s_sr, 1)
                    nc.tensor.matmul(bank[4][0:EP, bass.ds(i, 1)],
                                     above[:, bass.ds(i, 1), :].rearrange("k a p -> k (a p)"),
                                     ones_bf[0:EP, :], start=True, stop=True).then_inc(s_sb, 1)
                for u in range(4):
                    fetch(0, u, True)
                with pe.Fori(1, EJ // 4) as b:
                    for u in range(4):
                        fetch(b, u, False)

            @block.sync
            def _(sp):
                sp.dma_start(g_dram[E:E + 1, :], bc["c"][0:1, :]).then_inc(s_cst, 16)
                sp.wait_ge(s_cst, 16)


        class Update:
            def __init__(self, tag, parts, k, x_of, z, xt, sq, m_of=None, mt=None, weights=None, gated=True):
                self.wx, self.wm, self.wxg, self.wmg, self.b_row, self.b_col, self.beta = \
                    weights or (w_ut, w_ub, w_utg, w_ubg, bc["ub"], ub_col, bc["ubeta"])
                self.gated = gated
                self.parts, self.k, self.groups, self.quad = parts, k, k // QT, QT * parts
                self.x_of, self.z, self.xt, self.sq, self.m_of, self.mt = x_of, z, xt, sq, m_of, mt
                names = ["x_ready", "transposed", "copied", "h_wide", "squared", "products", "scales", "scaled",
                         "chain_scales"]
                if gated:
                    names += ["relued", "y_stats", "y_rstd", "final", "chain_z", "chain_y", "chain_rstd", "chain_final"]
                self.s = {n: sem(f"{tag}_{n}") for n in names}
                self.scal = sb(f"{tag}_scal", [128, 8, 2, k])
                self.ysm, self.yst, self.ynb = sb(f"{tag}_ysm", [128, 4, k]), sb(f"{tag}_yst", [128, k, 6]), \
                    sb(f"{tag}_ynb", [128, k])

            LNH, EX, RS, KX, G2, GV, LNY, RY = range(8)

            def q(self, n, slot):
                return self.scal[0:self.parts, n, slot % 2, :]

            def col(self, what, slot):
                at = 32 * (slot % 2) + 16 * what
                return bank[5][0:self.parts, at:at + self.k]

            def pe_transpose(self, pe, i, slot):
                s, p = self.s, self.parts
                pe.wait_ge(s["x_ready"], i + 1)
                for g in range(self.groups):
                    after(pe, s["copied"], self.groups * (i - 1) + g + 1)
                    for t in range(QT):
                        ins = nc.tensor.transpose(bank[g][:, t * p:(t + 1) * p], self.x_of(slot)[:, g * QT + t, :],
                                                  ident[0:p, 0:p])
                    if self.m_of:
                        for t in range(QT):
                            ins = nc.tensor.transpose(bank[1][:, t * p:(t + 1) * p], self.m_of(slot)[:, t, :],
                                                      ident[0:p, 0:p])
                    ins.then_inc(s["transposed"], 1)

            def act_copy(self, act, i):
                s = self.s
                after(act, s["products"], i)
                for g in range(self.groups):
                    act.wait_ge(s["transposed"], self.groups * i + g + 1)
                    ins = nc.scalar.activation(self.xt[g][:, 0:self.quad], bank[g][:, 0:self.quad], ACT.Copy)
                    if self.m_of:
                        ins = nc.scalar.activation(self.mt[:, 0:self.quad], bank[1][:, 0:self.quad], ACT.Copy)
                    ins.then_inc(s["copied"], 1)

            def pe_products(self, pe, i, slot):
                s, p = self.s, self.parts
                for g in range(self.groups):
                    n = self.groups * i + g
                    pe.wait_ge(s["copied"], n + 1)
                    after(pe, s["squared"], n)
                    ins = nc.tensor.matmul(bank[2][:, 0:self.quad], self.wx[:, :], self.xt[g][:, 0:self.quad],
                                           start=True, stop=not self.m_of)
                    if self.m_of:
                        ins = nc.tensor.matmul(bank[2][:, 0:self.quad], self.wm[:, :], self.mt[:, 0:self.quad],
                                               start=False, stop=True)
                    ins.then_inc(s["h_wide"], 1)
                    if g == 0:
                        after(pe, s["scaled"], i)
                        after(pe, s["scales"], i)
                    for t in range(QT):
                        cut = slice(t * p, (t + 1) * p)
                        hg = bank[3 + g][0:p, t * F:(t + 1) * F]
                        nc.tensor.matmul(hg, self.xt[g][:, cut], self.wxg[:, :], start=True, stop=False)
                        if self.m_of:
                            nc.tensor.matmul(hg, self.mt[:, cut], self.wmg[:, :], start=False, stop=False)
                        nc.tensor.matmul(hg, ones[0:1, 0:p], self.b_row[0:1, :], start=False, stop=True)
                        if not self.gated:
                            continue
                        nc.tensor.matmul(self.col(1, slot)[:, g * QT + t:g * QT + t + 1], self.xt[g][:, cut],
                                         gw_col[:, :], start=True, stop=True)
                for g in range(self.groups):
                    pe.wait_ge(s["squared"], self.groups * i + g + 1)
                    for t in range(QT):
                        ins = nc.tensor.matmul(self.col(0, slot)[:, g * QT + t:g * QT + t + 1],
                                               self.sq[g][:, t * p:(t + 1) * p], ones[:, 0:1], start=True, stop=True)
                ins.then_inc(s["products"], 1)

            def act_square(self, act, i):
                s = self.s
                for g in range(self.groups):
                    act.wait_ge(s["h_wide"], self.groups * i + g + 1)
                    nc.scalar.activation(self.sq[g][:, 0:self.quad], bank[2][:, 0:self.quad], ACT.Square,
                                         bias=self.b_col[:, :]).then_inc(s["squared"], 1)

            def act_scales(self, act, i, slot):
                s = self.s
                link = Chain(act, s["chain_scales"], 1, i)
                act.wait_ge(s["products"], i + 1)
                if self.gated:
                    nc.scalar.activation(self.q(self.EX, slot), self.col(1, slot), ACT.Exp,
                                         bias=ngb[0:self.parts, :], scale=-1.0)
                link(nc.scalar.activation(self.q(self.LNH, slot), self.col(0, slot), ACT.Ln,
                                          bias=eps_col[0:self.parts, :], scale=1.0 / F))
                nc.scalar.activation(self.q(self.RS, slot), self.q(self.LNH, slot), ACT.Exp, scale=-0.5)\
                    .then_inc(s["scales"], 1)
                link.end()

            def dve_z(self, dve, i, slot):
                s, V = self.s, nc.vector
                link = Chain(dve, s["chain_z"], 3, i)
                dve.wait_ge(s["scales"], i + 1)
                for t in range(self.k):
                    g, u = t // QT, t % QT
                    ins = V.scalar_tensor_tensor(out=self.z[0:self.parts, t, :],
                                                 in0=bank[3 + g][0:self.parts, u * F:(u + 1) * F],
                                                 scalar=self.q(self.RS, slot)[:, t:t + 1], in1=self.beta[0:self.parts, :],
                                                 op0=ALU.mult, op1=ALU.add)
                ins.then_inc(s["scaled"], 1)
                g2, kx = self.q(self.G2, slot), self.q(self.KX, slot)
                link(V.tensor_scalar(g2, self.q(self.EX, slot), GATE_CAP, 2.0, ALU.min, ALU.mult))
                V.tensor_scalar(kx, g2, 1.0, None, ALU.add)
                link(V.tensor_scalar(g2, g2, 0.5, 1.0, ALU.mult, ALU.add))
                link(V.tensor_tensor(g2, g2, g2, ALU.mult))
                link.end()

            def act_relu(self, act, i):
                s = self.s
                act.wait_ge(s["scaled"], i + 1)
                z = self.z[0:self.parts, :, :]
                nc.scalar.activation(z, z, ACT.Relu).then_inc(s["relued"], 1)

            def dve_y(self, dve, i, slot):
                s, V = self.s, nc.vector
                link = Chain(dve, s["chain_y"], 5, i)
                dve.wait_ge(s["relued"], i + 1)
                xb = self.x_of(slot)
                for t in range(self.k):
                    ins = V.scalar_tensor_tensor(out=xb[:, t, :], in0=xb[:, t, :],
                                                 scalar=self.q(self.KX, slot)[:, t:t + 1],
                                                 in1=self.z[0:self.parts, t, :], op0=ALU.mult, op1=ALU.add)
                link(ins)
                for t in range(self.k):
                    ins = V.bn_stats(self.yst[0:self.parts, t, :], xb[:, t, :])
                link(ins)
                link(stats_to_var(dve, link, self.yst, self.ysm, self.parts, self.k))
                V.scalar_tensor_tensor(out=self.q(self.GV, slot), in0=self.q(self.G2, slot), scalar=F * EPS,
                                       in1=self.ysm[0:self.parts, 3, :], op0=ALU.mult, op1=ALU.add)\
                    .then_inc(s["y_stats"], 1)
                link.end()

            def act_rstd(self, act, i, slot):
                s = self.s
                link = Chain(act, s["chain_rstd"], 1, i)
                act.wait_ge(s["y_stats"], i + 1)
                link(nc.scalar.activation(self.q(self.LNY, slot), self.q(self.GV, slot), ACT.Ln, scale=1.0 / F))
                nc.scalar.activation(self.q(self.RY, slot), self.q(self.LNY, slot), ACT.Exp, scale=-0.5)\
                    .then_inc(s["y_rstd"], 1)
                link.end()

            def dve_final(self, dve, i, slot):
                s, V = self.s, nc.vector
                link = Chain(dve, s["chain_final"], 1, i)
                dve.wait_ge(s["y_rstd"], i + 1)
                ry, nb = self.q(self.RY, slot), self.ynb[0:self.parts, :]
                link(V.scalar_tensor_tensor(out=nb, in0=self.ysm[0:self.parts, 0, :], scalar=-0.5, in1=ry,
                                            op0=ALU.mult, op1=ALU.mult))
                xb = self.x_of(slot)
                for t in range(self.k):
                    ins = V.tensor_scalar(xb[:, t, :], xb[:, t, :], ry[:, t:t + 1], nb[:, t:t + 1], ALU.mult, ALU.add)
                ins.then_inc(s["final"], 1)
                link.end()

        def carve():
            at = [0]

            def take(parts, *shape):
                size = 1
                for n in shape:
                    size *= n
                v = arena[0:parts, at[0]:at[0] + size]
                at[0] += size
                assert at[0] <= 12800
                return v if len(shape) == 1 else v.rearrange("p (a b) -> p a b", a=shape[0]) if len(shape) == 2 \
                    else v.rearrange("p (a b c) -> p a b c", a=shape[0], b=shape[1])
            return take

        take = carve()
        xbuf = take(128, UNROLL, T * F)
        z_dense = take(128, T, F)
        xt_dense = [take(128, QT * 128) for _ in range(2)]
        sq_dense = [take(128, QT * 128) for _ in range(2)]
        rows2 = take(EP, 2, 4 * F)
        rows2t = take(128, 4 * EP)
        idx2 = sb("idx2", [EP, 2, 4], i32)

        def x_tile(slot):
            return xbuf[:, slot, :].rearrange("p (k f) -> p k f", f=F)

        dense = Update("dense", NP, T, x_tile, z_dense, xt_dense, sq_dense)
        nst, nsm, nnb = sb("nst", [128, T, 6]), sb("nsm", [128, 4, T]), sb("nnb", [128, T])
        nln, nr = sb("nln", [128, T]), sb("nr", [128, T])
        s_xin = [sem(f"x_in{n}") for n in range(UNROLL)]
        s_xout = [sem(f"x_out{n}") for n in range(UNROLL)]
        s_rows = [sem(f"rows_in{n}") for n in range(2)]
        s_spill = [sem(f"rows_out{n}") for n in range(2)]
        s_cadd, s_nst, s_nr, s_nch, s_nrch, s_icp, s_rt, s_rc, s_sf, s_fc = (sem(n) for n in (
            "c_added", "norm_stats", "norm_rstd", "norm_chain", "norm_rstd_chain", "idx_copied",
            "rows_transposed", "rows_copied", "scored", "feat_copied"))
        STEPS = EJ // 2
        assert STEPS >= CHUNKS + 1 and CHUNKS - 1 >= 96

        def start_of(i):
            return LAST_START if isinstance(i, int) and i == CHUNKS - 1 else i * CHUNK

        with nc.Block() as block:
            @block.sync
            def _(sp):
                def body(i, slot):
                    if on(i, CHUNKS, 2):
                        sp.wait_ge(dense.s["final"], i - 1)
                        if isinstance(i, int) and i - 2 == CHUNKS - 1:
                            sp.wait_ge(s_xout[(slot - 3) % UNROLL], 16 * ((i - 3) // UNROLL + 1))
                        sp.dma_start(node_rows(out, start_of(i - 2)), x_tile((slot - 2) % UNROLL))\
                            .then_inc(s_xout[(slot - 2) % UNROLL], 16)
                    if on(i, CHUNKS, -1):
                        if not isinstance(i, int):
                            sp.wait_ge(s_xout[(slot + 1) % UNROLL], (block_no[0] + (slot + 1) // UNROLL) * 16)
                        else:
                            after(sp, s_xout[(slot + 1) % UNROLL], 16 * ((i + 1) // UNROLL))
                        sp.dma_start(x_tile((slot + 1) % UNROLL), node_rows(x, start_of(i + 1)))\
                            .then_inc(s_xin[(slot + 1) % UNROLL], 16)
                    if on(i, STEPS):
                        sp.wait_ge(s_rows[slot % 2], 64 * half(i, slot))
                        r = rows2[:, slot % 2, :].rearrange("p (k f) -> p k f", f=F)
                        sp.dma_start(edge_rows(xs_dram, i * 2, 2), r[:, 0:2, :]).then_inc(s_spill[slot % 2], 16)
                        sp.dma_start(edge_rows(xd_dram, i * 2, 2), r[:, 2:4, :]).then_inc(s_spill[slot % 2], 16)

                sp.dma_start(x_tile(0), node_rows(x, 0)).then_inc(s_xin[0], 16)
                steps2(sp, body)
                for n in range(UNROLL):
                    sp.wait_ge(s_xout[n], 16 * len(range(n, CHUNKS, UNROLL)))
                for n in range(2):
                    sp.wait_ge(s_spill[n], 32 * (STEPS // 2))

            @block.gpsimd
            def _(pool):
                def body(i, slot):
                    if on(i, STEPS):
                        after(pool, s_spill[slot % 2], 32 * (half(i, slot) - 1))
                        after(pool, s_rt, i - 1)
                        nc.gpsimd.tensor_copy(idx2[:, slot % 2, 0:2], src_i[:, bass.ds(i * 2, 2)])
                        nc.gpsimd.tensor_copy(idx2[:, slot % 2, 2:4], dst_i[:, bass.ds(i * 2, 2)]).then_inc(s_icp, 1)
                    if on(i, CHUNKS):
                        pool.wait_ge(s_xin[slot], 16 * quarter_of(i, slot))
                        nc.gpsimd.tensor_tensor(x_tile(slot), x_tile(slot), bcast(bc["c"], NP, T), ALU.add)\
                            .then_inc(s_cadd, 1)
                    if on(i, STEPS):
                        pool.wait_ge(s_icp, i + 1)
                        pool.sem_inc(s_go, 1)
                        for k in range(4):
                            nc.gpsimd.indirect_dma_start(
                                out=rows2[:, slot % 2, k * F:(k + 1) * F], out_offset=None, in_=x,
                                in_offset=bass.IndirectOffsetOnAxis(ap=idx2[:, slot % 2, k:k + 1], axis=0))\
                                .then_inc(s_rows[slot % 2], 16)
                steps2(pool, body)

            @block.vector
            def _(dve):
                V = nc.vector

                def body(i, slot):
                    if on(i, CHUNKS):
                        link = Chain(dve, s_nch, 3 + 1, i)
                        dve.wait_ge(s_cadd, i + 1)
                        for t in range(T):
                            ins = V.bn_stats(nst[:, t, :], x_tile(slot)[:, t, :])
                        link(ins)
                        stats_to_var(dve, link, nst, nsm, NP, T).then_inc(s_nst, 1)
                    if on(i, CHUNKS, 2):
                        dense.dve_final(dve, i - 2, (slot - 2) % UNROLL)
                    if on(i, CHUNKS, 1):
                        dense.dve_z(dve, i - 1, (slot - 1) % UNROLL)
                    if on(i, CHUNKS):
                        dve.wait_ge(s_nr, i + 1)
                        link(V.scalar_tensor_tensor(out=nnb[:, :], in0=nsm[:, 0, :], scalar=-0.5, in1=nr[:, :],
                                                    op0=ALU.mult, op1=ALU.mult))
                        link.end()
                        for t in range(T):
                            ins = V.tensor_scalar(x_tile(slot)[:, t, :], x_tile(slot)[:, t, :], nr[:, t:t + 1],
                                                  nnb[:, t:t + 1], ALU.mult, ALU.add)
                        ins.then_inc(dense.s["x_ready"], 1)
                    if on(i, CHUNKS, 1):
                        dense.dve_y(dve, i - 1, (slot - 1) % UNROLL)
                steps2(dve, body)

            @block.scalar
            def _(act):
                act.preload_act_table_set("natural_log_exp_and_others")
                def body(i, slot):
                    if on(i, CHUNKS, 1):
                        dense.act_scales(act, i - 1, (slot - 1) % UNROLL)
                    if on(i, CHUNKS):
                        link = Chain(act, s_nrch, 1, i)
                        act.wait_ge(s_nst, i + 1)
                        link(nc.scalar.activation(nln[:, :], nsm[:, 3, :], ACT.Ln, bias=eps_col[:, :], scale=1.0 / F))
                        link.end()
                        nc.scalar.activation(nr[:, :], nln[:, :], ACT.Exp, scale=-0.5).then_inc(s_nr, 1)
                    if on(i, CHUNKS, 1):
                        dense.act_relu(act, i - 1)
                    if on(i, STEPS):
                        act.wait_ge(s_rt, i + 1)
                        after(act, s_sf, i)
                        nc.scalar.activation(rows2t[:, :], bank[7][:, 0:4 * EP], ACT.Copy).then_inc(s_rc, 1)
                    if on(i, CHUNKS):
                        dense.act_copy(act, i)
                        dense.act_square(act, i)
                    if on(i, STEPS):
                        act.wait_ge(s_sf, i + 1)
                        nc.scalar.activation(edge_feat[:, bass.ds(i * 2 * F, 2 * F)], bank[7][0:EP, 0:2 * F],
                                             ACT.Copy).then_inc(s_fc, 1)
                    if on(i, CHUNKS, 1):
                        dense.act_rstd(act, i - 1, (slot - 1) % UNROLL)
                steps2(act, body)

            @block.tensor
            def _(pe):
                def body(i, slot):
                    if on(i, STEPS):
                        pe.wait_ge(s_rows[slot % 2], 64 * half(i, slot))
                        after(pe, s_fc, i)
                        for k in range(4):
                            ins = nc.tensor.transpose(bank[7][:, k * EP:(k + 1) * EP],
                                                      rows2[:, slot % 2, k * F:(k + 1) * F], ident[0:EP, 0:EP])
                        ins.then_inc(s_rt, 1)
                    if on(i, CHUNKS):
                        dense.pe_transpose(pe, i, slot)
                    if on(i, STEPS):
                        pe.wait_ge(s_rc, i + 1)
                        for k in range(2):
                            score = bank[6][0:EP, bass.ds(i * 4 + 2 * k, HEADS)]
                            nc.tensor.matmul(score, rows2t[:, k * EP:(k + 1) * EP], v_el[:, :], start=True, stop=False)
                            nc.tensor.matmul(score, rows2t[:, (2 + k) * EP:(3 + k) * EP], v_er[:, :], start=False,
                                             stop=True)
                            ins = nc.tensor.matmul(bank[7][0:EP, k * F:(k + 1) * F],
                                                   rows2t[:, k * EP:(k + 1) * EP], w_gat[:, :], start=True, stop=True)
                        ins.then_inc(s_sf, 1)
                    if on(i, CHUNKS):
                        dense.pe_products(pe, i, slot)
                steps2(pe, body)


        take = carve()
        score, ex, den = (take(EP, HEADS + 1, EJ) for _ in range(3))
        run_f, run_all = take(EP, EJ), take(EP, EJ)
        diag = take(EP, 2, EP)
        junk3 = take(EP, EP)
        ends = take(EP, 2, 4)
        raw = take(EP, EJ * HEADS)
        mx = take(EP, 8)
        s_dg, s_rows3, s_rd, s_ex, s_en, s_tt = (sem(n) for n in (
            "ends_ready", "end_rows", "scores_read", "exps_ready", "sums_ready", "totals_ready"))
        with nc.Block() as block:
            @block.scalar
            def _(act):
                act.preload_act_table_set("natural_log_exp_and_others")
                nc.scalar.activation(raw[:, :], bank[6][0:EP, 0:EJ * HEADS], ACT.Copy).then_inc(s_rd, 1)
                act.wait_ge(s_ex, 1)
                nc.scalar.activation(ex[:, 0:HEADS, :], ex[:, 0:HEADS, :], ACT.Exp).then_inc(s_ex, 1)

            @block.tensor
            def _(pe):
                for n in range(HEADS + 1):
                    pe.wait_ge(s_dg, n + 1)
                    nc.tensor.matmul(bank[n][0:EP, 0:EP], ones[0:EP, 0:EP], diag[:, 0, :], start=True, stop=True)
                    nc.tensor.matmul(bank[n][0:EP, 128:128 + EP], ones[0:EP, 0:EP], diag[:, 1, :], start=True,
                                     stop=True).then_inc(s_rows3, 1)
                pe.wait_ge(s_en, 1)
                a, b = ends[:, 0, 0:HEADS + 1], ends[:, 1, 0:HEADS + 1]
                nc.tensor.matmul(bank[3][0:EP, 0:HEADS + 1], cross[:, 0, :], a, start=True, stop=False)
                nc.tensor.matmul(bank[3][0:EP, 0:HEADS + 1], cross_sum[:, 0, :], b, start=False, stop=True)
                nc.tensor.matmul(bank[3][0:EP, 8:9 + HEADS], cross[:, 1, :], a, start=True, stop=False)
                nc.tensor.matmul(bank[3][0:EP, 8:9 + HEADS], cross_sum[:, 1, :], b, start=False, stop=True)\
                    .then_inc(s_tt, 1)

            @block.vector
            def _(dve):
                V = nc.vector
                dve.wait_ge(s_rd, 1)
                by_head = raw[:, :].rearrange("p (j h) -> p h j", h=HEADS)
                link(V.tensor_copy(score[:, 0:HEADS, :], by_head))
                link(V.scalar_tensor_tensor(out=score[:, 0:HEADS, :], in0=score[:, 0:HEADS, :], scalar=0.2,
                                            in1=score[:, 0:HEADS, :], op0=ALU.mult, op1=ALU.max))
                link(V.tensor_copy(score[:, HEADS, :], sc[1][:, :]))
                for n in range(HEADS + 1):
                    link(V.tensor_tensor_scan(run_f[:, :], pen_f[:, :], score[:, n, :], -BIG, ALU.add, ALU.max))
                    link(V.tensor_tensor_scan(run_all[:, ::-1], pen_b[:, ::-1], run_f[:, ::-1], -BIG, ALU.add, ALU.max))
                    link(V.tensor_scalar(diag[:, 0, :], ident[0:EP, 0:EP], run_all[:, 0:1], None, ALU.mult))
                    V.tensor_scalar(diag[:, 1, :], ident[0:EP, 0:EP], run_all[:, EJ - 1:EJ], None, ALU.mult)\
                        .then_inc(s_dg, 1)
                    dve.wait_ge(s_rows3, n + 1)
                    for q in range(4):
                        row = bank[n][0:EP, 128 * (q % 2):128 * (q % 2) + EP]
                        link(V.tensor_tensor_reduce(out=junk3[:, :], in0=cross_pen[:, q, :], in1=row, scale=1.0,
                                                    scalar=-BIG, op0=ALU.add, op1=ALU.max, accum_out=mx[:, q:q + 1]))
                    V.tensor_tensor(mx[:, 4:5], mx[:, 0:1], mx[:, 1:2], ALU.max)
                    link(V.tensor_tensor(mx[:, 5:6], mx[:, 2:3], mx[:, 3:4], ALU.max))
                    link(V.scalar_tensor_tensor(out=den[:, n, :], in0=pen_first[:, :], scalar=mx[:, 4:5],
                                                in1=run_all[:, :], op0=ALU.add, op1=ALU.max))
                    link(V.scalar_tensor_tensor(out=den[:, n, :], in0=pen_last[:, :], scalar=mx[:, 5:6],
                                                in1=den[:, n, :], op0=ALU.add, op1=ALU.max))
                V.tensor_copy(x1_idx[:, :], den[:, HEADS, :])
                V.tensor_tensor(ex[:, 0:HEADS, :], score[:, 0:HEADS, :], den[:, 0:HEADS, :], ALU.subtract)\
                    .then_inc(s_ex, 1)
                link(V.memset(ex[:, HEADS, :], 1.0))
                dve.wait_ge(s_ex, 2)
                for n in range(HEADS + 1):
                    link(V.tensor_tensor_scan(run_f[:, :], same[:, :], ex[:, n, :], 0.0, ALU.mult, ALU.add))
                    link(V.tensor_tensor_scan(den[:, n, ::-1], same_n[:, ::-1], run_f[:, ::-1], 0.0, ALU.mult, ALU.max))
                V.tensor_copy(ends[:, 0, 0:HEADS + 1], den[:, :, 0])
                V.tensor_copy(ends[:, 1, 0:HEADS + 1], den[:, :, EJ - 1]).then_inc(s_en, 1)
                dve.wait_ge(s_tt, 1)
                link(V.tensor_copy(mx[:, 0:3], bank[3][0:EP, 0:3]))
                link(V.tensor_copy(mx[:, 4:7], bank[3][0:EP, 8:11]))
                for n in range(HEADS + 1):
                    link(V.scalar_tensor_tensor(out=den[:, n, :], in0=first[:, :], scalar=mx[:, n:n + 1],
                                                in1=den[:, n, :], op0=ALU.mult, op1=ALU.max))
                    link(V.scalar_tensor_tensor(out=den[:, n, :], in0=in_last[:, :], scalar=mx[:, 4 + n:5 + n],
                                                in1=den[:, n, :], op0=ALU.mult, op1=ALU.max))
                link(V.tensor_scalar(den[:, HEADS, :], den[:, HEADS, :], 1e-8, None, ALU.add))
                link(V.reciprocal(den[:, :, :], den[:, :, :]))
                V.tensor_copy(rcnt[:, :], den[:, HEADS, :])
                link(V.tensor_tensor(alpha[:, :].rearrange("p (j h) -> p h j", h=HEADS), ex[:, 0:HEADS, :],
                                     den[:, 0:HEADS, :], ALU.mult))

        s_v, s_f, s_cy = (sem(n) for n in ("weighted", "summed", "carry_ready"))
        with nc.Block() as block:
            @block.gpsimd
            def _(pool):
                with pool.Fori(0, EG) as i:
                    v = edge_feat[:, bass.ds(i * QT * F, QT * F)].rearrange("p (a f) -> p a f", f=FO)
                    w = alpha[:, bass.ds(i * QT * HEADS, QT * HEADS)].rearrange("p (a b) -> p a b", b=1)
                    nc.gpsimd.tensor_tensor(v, v, w.to_broadcast([EP, QT * HEADS, FO]), ALU.mult).then_inc(s_v, 1)

            @block.vector
            def _(dve):
                V = nc.vector

                def add(i, t):
                    j = i * QT + t
                    if isinstance(i, int) and j == 0:
                        return
                    before = edge_feat[:, bass.ds((j - 1) * F, F)]
                    here = edge_feat[:, bass.ds(j * F, F)]
                    V.scalar_tensor_tensor(out=here, in0=before, scalar=same[:, bass.ds(j, 1)], in1=here,
                                           op0=ALU.mult, op1=ALU.add).then_inc(s_f, 1)
                    dve.wait_ge(s_f, j)
                dve.wait_ge(s_v, 1)
                for t in range(QT):
                    add(0, t)
                with dve.Fori(1, EG) as i:
                    dve.wait_ge(s_v, i + 1)
                    for t in range(QT):
                        add(i, t)
                dve.wait_ge(s_cy, 1)
                V.tensor_copy(carry[:, :], bank[0][0:EP, 0:F])

            @block.tensor
            def _(pe):
                pe.wait_ge(s_f, EJ - 1)
                nc.tensor.matmul(bank[0][0:EP, 0:F], carry_lhs[:, :], edge_feat[:, (EJ - 1) * F:EJ * F], start=True,
                                 stop=True).then_inc(s_cy, 1)

        take = carve()
        gbuf, dbuf = take(EP, UNROLL, QT * F), take(EP, UNROLL, QT * F)
        st5, sm5 = [sb(f"st5_{n}", [128, QT, 6]) for n in range(2)], [sb(f"sm5_{n}", [128, 4, QT]) for n in range(2)]
        ln5, r5, nb5 = ([sb(f"{a}5_{n}", [128, QT]) for n in range(2)] for a in ("ln", "r", "nb"))
        s_din, s_gout, s_dout = ([sem(f"{a}{n}") for n in range(UNROLL)] for a in ("xd_in", "g_out", "x1_out"))
        s_tot, s_bias, s_gg, s_uu = (sem(n) for n in ("total", "bias_added", "g_ready", "u_ready"))
        s_pch, s_v5, s_r5, s_nm5, s_ch5, s_ach5 = (([sem(f"{a}_{n}") for n in range(2)]) for a in (
            "p5_chain", "p5_stats", "p5_rstd", "p5_normed", "p5_dchain", "p5_achain"))

        def tiles(buf, slot):
            return buf[:, slot, :].rearrange("p (k f) -> p k f", f=F)

        def steps5(eng, body, extra):
            run_steps(eng, body, EG + extra, EG // UNROLL * UNROLL)

        with nc.Block() as block:
            @block.sync
            def _(sp):
                def body(i, slot):
                    if on(i, EG, -1):
                        n = (slot + 1) % UNROLL
                        after(sp, s_dout[n], 16 * (quarter_of(i, slot) - 1 + (slot + 1) // UNROLL))
                        sp.dma_start(tiles(dbuf, n), edge_rows(xd_dram, (i + 1) * QT, QT)).then_inc(s_din[n], 16)
                    if on(i, EG, 1):
                        n = (slot - 1) % UNROLL
                        sp.wait_ge(s_gg, i)
                        sp.dma_start(edge_rows(g_dram, (i - 1) * QT, QT), tiles(gbuf, n)).then_inc(s_gout[n], 16)
                    if on(i, EG, 2):
                        n = (slot - 2) % UNROLL
                        sp.wait_ge(s_nm5[1], i - 1)
                        sp.dma_start(edge_rows(x1_dram, (i - 2) * QT, QT), tiles(dbuf, n)).then_inc(s_dout[n], 16)
                sp.dma_start(tiles(dbuf, 0), edge_rows(xd_dram, 0, QT)).then_inc(s_din[0], 16)
                steps5(sp, body, 2)
                for n in range(UNROLL):
                    sp.wait_ge(s_gout[n], 16 * len(range(n, EG, UNROLL)))
                    sp.wait_ge(s_dout[n], 16 * len(range(n, EG, UNROLL)))

            def norm_stats(dve, which, buf, i, slot):
                V = nc.vector
                link = Chain(dve, s_ch5[which], 4, i)
                for t in range(QT):
                    ins = V.bn_stats(st5[which][0:EP, t, :], tiles(buf, slot)[:, t, :])
                link(ins)
                stats_to_var(dve, link, st5[which], sm5[which], EP, QT).then_inc(s_v5[which], 1)
                return link

            def norm_apply(dve, which, buf, i, slot, link):
                V = nc.vector
                dve.wait_ge(s_r5[which], i + 1)
                r, nb = r5[which][0:EP, :], nb5[which][0:EP, :]
                link(V.scalar_tensor_tensor(out=nb, in0=sm5[which][0:EP, 0, :], scalar=-0.5, in1=r, op0=ALU.mult,
                                            op1=ALU.mult))
                for t in range(QT):
                    ins = V.tensor_scalar(tiles(buf, slot)[:, t, :], tiles(buf, slot)[:, t, :], r[:, t:t + 1],
                                          nb[:, t:t + 1], ALU.mult, ALU.add)
                ins.then_inc(s_nm5[which], 1)
                link.end()

            def norm_rstd(act, which, i):
                link = Chain(act, s_ach5[which], 1, i)
                act.wait_ge(s_v5[which], i + 1)
                link(nc.scalar.activation(ln5[which][0:EP, :], sm5[which][0:EP, 3, :], ACT.Ln, bias=eps_col[0:EP, :],
                                          scale=1.0 / F))
                nc.scalar.activation(r5[which][0:EP, :], ln5[which][0:EP, :], ACT.Exp, scale=-0.5)\
                    .then_inc(s_r5[which], 1)
                link.end()

            @block.vector
            def _(dve):
                V = nc.vector

                def body(i, slot):
                    if on(i, EG):
                        after(dve, s_gout[slot], 16 * (quarter_of(i, slot) - 1))
                        for t in range(QT):
                            j = i * QT + t
                            ins = V.scalar_tensor_tensor(out=tiles(gbuf, slot)[:, t, :], in0=carry[:, :],
                                                         scalar=first[:, bass.ds(j, 1)],
                                                         in1=edge_feat[:, bass.ds(j * F, F)], op0=ALU.mult, op1=ALU.add)
                        ins.then_inc(s_tot, 1)
                    if on(i, EG, 1):
                        dve.wait_ge(s_bias, i)
                        one = norm_stats(dve, 0, gbuf, i - 1, (slot - 1) % UNROLL)
                    if on(i, EG, 2):
                        dve.wait_ge(s_uu, i - 1)
                        two = norm_stats(dve, 1, dbuf, i - 2, (slot - 2) % UNROLL)
                    if on(i, EG, 1):
                        norm_apply(dve, 0, gbuf, i - 1, (slot - 1) % UNROLL, one)
                    if on(i, EG, 2):
                        norm_apply(dve, 1, dbuf, i - 2, (slot - 2) % UNROLL, two)
                steps5(dve, body, 2)

            @block.scalar
            def _(act):
                act.preload_act_table_set("natural_log_exp_and_others")

                def body(i, slot):
                    if on(i, EG, 1):
                        norm_rstd(act, 0, i - 1)
                    if on(i, EG, 2):
                        norm_rstd(act, 1, i - 2)
                steps5(act, body, 2)

            @block.gpsimd
            def _(pool):
                G = nc.gpsimd

                def body(i, slot):
                    if on(i, EG):
                        pool.wait_ge(s_tot, i + 1)
                        G.tensor_tensor(tiles(gbuf, slot), tiles(gbuf, slot), bcast(bc["bias"], EP, QT), ALU.add)\
                            .then_inc(s_bias, 1)
                    if on(i, EG, 1):
                        n = (slot - 1) % UNROLL
                        pool.wait_ge(s_nm5[0], i)
                        G.tensor_tensor(tiles(gbuf, n), tiles(gbuf, n), bcast(bc["gamma"], EP, QT), ALU.mult)\
                            .then_inc(s_pch[0], 1)
                        pool.wait_ge(s_pch[0], i)
                        G.tensor_tensor(tiles(gbuf, n), tiles(gbuf, n), bcast(bc["beta"], EP, QT), ALU.add)\
                            .then_inc(s_gg, 1)
                        pool.wait_ge(s_gg, i)
                        pool.wait_ge(s_din[n], 16 * (quarter_of(i, slot) - 1 + (1 if slot else 0)))
                        G.tensor_tensor(tiles(dbuf, n), tiles(dbuf, n), tiles(gbuf, n), ALU.add).then_inc(s_uu, 1)
                steps5(pool, body, 2)

        take = carve()
        sbuf = take(EP, UNROLL, QT * F)
        grow, drow = take(EP, UNROLL, QT * F), take(EP, UNROLL, QT * F)
        z6 = take(EP, QT, F)
        xt6, mt6, sq6 = take(128, QT * EP), take(128, QT * EP), take(128, QT * EP)
        idx6 = sb("idx6", [EP, UNROLL, 2 * QT], i32)
        st6, sm6, ln6, r6, nb6 = sb("st6", [128, QT, 6]), sb("sm6", [128, 4, QT]), sb("ln6", [128, QT]), \
            sb("r6", [128, QT]), sb("nb6", [128, QT])
        msg = Update("msg", EP, QT, lambda slot: tiles(sbuf, slot), z6, [xt6], [sq6],
                     m_of=lambda slot: tiles(drow, slot), mt=mt6,
                     weights=(w_ma, w_mb, w_mag, w_mbg, bc["mb"], mb_col, bc["mbeta"]), gated=False)
        s_sin, s_gin = ([sem(f"{a}{n}") for n in range(UNROLL)] for a in ("xs_in", "gathered"))
        s_icp6, s_c6, s_v6, s_r6, s_a6, s_w6, s_f6, s_cy6 = (sem(n) for n in (
            "idx6_copied", "m_chain", "m_stats", "m_rstd", "m_achain", "m_weighted",
            "m_summed", "carry6_ready"))
        with nc.Block() as block:
            @block.sync
            def _(sp):
                def body(i, slot):
                    if on(i, EG, -1):
                        n = (slot + 1) % UNROLL
                        after(sp, msg.s["transposed"], i - 2)
                        sp.dma_start(tiles(sbuf, n), edge_rows(xs_dram, (i + 1) * QT, QT)).then_inc(s_sin[n], 16)
                sp.dma_start(tiles(sbuf, 0), edge_rows(xs_dram, 0, QT)).then_inc(s_sin[0], 16)
                steps5(sp, body, 0)

            @block.gpsimd
            def _(pool):
                def body(i, slot):
                    after(pool, msg.s["transposed"], i - 3)
                    if not isinstance(i, int) or i >= UNROLL:
                        pool.wait_ge(s_gin[slot], 128 * (quarter_of(i, slot) - 1))
                    cols = idx6[:, slot, :]
                    nc.gpsimd.tensor_copy(cols[:, 0:QT], g_idx[:, bass.ds(i * QT, QT)])
                    nc.gpsimd.tensor_copy(cols[:, QT:2 * QT], x1_idx[:, bass.ds(i * QT, QT)]).then_inc(s_icp6, 1)
                    pool.wait_ge(s_icp6, i + 1)
                    pool.sem_inc(s_go, 1)
                    for k in range(2 * QT):
                        rows, table = (grow, g_dram) if k < QT else (drow, x1_dram)
                        nc.gpsimd.indirect_dma_start(
                            out=rows[:, slot, (k % QT) * F:(k % QT + 1) * F], out_offset=None, in_=table,
                            in_offset=bass.IndirectOffsetOnAxis(ap=cols[:, k:k + 1], axis=0))\
                            .then_inc(s_gin[slot], 16)
                steps5(pool, body, 0)

            @block.vector
            def _(dve):
                V = nc.vector

                def body(i, slot):
                    if on(i, EG):
                        link = Chain(dve, s_c6, 5, i)
                        dve.wait_ge(s_sin[slot], 16 * quarter_of(i, slot))
                        dve.wait_ge(s_gin[slot], 128 * quarter_of(i, slot))
                        link(V.tensor_tensor(tiles(sbuf, slot), tiles(sbuf, slot), tiles(grow, slot), ALU.add))
                        for t in range(QT):
                            ins = V.bn_stats(st6[0:EP, t, :], tiles(sbuf, slot)[:, t, :])
                        link(ins)
                        stats_to_var(dve, link, st6, sm6, EP, QT).then_inc(s_v6, 1)
                    if on(i, EG, 1):
                        n = (slot - 1) % UNROLL
                        dve.wait_ge(msg.s["scales"], i)
                        for t in range(QT):
                            ins = V.scalar_tensor_tensor(out=z6[:, t, :], in0=bank[3][0:EP, t * F:(t + 1) * F],
                                                         scalar=msg.q(msg.RS, n)[:, t:t + 1],
                                                         in1=bc["mbeta"][0:EP, :], op0=ALU.mult, op1=ALU.add)
                        ins.then_inc(msg.s["scaled"], 1)
                        dve.wait_ge(msg.s["scaled"], i)
                        for t in range(QT):
                            j = (i - 1) * QT + t
                            to = edge_feat[:, bass.ds(j * F, F)] if isinstance(i, int) and j == 0 else z6[:, t, :]
                            ins = V.tensor_scalar(to, z6[:, t, :], 0.0, w_edge[:, bass.ds(j, 1)], ALU.max, ALU.mult)
                        ins.then_inc(s_w6, 1)
                        dve.wait_ge(s_w6, i)
                        for t in range(QT):
                            j = (i - 1) * QT + t
                            if isinstance(i, int) and j == 0:
                                continue
                            V.scalar_tensor_tensor(out=edge_feat[:, bass.ds(j * F, F)],
                                                   in0=edge_feat[:, bass.ds((j - 1) * F, F)],
                                                   scalar=same[:, bass.ds(j, 1)], in1=z6[:, t, :],
                                                   op0=ALU.mult, op1=ALU.add).then_inc(s_f6, 1)
                            dve.wait_ge(s_f6, j)
                    if on(i, EG):
                        dve.wait_ge(s_r6, i + 1)
                        link(V.scalar_tensor_tensor(out=nb6[0:EP, :], in0=sm6[0:EP, 0, :], scalar=-0.5,
                                                    in1=r6[0:EP, :], op0=ALU.mult, op1=ALU.mult))
                        link.end()
                        for t in range(QT):
                            row = tiles(sbuf, slot)[:, t, :]
                            ins = V.tensor_scalar(row, row, r6[0:EP, t:t + 1], nb6[0:EP, t:t + 1], ALU.mult, ALU.add)
                        ins.then_inc(msg.s["x_ready"], 1)
                steps5(dve, body, 1)
                dve.wait_ge(s_cy6, 1)
                V.tensor_copy(carry[:, :], bank[0][0:EP, 0:F])

            @block.scalar
            def _(act):
                act.preload_act_table_set("natural_log_exp_and_others")

                def body(i, slot):
                    if on(i, EG, 1):
                        msg.act_scales(act, i - 1, (slot - 1) % UNROLL)
                    if on(i, EG):
                        link = Chain(act, s_a6, 1, i)
                        act.wait_ge(s_v6, i + 1)
                        link(nc.scalar.activation(ln6[0:EP, :], sm6[0:EP, 3, :], ACT.Ln, bias=eps_col[0:EP, :],
                                                  scale=1.0 / F))
                        nc.scalar.activation(r6[0:EP, :], ln6[0:EP, :], ACT.Exp, scale=-0.5).then_inc(s_r6, 1)
                        link.end()
                        msg.act_copy(act, i)
                        msg.act_square(act, i)
                steps5(act, body, 1)

            @block.tensor
            def _(pe):
                def body(i, slot):
                    msg.pe_transpose(pe, i, slot)
                    msg.pe_products(pe, i, slot)
                steps5(pe, body, 0)
                pe.wait_ge(s_f6, EJ - 1)
                nc.tensor.matmul(bank[0][0:EP, 0:F], carry_lhs[:, :], edge_feat[:, (EJ - 1) * F:EJ * F], start=True,
                                 stop=True).then_inc(s_cy6, 1)

        take = carve()
        ubuf, mbuf = take(EP, UNROLL, QT * F), take(EP, UNROLL, QT * F)
        z7 = take(EP, QT, F)
        xt7, mt7, sq7 = take(128, QT * EP), take(128, QT * EP), take(128, QT * EP)
        idx7 = sb("idx7", [EP, UNROLL, QT], i32)
        upd = Update("upd", EP, QT, lambda slot: tiles(ubuf, slot), z7, [xt7], [sq7],
                     m_of=lambda slot: tiles(mbuf, slot), mt=mt7)
        s_uin, s_uout = ([sem(f"{a}{n}") for n in range(UNROLL)] for a in ("x1_in", "rows_scattered"))
        s_icp7, s_m7 = (sem(n) for n in ("idx7_copied", "mean_chain"))
        with nc.Block() as block:
            @block.sync
            def _(sp):
                def body(i, slot):
                    if on(i, EG, -1):
                        n = (slot + 1) % UNROLL
                        after(sp, s_uout[n], 16 * QT * (quarter_of(i, slot) - 1 + (slot + 1) // UNROLL))
                        sp.dma_start(tiles(ubuf, n), edge_rows(x1_dram, (i + 1) * QT, QT)).then_inc(s_uin[n], 16)
                sp.dma_start(tiles(ubuf, 0), edge_rows(x1_dram, 0, QT)).then_inc(s_uin[0], 16)
                steps5(sp, body, 0)

            @block.vector
            def _(dve):
                V = nc.vector

                def body(i, slot):
                    if on(i, EG):
                        after(dve, upd.s["transposed"], i - 3)
                        for t in range(QT):
                            j = i * QT + t
                            ins = V.scalar_tensor_tensor(out=tiles(mbuf, slot)[:, t, :], in0=carry[:, :],
                                                         scalar=first[:, bass.ds(j, 1)],
                                                         in1=edge_feat[:, bass.ds(j * F, F)], op0=ALU.mult, op1=ALU.add)
                        ins.then_inc(s_m7, 1)
                        dve.wait_ge(s_m7, i + 1)
                        dve.wait_ge(s_uin[slot], 16 * quarter_of(i, slot))
                        for t in range(QT):
                            m = tiles(mbuf, slot)[:, t, :]
                            ins = V.tensor_scalar(m, m, rcnt[:, bass.ds(i * QT + t, 1)], None, ALU.mult)
                        ins.then_inc(upd.s["x_ready"], 1)
                    if on(i, EG, 2):
                        upd.dve_final(dve, i - 2, (slot - 2) % UNROLL)
                    if on(i, EG, 1):
                        upd.dve_z(dve, i - 1, (slot - 1) % UNROLL)
                        upd.dve_y(dve, i - 1, (slot - 1) % UNROLL)
                steps5(dve, body, 2)

            @block.scalar
            def _(act):
                act.preload_act_table_set("natural_log_exp_and_others")

                def body(i, slot):
                    if on(i, EG, 1):
                        upd.act_scales(act, i - 1, (slot - 1) % UNROLL)
                    if on(i, EG):
                        upd.act_copy(act, i)
                    if on(i, EG, 1):
                        upd.act_relu(act, i - 1)
                    if on(i, EG):
                        upd.act_square(act, i)
                    if on(i, EG, 1):
                        upd.act_rstd(act, i - 1, (slot - 1) % UNROLL)
                steps5(act, body, 1)

            @block.tensor
            def _(pe):
                def body(i, slot):
                    upd.pe_transpose(pe, i, slot)
                    upd.pe_products(pe, i, slot)
                steps5(pe, body, 0)

            @block.gpsimd
            def _(pool):
                def body(i, slot):
                    if on(i, EG):
                        after(pool, s_uout[slot], 16 * QT * (quarter_of(i, slot) - 1))
                        nc.gpsimd.tensor_copy(idx7[:, slot, :], out_idx[:, bass.ds(i * QT, QT)]).then_inc(s_icp7, 1)
                    if on(i, EG, 2):
                        n = (slot - 2) % UNROLL
                        pool.wait_ge(s_icp7, i - 1)
                        pool.wait_ge(upd.s["final"], i - 1)
                        pool.sem_inc(s_go, 1)
                        for k in range(QT):
                            nc.gpsimd.indirect_dma_start(
                                out=out, out_offset=bass.IndirectOffsetOnAxis(ap=idx7[:, n, k:k + 1], axis=0),
                                in_=ubuf[:, n, k * F:(k + 1) * F], in_offset=None, bounds_check=N - 1,
                                oob_is_err=False).then_inc(s_uout[n], 16)
                steps5(pool, body, 2)
                for n in range(UNROLL):
                    pool.wait_ge(s_uout[n], 16 * QT * len(range(n, EG, UNROLL)))



_INS = ['x', 'src', 'dst', 'edge_weight', 'L0_gnn_W', 'L0_gnn_attn_l', 'L0_gnn_attn_r', 'L0_gnn_bias', 'L0_gnn_gamma',
        'L0_gnn_beta', 'L1_gnn_msg_w', 'L1_gnn_msg_b', 'L1_gnn_msg_g', 'L1_gnn_msg_beta', 'L1_gnn_upd_w',
        'L1_gnn_upd_b', 'L1_gnn_upd_g', 'L1_gnn_upd_beta', 'L1_gnn_gate_w', 'L1_gnn_gate_b']


def kernel(**inputs):
    import numpy as np
    import concourse.bacc as bacc
    from concourse.bass_utils import run_bass_kernel_spmd

    nc = bacc.Bacc("TRN2", target_bir_lowering=False, num_devices=1)
    arrays, args = {}, []
    for name in _INS:
        a = np.ascontiguousarray(inputs[name])
        arrays["in_" + name] = a
        args.append(nc.dram_tensor("in_" + name, a.shape, mybir.dt.from_np(a.dtype), kind="ExternalInput").ap())
    shape = np.asarray(inputs['x']).shape
    args.append(nc.dram_tensor("out_rows", shape, mybir.dt.float32, kind="ExternalOutput").ap())
    gnn_resnorm_kernel(nc, *args)
    r = run_bass_kernel_spmd(nc, [arrays], core_ids=[0])
    return r.results[0]["out_rows"]
```

```python
import concourse.bass as bass
from concourse import mybir
from contextlib import ExitStack


def gnn_resnorm_kernel(nc, x, src, dst, edge_weight, gat_w, attn_l, attn_r, gat_bias, gat_gamma, gat_beta,
                       msg_w, msg_b, msg_g, msg_beta, upd_w, upd_b, upd_g, upd_beta, gate_w, gate_b, out):
    f32 = mybir.dt.float32
    i32 = mybir.dt.int32
    bf16 = mybir.dt.bfloat16
    ALU = mybir.AluOpType
    ACT = mybir.ActivationFunctionType
    X = mybir.AxisListType.X

    N, F = x.shape
    E = src.shape[0]
    HEADS, FO = attn_l.shape
    EP = 125
    EJ = E // EP
    assert E == EP * EJ and EJ % 8 == 0 and F == 128 and HEADS * FO == F
    NP = 128
    T = 8
    CHUNK = NP * T
    CHUNKS = -(-N // CHUNK)
    LAST_START = N - CHUNK
    QT = 4
    EG = EJ // QT
    EPS = 1e-5
    BIG = 1e30
    GATE_CAP = 1e8
    SKIP = 1 << 20
    U = 6
    OUT_SPLIT = 4

    xs_dram = nc.dram_tensor("xs_rows", (E, F), f32, kind="Internal").ap()
    xd_dram = nc.dram_tensor("xd_rows", (E, F), f32, kind="Internal").ap()
    g_dram = nc.dram_tensor("g_rows", (E + 1, F), f32, kind="Internal").ap()
    x1_dram = nc.dram_tensor("x1_rows", (E, F), f32, kind="Internal").ap()

    def edge_rows(table, j, k):
        return table[0:E, :].rearrange("(p j) f -> p j f", j=EJ)[:, bass.ds(j, k), :]

    def node_rows(table, start):
        return table[bass.ds(start, CHUNK), :].rearrange("(p k) f -> p k f", k=T)

    ctx = ExitStack()
    with ctx:
        def sb(name, shape, dt=f32):
            return ctx.enter_context(nc.sbuf_tensor(name, shape, dt))

        def pb(name, shape, dt=f32):
            return ctx.enter_context(nc.psum_tensor(name, shape, dt))

        def sem(name):
            return ctx.enter_context(nc.semaphore(name))

        edge_feat = sb("edge_feat", [EP, EJ * F])
        arena = sb("arena", [128, 12800])
        ident = sb("ident", [128, 128])
        ones = sb("ones", [128, 128])
        ones_bf = sb("ones_bf", [128, 128], bf16)
        eps_col = sb("eps_col", [128, 1])
        w_gat = sb("w_gat", [F, F + HEADS])
        w_ma, w_mb, w_ub = (sb(n, [F, F]) for n in ("w_ma", "w_mb", "w_ub"))
        w_ut = sb("w_ut", [F, F + 1])
        v_er = sb("v_er", [F, HEADS])
        bias_m, bias_u = sb("bias_m", [3, 4 * F], bf16), sb("bias_u", [3, 3 * (F + 1)], bf16)
        bc = {n: sb("bc_" + n, [128, F]) for n in ("al", "ar", "bias", "gamma", "beta", "mb", "mg", "mbeta",
                                                   "ub", "ug", "ubeta", "c")}
        gb_bc = sb("gb_bc", [128, 1])
        src_i, dst_i = sb("src_i", [EP, EJ], i32), sb("dst_i", [EP, EJ], i32)
        src_f, dst_f = sb("src_f", [EP, EJ]), sb("dst_f", [EP, EJ])
        w_edge = sb("w_edge", [EP, EJ])
        same = sb("same", [EP, EJ])
        first = sb("first", [EP, EJ])
        pen_f, pen_b = sb("pen_f", [EP, EJ]), sb("pen_b", [EP, EJ])
        same_n = sb("same_n", [EP, EJ])
        pen_first, pen_last = sb("pen_first", [EP, EJ]), sb("pen_last", [EP, EJ])
        in_last = sb("in_last", [EP, EJ])
        cross = sb("cross", [EP, 4, EP])
        cross_pen = sb("cross_pen", [EP, 4, EP])
        cross_sum = sb("cross_sum", [EP, 2, EP])
        carry_lhs = sb("carry_lhs", [EP, EP])
        nz = sb("nz", [EP, 1])
        alpha = sb("alpha", [EP, EJ * HEADS])
        rcnt = sb("rcnt", [EP, EJ])
        g_idx, x1_idx, out_idx = (sb(n, [EP, EJ], i32) for n in ("g_idx", "x1_idx", "out_idx"))
        carry = sb("carry", [EP, F])
        sc = [sb(f"sc{n}", [EP, EJ]) for n in range(6)]
        small = sb("small", [128, 16])

        bank = [pb(f"bank{n}", [128, 512]) for n in range(8)]

        class Chain:

            def __init__(self, eng, s, per_run, run, already=0):
                self.eng, self.s, self.per_run, self.base, self.k = eng, s, per_run, run * per_run, already

            def __call__(self, ins):
                self.k += 1
                ins.then_inc(self.s, 1)
                self.eng.wait_ge(self.s, self.base + self.k)

            def end(self):
                assert self.k == self.per_run, (self.k, self.per_run)

        s_line = sem("vector_line")
        s_go = sem("rows_may_move")
        line = [0]

        def link(ins):
            line[0] += 1
            ins.then_inc(s_line, 1)
            nc.vector.wait_ge(s_line, line[0])

        def after(eng, s, count):
            if isinstance(count, int) and count <= 0:
                return
            eng.wait_ge(s, count)

        class Item:

            def __init__(self, block_, slot, n=None):
                self.block, self.slot = block_, slot
                self.n = block_ * U + slot if n is None else n
                self.known = isinstance(block_, int)

            def back(self, k):
                return Item(self.block + (self.slot - k) // U, (self.slot - k) % U, self.n - k)

            def ring(self, places):
                return self.slot % places

            def uses(self, places):
                return self.block * (U // places) + self.slot // places

            def on(self, count):
                return not self.known or 0 <= self.n < count

        class Ring:

            def __init__(self, name, unit=16):
                self.sems, self.base, self.unit = [sem(f"{name}{n}") for n in range(U)], [0] * U, unit

            def of(self, it):
                return self.sems[it.slot]

            def before(self, it):
                return self.base[it.slot] + self.unit * it.uses(U)

            def done(self, it):
                return self.base[it.slot] + self.unit * (it.uses(U) + 1)

            def wait_all(self, eng, items):
                for n in range(U):
                    eng.wait_ge(self.sems[n], self.base[n] + self.unit * len(range(n, items, U)))

            def end_phase(self, items):
                for n in range(U):
                    self.base[n] += self.unit * len(range(n, items, U))

        ring_in, ring_out = Ring("loaded"), Ring("stored")

        def run_steps(eng, body, steps, items):
            blocks = (items - 2) // U
            for i in range(U):
                body(Item(0, i))
            with eng.Fori(1, blocks) as b:
                for u in range(U):
                    body(Item(b, u))
            for i in range(blocks * U, steps):
                body(Item(i // U, i % U))

        def bcast(row, parts, k):
            return row[0:parts, :].rearrange("p (a f) -> p a f", a=1).to_broadcast([parts, k, F])

        s_ld, s_nx, s_pool0, s_p0, s_st, s_row0 = (sem(n) for n in (
            "setup_loaded", "next_cleared", "ident_ready", "setup_rows", "c_row_stored", "rows_read"))
        src_all = edge_feat[:, 0:E].bitcast(i32)
        dprev = sc[0][:, :].bitcast(i32)
        dnext = small[:, 8:9].bitcast(i32)
        dgT = arena[0:EP, 0:EP]
        n_loads = [0]
        with nc.Block() as block:
            @block.sync
            def _(sp):
                def load(dst_ap, src_ap):
                    n_loads[0] += 1
                    sp.dma_start(dst_ap, src_ap, allow_slow_non_contiguous=True).then_inc(s_ld, 16)

                load(dst_i[:, :], dst.rearrange("(p j) -> p j", j=EJ))
                load(src_i[:, :], src.rearrange("(p j) -> p j", j=EJ))
                for w, d in ((gat_w, w_gat), (msg_w[0:F, :], w_ma), (msg_w[F:2 * F, :], w_mb),
                             (upd_w[0:F, :], w_ut), (upd_w[F:2 * F, :], w_ub)):
                    load(d[:, 0:F], w)
                rows = (("al", attn_l.rearrange("h f -> (h f)")), ("ar", attn_r.rearrange("h f -> (h f)")),
                        ("bias", gat_bias), ("gamma", gat_gamma), ("beta", gat_beta), ("mb", msg_b), ("mg", msg_g),
                        ("mbeta", msg_beta), ("ub", upd_b), ("ug", upd_g), ("ubeta", upd_beta))
                for name, v in rows:
                    load(bc[name][:, :], v.partition_broadcast(128))
                load(w_ut[:, F:F + 1], gate_w)
                load(gb_bc[:, :], gate_b.partition_broadcast(128))
                load(w_edge[:, :], edge_weight.rearrange("(p j) -> p j", j=EJ))
                load(dprev[1:EP, :], dst[0:E - EJ].rearrange("(p j) -> p j", j=EJ))
                quarter = E // 4
                for q in range(4):
                    load(src_all[:, q * quarter:(q + 1) * quarter],
                         src[q * quarter:(q + 1) * quarter].partition_broadcast(EP))
                sp.wait_ge(s_nx, 1)
                load(dnext[0:EP - 1, :], dst[EJ:E].rearrange("(p j) -> p j", j=EJ)[:, 0:1])
            LOADED = 16 * n_loads[0]

            @block.gpsimd
            def _(pool):
                nc.gpsimd.memset(ident[:, :], 0.0).then_inc(s_pool0, 1)
                pool.wait_ge(s_pool0, 1)
                nc.gpsimd.affine_select(out=ident[:, :], in_=ident[:, :], compare_op=ALU.not_equal, fill=1.0,
                                        base=0, pattern=[[-1, 128]], channel_multiplier=1).then_inc(s_pool0, 1)
                nc.gpsimd.iota(sc[1][:, :].bitcast(i32), pattern=[[1, EJ]], base=0,
                               channel_multiplier=EJ).then_inc(s_pool0, 1)
                pool.wait_ge(s_p0, 3)
                nc.gpsimd.affine_select(out=carry_lhs[:, :], in_=carry_lhs[:, :], compare_op=ALU.is_gt, fill=0.0,
                                        base=0, pattern=[[1, EP]], channel_multiplier=-1).then_inc(s_pool0, 1)

            @block.tensor
            def _(pe):
                pe.wait_ge(s_p0, 1)
                nc.tensor.matmul(bank[0][0:EP, 0:EP], ones[0:EP, 0:EP], arena[0:EP, 0:EP], start=True,
                                 stop=True).then_inc(s_row0, 1)
                pe.wait_ge(s_p0, 2)
                nc.tensor.matmul(bank[1][0:EP, 0:EP], ones[0:EP, 0:EP], arena[0:EP, 128:128 + EP], start=True,
                                 stop=True).then_inc(s_row0, 1)

            @block.scalar
            def _(act):
                act.preload_act_table_set("natural_log_exp_and_others")
                act.wait_ge(s_p0, 4)
                nc.scalar.activation(small[:, 4:5], small[:, 3:4], ACT.Ln, bias=eps_col[:, :],
                                     scale=1.0 / F).then_inc(s_st, 1)
                act.wait_ge(s_st, 1)
                nc.scalar.activation(small[:, 5:6], small[:, 4:5], ACT.Exp, scale=-0.5).then_inc(s_st, 1)

            @block.vector
            def _(dve):
                V = nc.vector
                V.memset(ones[:, :], 1.0)
                V.memset(ones_bf[:, :], 1.0)
                V.memset(eps_col[:, :], EPS)
                link(V.memset(dprev[0:1, :], 0))
                V.memset(small[:, 8:9], -1.0).then_inc(s_nx, 1)
                dve.wait_ge(s_ld, LOADED)
                dve.wait_ge(s_pool0, 3)
                link(V.tensor_copy(src_f[:, :], src_i[:, :]))
                link(V.tensor_copy(dst_f[:, :], dst_i[:, :]))
                link(V.tensor_copy(sc[1][:, :], sc[1][:, :].bitcast(i32)))
                fd, ld = dst_f[:, 0:1], dst_f[:, EJ - 1:EJ]
                V.tensor_scalar(arena[0:EP, 0:EP], ident[0:EP, 0:EP], fd, None, ALU.mult).then_inc(s_p0, 1)
                V.tensor_scalar(arena[0:EP, 128:128 + EP], ident[0:EP, 0:EP], ld, None, ALU.mult).then_inc(s_p0, 1)
                for row, v in (("al", w_gat[:, F:F + HEADS]), ("ar", v_er[:, :])):
                    tmp = arena[:, 256:256 + F]
                    link(V.tensor_tensor(tmp, w_gat[:, 0:F], bc[row][:, :], ALU.mult))
                    link(V.tensor_reduce(v, tmp.rearrange("p (h f) -> p h f", h=HEADS), X, ALU.add))
                for w in (w_ma, w_mb, w_ut, w_ub):
                    link(V.tensor_reduce(small[:, 0:1], w[:, 0:F], X, ALU.add))
                    link(V.tensor_scalar(small[:, 1:2], small[:, 0:1], 1.0 / F, None, ALU.mult))
                    link(V.tensor_scalar(w[:, 0:F], w[:, 0:F], small[:, 1:2], None, ALU.subtract))
                for row, width, parts_of in (("mb", F, bias_m), ("ub", F + 1, bias_u)):
                    full, rest = (arena[:, 512 + 256 * n:512 + 256 * n + width] for n in range(2))
                    link(V.tensor_reduce(small[:, 0:1], bc[row][:, :], X, ALU.add))
                    link(V.tensor_scalar(small[:, 1:2], small[:, 0:1], 1.0 / F, None, ALU.mult))
                    if width > F:
                        V.tensor_copy(full[:, F:F + 1], gb_bc[:, :])
                    link(V.tensor_scalar(full[:, 0:F], bc[row][:, :], small[:, 1:2], None, ALU.subtract))
                    half_row = arena[:, 1280:1280 + F].bitcast(bf16)[:, 0:width]
                    for n in range(3):
                        link(V.tensor_copy(half_row, full))
                        if n:
                            link(V.scalar_tensor_tensor(out=rest[0:3, :], in0=half_row[0:3, :],
                                                        scalar=ident[0:3, n:n + 1], in1=rest[0:3, :], op0=ALU.mult,
                                                        op1=ALU.add))
                        else:
                            link(V.tensor_scalar(rest[0:3, :], half_row[0:3, :], ident[0:3, 0:1], None, ALU.mult))
                        link(V.tensor_tensor(full, full, half_row, ALU.subtract))
                    for n in range(parts_of.shape[1] // width):
                        V.tensor_copy(parts_of[:, n * width:(n + 1) * width], rest[0:3, :])
                link(V.bn_stats(small[:, 9:15], bc["bias"][:, :]))
                st = small[:, 9:15]
                V.tensor_tensor(small[:, 0:1], st[:, 1:2], st[:, 4:5], ALU.add)
                V.tensor_tensor(small[:, 1:2], st[:, 1:2], st[:, 4:5], ALU.subtract)
                link(V.tensor_tensor(small[:, 2:3], st[:, 2:3], st[:, 5:6], ALU.add))
                link(V.tensor_tensor(small[:, 1:2], small[:, 1:2], small[:, 1:2], ALU.mult))
                dve.wait_ge(s_row0, 2)
                for n, (rows_, key) in enumerate(((0, fd), (1, fd), (0, ld), (1, ld))):
                    link(V.tensor_scalar(cross[:, n, :], bank[rows_][0:EP, 0:EP], key, None, ALU.is_equal))
                V.tensor_copy(carry_lhs[:, :], cross[:, 2, :]).then_inc(s_p0, 1)
                V.scalar_tensor_tensor(out=small[:, 3:4], in0=small[:, 1:2], scalar=float(F // 4),
                                       in1=small[:, 2:3], op0=ALU.mult, op1=ALU.add).then_inc(s_p0, 1)
                link(V.tensor_tensor(nz[:, :], fd, ld, ALU.not_equal))
                link(V.tensor_scalar(cross_pen[:, :, :], cross[:, :, :], -1.0, BIG, ALU.add, ALU.mult))
                link(V.tensor_scalar(cross_sum[:, 0, :], cross[:, 2, :], nz[:, :], None, ALU.mult))
                link(V.tensor_scalar(cross_sum[:, 1, :], cross[:, 3, :], nz[:, :], None, ALU.mult))
                link(V.memset(same[:, :], 0.0))
                link(V.memset(same_n[:, :], 0.0))
                link(V.tensor_tensor(same[:, 1:EJ], dst_f[:, 1:EJ], dst_f[:, 0:EJ - 1], ALU.is_equal))
                link(V.tensor_copy(same_n[:, 0:EJ - 1], same[:, 1:EJ]))
                link(V.tensor_scalar(first[:, :], dst_f[:, :], fd, None, ALU.is_equal))
                link(V.tensor_scalar(in_last[:, :], dst_f[:, :], ld, None, ALU.is_equal))
                for a, b in ((same, pen_f), (same_n, pen_b), (first, pen_first), (in_last, pen_last)):
                    link(V.tensor_scalar(b[:, :], a[:, :], -1.0, BIG, ALU.add, ALU.mult))
                last = sc[2]
                link(V.tensor_scalar(last[:, :], same_n[:, :], -1.0, 1.0, ALU.mult, ALU.add))
                link(V.tensor_copy(small[0:EP, 6:7], dnext[0:EP, :]))
                link(V.tensor_tensor(last[:, EJ - 1:EJ], small[0:EP, 6:7], ld, ALU.not_equal))
                link(V.scalar_tensor_tensor(out=sc[3][:, :], in0=dst_f[:, :], scalar=float(-SKIP), in1=last[:, :],
                                            op0=ALU.add, op1=ALU.mult))
                link(V.tensor_scalar(out_idx[:, :], sc[3][:, :], float(SKIP), None, ALU.add))
                dve.wait_ge(s_st, 2)
                link(V.scalar_tensor_tensor(out=small[:, 2:3], in0=small[:, 0:1], scalar=-0.5, in1=small[:, 5:6],
                                            op0=ALU.mult, op1=ALU.mult))
                link(V.tensor_scalar(bc["c"][:, :], bc["bias"][:, :], small[:, 5:6], small[:, 2:3], ALU.mult, ALU.add))
                link(V.tensor_tensor(bc["c"][:, :], bc["c"][:, :], bc["gamma"][:, :], ALU.mult))
                link(V.tensor_tensor(bc["c"][:, :], bc["c"][:, :], bc["beta"][:, :], ALU.add))

        above = arena[:, :].bitcast(bf16)[0:EP, 0:E].rearrange("k (j p) -> k j p", p=EP)
        step_hi, step_lo = (sb(n, [EP, EJ], bf16) for n in ("step_hi", "step_lo"))
        s_sp, s_sr, s_sc, s_ss, s_sb, s_cst = (sem(n) for n in (
            "search_ready", "row_fetched", "row_counted", "row_signed", "search_done",
            "c_stored"))
        junk_d, junk_a = (sb(n, [EP, 4, EJ], bf16) for n in ("junk_d", "junk_a"))
        qm = sc[4]
        cle, sgn = sc[2], sc[3]
        with nc.Block() as block:
            @block.vector
            def _(dve):
                V = nc.vector
                link(V.tensor_copy(sc[5][:, :], dprev[:, :]))
                link(V.tensor_tensor(sc[2][:, :], dst_f[:, :], sc[5][:, :], ALU.subtract))
                link(V.tensor_scalar(sc[3][:, :], sc[2][:, :], 1.0 / 512, float(3 << 22), ALU.mult, ALU.add))
                link(V.tensor_scalar(sc[3][:, :], sc[3][:, :], float(-(3 << 22)), 512.0, ALU.add, ALU.mult))
                link(V.tensor_copy(step_hi[:, :], sc[3][:, :]))
                link(V.tensor_tensor(step_lo[:, :], sc[2][:, :], sc[3][:, :], ALU.subtract))
                link(V.tensor_scalar(qm[:, :], src_f[:, :], -0.5, None, ALU.add))
                part = EJ // 5
                for q in range(5):
                    view = src_all.rearrange("k (p j) -> k j p", j=EJ)[:, q * part:(q + 1) * part, :]
                    ins = V.tensor_scalar(above[:, q * part:(q + 1) * part, :], view, dst_f[:, 0:1], None, ALU.is_ge)
                    ins.then_inc(s_sp, 1)
                def count(b, u):
                    i = b * 4 + u
                    dve.wait_ge(s_sr, i + 1)
                    V.tensor_scalar(junk_d[:, u, :], bank[u][0:EP, 0:EJ], src_f[:, bass.ds(i, 1)],
                                    None, ALU.is_le, ALU.add, accum_out=cle[:, bass.ds(i, 1)]).then_inc(s_sc, 1)
                with dve.Fori(0, EJ // 4) as b:
                    for u in range(4):
                        count(b, u)
                dve.wait_ge(s_sc, EJ)
                dve.wait_ge(s_ss, EJ)
                dve.wait_ge(s_sb, EJ)
                part_no = sc[5]
                V.tensor_copy(part_no[:, :], bank[4][0:EP, 0:EJ])
                link(V.tensor_scalar(cle[:, :], cle[:, :], 1.0, None, ALU.mult))
                link(V.scalar_tensor_tensor(out=qm[:, :], in0=cle[:, :], scalar=2.0, in1=sgn[:, :], op0=ALU.mult,
                                            op1=ALU.subtract))
                link(V.tensor_scalar(qm[:, :], qm[:, :], float(EJ) + 0.5, None, ALU.is_gt))
                link(V.scalar_tensor_tensor(out=qm[:, :], in0=part_no[:, :], scalar=0.5, in1=qm[:, :], op0=ALU.is_gt,
                                            op1=ALU.mult))
                link(V.scalar_tensor_tensor(out=cle[:, :], in0=part_no[:, :], scalar=float(EJ), in1=cle[:, :],
                                            op0=ALU.mult, op1=ALU.add))
                link(V.scalar_tensor_tensor(out=cle[:, :], in0=cle[:, :], scalar=float(-EJ - 1 - E), in1=qm[:, :],
                                            op0=ALU.add, op1=ALU.mult))
                link(V.tensor_scalar(g_idx[:, :], cle[:, :], float(E), None, ALU.add))

            @block.scalar
            def _(act):
                act.preload_act_table_set("natural_log_exp_and_others")
                def signs(b, u):
                    i = b * 4 + u
                    act.wait_ge(s_sc, i + 1)
                    nc.scalar.activation(junk_a[:, u, :], bank[u][0:EP, 0:EJ], ACT.Sign, bias=qm[:, bass.ds(i, 1)], scale=-1.0,
                                         accum_out=sgn[:, bass.ds(i, 1)]).then_inc(s_ss, 1)
                act.wait_ge(s_sp, 5)
                with act.Fori(0, EJ // 4) as b:
                    for u in range(4):
                        signs(b, u)

            @block.tensor
            def _(pe):
                pe.wait_ge(s_sp, 5)

                def fetch(b, u, head):
                    i = b * 4 + u
                    if not head:
                        pe.wait_ge(s_ss, i - 3)
                    nc.tensor.matmul(bank[u][0:EP, 0:EJ], above[:, bass.ds(i, 1), :].rearrange("k a p -> k (a p)"),
                                     step_hi[:, :], start=True, stop=False)
                    nc.tensor.matmul(bank[u][0:EP, 0:EJ], above[:, bass.ds(i, 1), :].rearrange("k a p -> k (a p)"),
                                     step_lo[:, :], start=False, stop=True).then_inc(s_sr, 1)
                    nc.tensor.matmul(bank[4][0:EP, bass.ds(i, 1)],
                                     above[:, bass.ds(i, 1), :].rearrange("k a p -> k (a p)"),
                                     ones_bf[0:EP, 0:1], start=True, stop=True).then_inc(s_sb, 1)
                for u in range(4):
                    fetch(0, u, True)
                with pe.Fori(1, EJ // 4) as b:
                    for u in range(4):
                        fetch(b, u, False)

            @block.sync
            def _(sp):
                sp.dma_start(g_dram[E:E + 1, :], bc["c"][0:1, :]).then_inc(s_cst, 16)
                sp.wait_ge(s_cst, 16)


        class Norm:
            def __init__(self, tag, parts, k, x_of, more_eps=None):
                self.parts, self.k, self.x_of, self.more_eps = parts, k, x_of, more_eps
                self.st, self.sm, self.ln = sb(f"{tag}_st", [128, k, 6]), sb(f"{tag}_sm", [128, 4, k]), \
                    sb(f"{tag}_ln", [128, k])
                self.r, self.nb = sb(f"{tag}_r", [128, 2, k]), sb(f"{tag}_nb", [128, 2, k])
                self.s_stats, self.s_rstd, self.s_shift, self.s_done_v, self.s_done_a, self.s_links, self.s_alinks = (
                    sem(f"{tag}_{n}") for n in ("stats", "rstd", "shift", "normed_v", "normed_a", "vchain", "achain"))

            def dve_stats(self, dve, it):
                V, p, k = nc.vector, self.parts, self.k
                chain = Chain(dve, self.s_links, 3, it.n)
                for t in range(k):
                    ins = V.bn_stats(self.st[0:p, t, :], self.x_of(it)[:, t, :])
                chain(ins)
                s, d, v, v128 = (self.sm[0:p, q, 0:k] for q in range(4))
                st = self.st[0:p, 0:k, :]
                V.tensor_tensor(s, st[:, :, 1], st[:, :, 4], ALU.add)
                V.tensor_tensor(d, st[:, :, 1], st[:, :, 4], ALU.subtract)
                if self.more_eps:
                    chain(V.scalar_tensor_tensor(out=v, in0=self.more_eps(it), scalar=F * EPS, in1=st[:, :, 2],
                                                 op0=ALU.mult, op1=ALU.add))
                    V.tensor_tensor(v, v, st[:, :, 5], ALU.add)
                else:
                    chain(V.tensor_tensor(v, st[:, :, 2], st[:, :, 5], ALU.add))
                chain(V.tensor_tensor(d, d, d, ALU.mult))
                V.scalar_tensor_tensor(out=v128, in0=d, scalar=float(F // 4), in1=v, op0=ALU.mult, op1=ALU.add)\
                    .then_inc(self.s_stats, 1)
                chain.end()

            def act_rstd(self, act, it):
                p, k = self.parts, self.k
                chain = Chain(act, self.s_alinks, 1, it.n)
                act.wait_ge(self.s_stats, it.n + 1)
                if self.more_eps:
                    chain(nc.scalar.activation(self.ln[0:p, :], self.sm[0:p, 3, :], ACT.Ln, scale=1.0 / F))
                else:
                    chain(nc.scalar.activation(self.ln[0:p, :], self.sm[0:p, 3, :], ACT.Ln, bias=eps_col[0:p, :],
                                               scale=1.0 / F))
                nc.scalar.activation(self.r[0:p, it.ring(2), :], self.ln[0:p, :], ACT.Exp, scale=-0.5)\
                    .then_inc(self.s_rstd, 1)
                chain.end()

            def dve_shift(self, dve, it):
                p = self.parts
                dve.wait_ge(self.s_rstd, it.n + 1)
                nc.vector.scalar_tensor_tensor(out=self.nb[0:p, it.ring(2), :], in0=self.sm[0:p, 0, :], scalar=-0.5,
                                               in1=self.r[0:p, it.ring(2), :], op0=ALU.mult, op1=ALU.mult)\
                    .then_inc(self.s_shift, 1)

            def dve_apply(self, dve, it, tiles_):
                dve.wait_ge(self.s_shift, it.n + 1)
                xb, p, par = self.x_of(it), self.parts, it.ring(2)
                for t in tiles_:
                    ins = nc.vector.tensor_scalar(xb[:, t, :], xb[:, t, :], self.r[0:p, par, t:t + 1],
                                                  self.nb[0:p, par, t:t + 1], ALU.mult, ALU.add)
                ins.then_inc(self.s_done_v, 1)

            def act_apply(self, act, it, tiles_):
                act.wait_ge(self.s_shift, it.n + 1)
                xb, p, par = self.x_of(it), self.parts, it.ring(2)
                for t in tiles_:
                    ins = nc.scalar.activation(xb[:, t, :], xb[:, t, :], ACT.Identity, scale=self.r[0:p, par, t:t + 1],
                                               bias=self.nb[0:p, par, t:t + 1])
                ins.then_inc(self.s_done_a, 1)

        class Layer:
            def __init__(self, tag, parts, k, x_of, z_of, xt, junk, banks, weights, m_of=None, mt=None, gated=True):
                self.wx, self.wm, self.bias3, self.gain, self.beta = weights
                self.gated, self.width = gated, F + 1 if gated else F
                self.parts, self.k, self.groups, self.quad = parts, k, k // QT, QT * parts
                self.x_of, self.z_of, self.xt, self.junk, self.m_of, self.mt = x_of, z_of, xt, junk, m_of, mt
                self.banks, self.nb = banks, len(banks[0])
                self.per_bank = -(-k // self.nb)
                names = ["x_ready", "transposed", "copied", "products", "squared", "scales", "scaled", "shifted",
                         "chain_scales"] + (["relued", "chain_z", "y_done"] if gated else [])
                self.s = {n: sem(f"{tag}_{n}") for n in names}
                self.scal = sb(f"{tag}_scal", [128, 7, 2, k])
                if gated:
                    self.last = Norm(tag + "_out", parts, k, x_of, more_eps=lambda it: self.q(self.G2, it))

            SQ, LNH, RS, EX, KX, G, G2 = range(7)

            def q(self, n, it):
                return self.scal[0:self.parts, n, it.ring(2), :]

            def cuts(self):
                return [range(b * self.per_bank, min(self.k, (b + 1) * self.per_bank)) for b in range(self.nb)]

            def h(self, it, t, width=None):
                bank_no = self.banks[it.ring(len(self.banks))][t // self.per_bank]
                at = (t % self.per_bank) * self.width
                return bank[bank_no][0:self.parts, at:at + (width or F)]

            def gate_cols(self, it, b):
                n = len(self.cuts()[b])
                full = bank[self.banks[it.ring(len(self.banks))][b]][0:self.parts, 0:n * self.width]
                return full.rearrange("p (k w) -> p k w", w=self.width)[:, :, F]

            def pe_transpose(self, pe, it):
                s, p = self.s, self.parts
                for g in range(self.groups):
                    after(pe, s["copied"], self.groups * (it.n - 1) + g + 1)
                    for t in range(QT):
                        ins = nc.tensor.transpose(bank[g][:, t * p:(t + 1) * p], self.x_of(it)[:, g * QT + t, :],
                                                  ident[0:p, 0:p])
                    if self.m_of:
                        for t in range(QT):
                            ins = nc.tensor.transpose(bank[1][:, t * p:(t + 1) * p], self.m_of(it)[:, t, :],
                                                      ident[0:p, 0:p])
                    ins.then_inc(s["transposed"], 1)

            def act_copy(self, act, it):
                s, par = self.s, it.ring(2)
                after(act, s["products"], self.nb * (it.n - 1))
                for g in range(self.groups):
                    act.wait_ge(s["transposed"], self.groups * it.n + g + 1)
                    ins = nc.scalar.activation(self.xt[par][:, g * self.quad:(g + 1) * self.quad],
                                               bank[g][:, 0:self.quad], ACT.Copy)
                    if self.m_of:
                        ins = nc.scalar.activation(self.mt[par][:, :], bank[1][:, 0:self.quad], ACT.Copy)
                    ins.then_inc(s["copied"], 1)

            def pe_products(self, pe, it):
                s, p, par = self.s, self.parts, it.ring(2)
                for b, tiles_ in enumerate(self.cuts()):
                    pe.wait_ge(s["copied"], self.groups * it.n + tiles_[-1] // QT + 1)
                    after(pe, s["scaled"], self.nb * (it.n - len(self.banks)) + b + 1)
                    whole = bank[self.banks[it.ring(len(self.banks))][b]][0:p, 0:len(tiles_) * self.width]
                    nc.tensor.matmul(whole, ones_bf[0:3, 0:p], self.bias3[0:3, 0:len(tiles_) * self.width],
                                     start=True, stop=False)
                    for t in tiles_:
                        last = t == tiles_[-1]
                        ins = nc.tensor.matmul(self.h(it, t, self.width), self.xt[par][:, t * p:(t + 1) * p],
                                               self.wx[:, 0:self.width], start=False, stop=last and not self.m_of)
                        if self.m_of:
                            ins = nc.tensor.matmul(self.h(it, t), self.mt[par][:, t * p:(t + 1) * p], self.wm[:, :],
                                                   start=False, stop=last)
                    ins.then_inc(s["products"], 1)

            def act_scales(self, act, it):
                s, p = self.s, self.parts
                chain = Chain(act, s["chain_scales"], 2, it.n)
                for b, tiles_ in enumerate(self.cuts()):
                    act.wait_ge(s["products"], self.nb * it.n + b + 1)
                    if self.gated:
                        nc.scalar.activation(self.q(self.EX, it)[:, tiles_[0]:tiles_[-1] + 1], self.gate_cols(it, b),
                                             ACT.Exp, scale=-1.0)
                    for t in tiles_:
                        ins = nc.scalar.activation(self.junk[0:p, t, :], self.h(it, t), ACT.Square,
                                                   accum_out=self.q(self.SQ, it)[:, t:t + 1])
                chain(ins)
                chain(nc.scalar.activation(self.q(self.LNH, it), self.q(self.SQ, it), ACT.Ln, bias=eps_col[0:p, :],
                                           scale=1.0 / F))
                nc.scalar.activation(self.q(self.RS, it), self.q(self.LNH, it), ACT.Exp, scale=-0.5)\
                    .then_inc(s["scales"], 1)
                chain.end()

            def dve_z(self, dve, it):
                s, V = self.s, nc.vector
                dve.wait_ge(s["scales"], it.n + 1)
                if self.gated:
                    chain = Chain(dve, s["chain_z"], 1, it.n)
                    g, kx = self.q(self.G, it), self.q(self.KX, it)
                    chain(V.tensor_scalar(g, self.q(self.EX, it), GATE_CAP, 1.0, ALU.min, ALU.add))
                    V.tensor_tensor(self.q(self.G2, it), g, g, ALU.mult)
                    V.tensor_scalar(kx, g, 2.0, -1.0, ALU.mult, ALU.add)
                    chain.end()
                for tiles_ in self.cuts():
                    for t in tiles_:
                        ins = V.scalar_tensor_tensor(out=self.z_of(it)[:, t, :], in0=self.h(it, t),
                                                     scalar=self.q(self.RS, it)[:, t:t + 1],
                                                     in1=self.gain[0:self.parts, :], op0=ALU.mult, op1=ALU.mult)
                    ins.then_inc(s["scaled"], 1)

            def shift(self, eng, it):
                eng.wait_ge(self.s["scaled"], self.nb * (it.n + 1))
                eng.tensor_tensor(self.z_of(it), self.z_of(it), bcast(self.beta, self.parts, self.k), ALU.add)\
                    .then_inc(self.s["shifted"], 1)

            def act_relu(self, act, it):
                act.wait_ge(self.s["shifted"], it.n + 1)
                nc.scalar.activation(self.z_of(it), self.z_of(it), ACT.Relu).then_inc(self.s["relued"], 1)

            def dve_y(self, dve, it):
                s = self.s
                dve.wait_ge(s["relued"], it.n + 1)
                xb = self.x_of(it)
                for t in range(self.k):
                    ins = nc.vector.scalar_tensor_tensor(out=xb[:, t, :], in0=xb[:, t, :],
                                                         scalar=self.q(self.KX, it)[:, t:t + 1],
                                                         in1=self.z_of(it)[:, t, :], op0=ALU.mult, op1=ALU.add)
                ins.then_inc(s["y_done"], 1)

            def dve_y_stats(self, dve, it):
                dve.wait_ge(self.s["y_done"], it.n + 1)
                self.last.dve_stats(dve, it)

        def carve():
            at = [0]

            def take(parts, *shape):
                size = 1
                for n in shape:
                    size *= n
                v = arena[0:parts, at[0]:at[0] + size]
                at[0] += size
                assert at[0] <= 12800
                return v if len(shape) == 1 else v.rearrange("p (a b) -> p a b", a=shape[0]) if len(shape) == 2 \
                    else v.rearrange("p (a b c) -> p a b c", a=shape[0], b=shape[1])
            return take

        def tiles(buf, it):
            return buf[:, it.ring(buf.shape[1]), :].rearrange("p (k f) -> p k f", f=F)

        take = carve()
        xbuf = take(128, U, T * F)
        z_dense = take(128, 2, T * F)
        xt_dense = [take(128, T * 128) for _ in range(2)]
        junk2 = take(128, T * F // 2).bitcast(bf16).rearrange("p (k f) -> p k f", f=F)
        rows2 = take(EP, 2, 4 * F)
        rows2t = take(128, 4 * EP)
        idx2 = sb("idx2", [EP, 2, 4], i32)
        scores = alpha

        dense = Layer("dense", NP, T, lambda it: tiles(xbuf, it), lambda it: tiles(z_dense, it), xt_dense, junk2,
                      [[2, 3, 4]], (w_ut, None, bias_u, bc["ug"], bc["ubeta"]))
        norm1 = Norm("norm1", NP, T, lambda it: tiles(xbuf, it))
        s_rows = [sem(f"rows_in{n}") for n in range(2)]
        s_spill = [sem(f"rows_out{n}") for n in range(2)]
        s_cadd, s_icp, s_rt, s_rc, s_sf, s_fc = (sem(n) for n in (
            "c_added", "idx_copied", "rows_transposed", "rows_copied", "scored", "feat_copied"))
        PAIRS = EJ // 2
        STEPS2 = max(PAIRS + 1, CHUNKS + 4)

        def start_of(it):
            return LAST_START if it.known and it.n == CHUNKS - 1 else it.n * CHUNK

        with nc.Block() as block:
            @block.sync
            def _(sp):
                def body(step):
                    chunk = step.back(-1)
                    if chunk.on(CHUNKS):
                        after(sp, ring_out.of(chunk), ring_out.before(chunk))
                        sp.dma_start(tiles(xbuf, chunk), node_rows(x, start_of(chunk))).then_inc(ring_in.of(chunk), 16)
                    pair = step.back(1)
                    if pair.on(PAIRS):
                        p2 = pair.ring(2)
                        sp.wait_ge(s_rows[p2], 64 * (pair.uses(2) + 1))
                        sp.dma_start(edge_rows(xs_dram, pair.n * 2, 2), tiles(rows2, pair)[:, 0:2, :])\
                            .then_inc(s_spill[p2], 16)
                        sp.dma_start(edge_rows(xd_dram, pair.n * 2, 2), tiles(rows2, pair)[:, 2:4, :])\
                            .then_inc(s_spill[p2], 16)
                    chunk = step.back(4)
                    if chunk.on(CHUNKS):
                        sp.wait_ge(dense.last.s_done_v, chunk.n + 1)
                        sp.wait_ge(dense.last.s_done_a, chunk.n + 1)
                        if chunk.known and chunk.n == CHUNKS - 1:
                            before = chunk.back(1)
                            sp.wait_ge(ring_out.of(before), ring_out.done(before))
                        sp.dma_start(node_rows(out, start_of(chunk)), tiles(xbuf, chunk))\
                            .then_inc(ring_out.of(chunk), 16)

                sp.dma_start(tiles(xbuf, Item(0, 0)), node_rows(x, 0)).then_inc(ring_in.of(Item(0, 0)), 16)
                run_steps(sp, body, STEPS2, min(PAIRS, CHUNKS))
                ring_out.wait_all(sp, CHUNKS)
                for n in range(2):
                    sp.wait_ge(s_spill[n], 32 * (PAIRS // 2))

            @block.gpsimd
            def _(pool):
                def body(it):
                    chunk = it.back(-1)
                    if it.known and it.n == 0:
                        cadd(it)
                    if it.on(PAIRS):
                        p2 = it.ring(2)
                        after(pool, s_spill[p2], 32 * it.uses(2))
                        after(pool, s_rt, it.n - 1)
                        nc.gpsimd.tensor_copy(idx2[:, p2, 0:2], src_i[:, bass.ds(it.n * 2, 2)])
                        nc.gpsimd.tensor_copy(idx2[:, p2, 2:4], dst_i[:, bass.ds(it.n * 2, 2)]).then_inc(s_icp, 1)
                        pool.wait_ge(s_icp, it.n + 1)
                        pool.sem_inc(s_go, 1)
                        for k in range(4):
                            nc.gpsimd.indirect_dma_start(
                                out=rows2[:, p2, k * F:(k + 1) * F], out_offset=None, in_=x,
                                in_offset=bass.IndirectOffsetOnAxis(ap=idx2[:, p2, k:k + 1], axis=0))\
                                .then_inc(s_rows[p2], 16)
                    if chunk.on(CHUNKS):
                        cadd(chunk)
                    if it.back(2).on(CHUNKS):
                        dense.shift(pool, it.back(2))

                def cadd(chunk):
                    pool.wait_ge(ring_in.of(chunk), ring_in.done(chunk))
                    nc.gpsimd.tensor_tensor(tiles(xbuf, chunk), tiles(xbuf, chunk), bcast(bc["c"], NP, T), ALU.add)\
                        .then_inc(s_cadd, 1)
                run_steps(pool, body, STEPS2, min(PAIRS, CHUNKS))

            @block.vector
            def _(dve):
                def body(it):
                    if it.on(CHUNKS):
                        dve.wait_ge(s_cadd, it.n + 1)
                        norm1.dve_stats(dve, it)
                    if it.back(4).on(CHUNKS):
                        dense.last.dve_shift(dve, it.back(4))
                    if it.back(2).on(CHUNKS):
                        dense.dve_z(dve, it.back(2))
                    if it.back(4).on(CHUNKS):
                        dense.last.dve_apply(dve, it.back(4), range(OUT_SPLIT, T))
                    if it.back(3).on(CHUNKS):
                        dense.dve_y(dve, it.back(3))
                    if it.on(CHUNKS):
                        norm1.dve_shift(dve, it)
                    if it.back(3).on(CHUNKS):
                        dense.dve_y_stats(dve, it.back(3))
                run_steps(dve, body, STEPS2, min(PAIRS, CHUNKS))

            @block.scalar
            def _(act):
                act.preload_act_table_set("natural_log_exp_and_others")

                def body(it):
                    chunk = it.back(1)
                    if chunk.on(CHUNKS):
                        dense.act_copy(act, chunk)
                    if it.back(4).on(CHUNKS):
                        dense.last.act_apply(act, it.back(4), range(OUT_SPLIT))
                    if chunk.on(PAIRS):
                        act.wait_ge(s_rt, chunk.n + 1)
                        after(act, s_sf, chunk.n)
                        nc.scalar.activation(rows2t[:, :], bank[6][:, 0:4 * EP], ACT.Copy).then_inc(s_rc, 1)
                    if it.on(CHUNKS):
                        norm1.act_rstd(act, it)
                    if chunk.on(CHUNKS):
                        dense.act_scales(act, chunk)
                    if it.on(CHUNKS):
                        norm1.act_apply(act, it, range(T))
                    if it.back(3).on(CHUNKS):
                        dense.last.act_rstd(act, it.back(3))
                    if it.back(2).on(CHUNKS):
                        dense.act_relu(act, it.back(2))
                    if chunk.on(PAIRS):
                        act.wait_ge(s_sf, chunk.n + 1)
                        got = bank[7][0:EP, 0:2 * (F + HEADS)].rearrange("p (k f) -> p k f", k=2)
                        nc.scalar.activation(
                            edge_feat[:, bass.ds(chunk.n * 2 * F, 2 * F)].rearrange("p (k f) -> p k f", k=2),
                            got[:, :, 0:F], ACT.Copy)
                        nc.scalar.activation(
                            scores[:, bass.ds(chunk.n * 2 * HEADS, 2 * HEADS)].rearrange("p (k f) -> p k f", k=2),
                            got[:, :, F:F + HEADS], ACT.Copy).then_inc(s_fc, 1)
                run_steps(act, body, STEPS2, min(PAIRS, CHUNKS))

            @block.tensor
            def _(pe):
                def body(it):
                    pair = it.back(1)
                    if it.back(1).on(CHUNKS):
                        pe.wait_ge(norm1.s_done_a, pair.n + 1)
                        dense.pe_transpose(pe, pair)
                    if pair.on(PAIRS):
                        pe.wait_ge(s_rows[pair.ring(2)], 64 * (pair.uses(2) + 1))
                        after(pe, s_rc, pair.n)
                        for k in range(4):
                            ins = nc.tensor.transpose(bank[6][:, k * EP:(k + 1) * EP],
                                                      tiles(rows2, pair)[:, k, :], ident[0:EP, 0:EP])
                        ins.then_inc(s_rt, 1)
                    if pair.on(CHUNKS):
                        dense.pe_products(pe, pair)
                    if pair.on(PAIRS):
                        pe.wait_ge(s_rc, pair.n + 1)
                        after(pe, s_fc, pair.n)
                        for k in range(2):
                            at = k * (F + HEADS)
                            nc.tensor.matmul(bank[7][0:EP, at:at + F + HEADS], rows2t[:, k * EP:(k + 1) * EP],
                                             w_gat[:, :], start=True, stop=False)
                            ins = nc.tensor.matmul(bank[7][0:EP, at + F:at + F + HEADS],
                                                   rows2t[:, (2 + k) * EP:(3 + k) * EP], v_er[:, :], start=False,
                                                   stop=True)
                        ins.then_inc(s_sf, 1)
                run_steps(pe, body, STEPS2, min(PAIRS, CHUNKS))

        ring_in.end_phase(CHUNKS)
        ring_out.end_phase(CHUNKS)

        take = carve()
        score, ex, den = (take(EP, HEADS + 1, EJ) for _ in range(3))
        run_f, run_all = take(EP, EJ), take(EP, EJ)
        diag = take(EP, 2, EP)
        junk3 = take(EP, EP)
        ends = take(EP, 2, 4)
        mx = take(EP, 8)
        s_dg, s_rows3, s_ex, s_en, s_tt = (sem(n) for n in (
            "ends_ready", "end_rows", "exps_ready", "sums_ready", "totals_ready"))
        with nc.Block() as block:
            @block.scalar
            def _(act):
                act.preload_act_table_set("natural_log_exp_and_others")
                act.wait_ge(s_ex, 1)
                nc.scalar.activation(ex[:, 0:HEADS, :], ex[:, 0:HEADS, :], ACT.Exp).then_inc(s_ex, 1)

            @block.tensor
            def _(pe):
                for n in range(HEADS + 1):
                    pe.wait_ge(s_dg, n + 1)
                    nc.tensor.matmul(bank[n][0:EP, 0:EP], ones[0:EP, 0:EP], diag[:, 0, :], start=True, stop=True)
                    nc.tensor.matmul(bank[n][0:EP, 128:128 + EP], ones[0:EP, 0:EP], diag[:, 1, :], start=True,
                                     stop=True).then_inc(s_rows3, 1)
                pe.wait_ge(s_en, 1)
                a, b = ends[:, 0, 0:HEADS + 1], ends[:, 1, 0:HEADS + 1]
                nc.tensor.matmul(bank[3][0:EP, 0:HEADS + 1], cross[:, 0, :], a, start=True, stop=False)
                nc.tensor.matmul(bank[3][0:EP, 0:HEADS + 1], cross_sum[:, 0, :], b, start=False, stop=True)
                nc.tensor.matmul(bank[3][0:EP, 8:9 + HEADS], cross[:, 1, :], a, start=True, stop=False)
                nc.tensor.matmul(bank[3][0:EP, 8:9 + HEADS], cross_sum[:, 1, :], b, start=False, stop=True)\
                    .then_inc(s_tt, 1)

            @block.vector
            def _(dve):
                V = nc.vector
                by_head = scores[:, :].rearrange("p (j h) -> p h j", h=HEADS)
                link(V.tensor_copy(score[:, 0:HEADS, :], by_head))
                link(V.scalar_tensor_tensor(out=score[:, 0:HEADS, :], in0=score[:, 0:HEADS, :], scalar=0.2,
                                            in1=score[:, 0:HEADS, :], op0=ALU.mult, op1=ALU.max))
                link(V.tensor_copy(score[:, HEADS, :], sc[1][:, :]))
                for n in range(HEADS + 1):
                    link(V.tensor_tensor_scan(run_f[:, :], pen_f[:, :], score[:, n, :], -BIG, ALU.add, ALU.max))
                    link(V.tensor_tensor_scan(run_all[:, ::-1], pen_b[:, ::-1], run_f[:, ::-1], -BIG, ALU.add, ALU.max))
                    link(V.tensor_scalar(diag[:, 0, :], ident[0:EP, 0:EP], run_all[:, 0:1], None, ALU.mult))
                    V.tensor_scalar(diag[:, 1, :], ident[0:EP, 0:EP], run_all[:, EJ - 1:EJ], None, ALU.mult)\
                        .then_inc(s_dg, 1)
                    dve.wait_ge(s_rows3, n + 1)
                    for q in range(4):
                        row = bank[n][0:EP, 128 * (q % 2):128 * (q % 2) + EP]
                        link(V.tensor_tensor_reduce(out=junk3[:, :], in0=cross_pen[:, q, :], in1=row, scale=1.0,
                                                    scalar=-BIG, op0=ALU.add, op1=ALU.max, accum_out=mx[:, q:q + 1]))
                    V.tensor_tensor(mx[:, 4:5], mx[:, 0:1], mx[:, 1:2], ALU.max)
                    link(V.tensor_tensor(mx[:, 5:6], mx[:, 2:3], mx[:, 3:4], ALU.max))
                    link(V.scalar_tensor_tensor(out=den[:, n, :], in0=pen_first[:, :], scalar=mx[:, 4:5],
                                                in1=run_all[:, :], op0=ALU.add, op1=ALU.max))
                    link(V.scalar_tensor_tensor(out=den[:, n, :], in0=pen_last[:, :], scalar=mx[:, 5:6],
                                                in1=den[:, n, :], op0=ALU.add, op1=ALU.max))
                V.tensor_copy(x1_idx[:, :], den[:, HEADS, :])
                V.tensor_tensor(ex[:, 0:HEADS, :], score[:, 0:HEADS, :], den[:, 0:HEADS, :], ALU.subtract)\
                    .then_inc(s_ex, 1)
                link(V.memset(ex[:, HEADS, :], 1.0))
                dve.wait_ge(s_ex, 2)
                for n in range(HEADS + 1):
                    link(V.tensor_tensor_scan(run_f[:, :], same[:, :], ex[:, n, :], 0.0, ALU.mult, ALU.add))
                    link(V.tensor_tensor_scan(den[:, n, ::-1], same_n[:, ::-1], run_f[:, ::-1], 0.0, ALU.mult, ALU.max))
                V.tensor_copy(ends[:, 0, 0:HEADS + 1], den[:, :, 0])
                V.tensor_copy(ends[:, 1, 0:HEADS + 1], den[:, :, EJ - 1]).then_inc(s_en, 1)
                dve.wait_ge(s_tt, 1)
                link(V.tensor_copy(mx[:, 0:3], bank[3][0:EP, 0:3]))
                link(V.tensor_copy(mx[:, 4:7], bank[3][0:EP, 8:11]))
                for n in range(HEADS + 1):
                    link(V.scalar_tensor_tensor(out=den[:, n, :], in0=first[:, :], scalar=mx[:, n:n + 1],
                                                in1=den[:, n, :], op0=ALU.mult, op1=ALU.max))
                    link(V.scalar_tensor_tensor(out=den[:, n, :], in0=in_last[:, :], scalar=mx[:, 4 + n:5 + n],
                                                in1=den[:, n, :], op0=ALU.mult, op1=ALU.max))
                link(V.tensor_scalar(den[:, HEADS, :], den[:, HEADS, :], 1e-8, None, ALU.add))
                link(V.reciprocal(den[:, :, :], den[:, :, :]))
                V.tensor_copy(rcnt[:, :], den[:, HEADS, :])
                link(V.tensor_tensor(alpha[:, :].rearrange("p (j h) -> p h j", h=HEADS), ex[:, 0:HEADS, :],
                                     den[:, 0:HEADS, :], ALU.mult))

        s_v, s_f, s_cy = (sem(n) for n in ("weighted", "summed", "carry_ready"))
        with nc.Block() as block:
            @block.gpsimd
            def _(pool):
                with pool.Fori(0, EG) as i:
                    v = edge_feat[:, bass.ds(i * QT * F, QT * F)].rearrange("p (a f) -> p a f", f=FO)
                    w = alpha[:, bass.ds(i * QT * HEADS, QT * HEADS)].rearrange("p (a b) -> p a b", b=1)
                    nc.gpsimd.tensor_tensor(v, v, w.to_broadcast([EP, QT * HEADS, FO]), ALU.mult).then_inc(s_v, 1)

            @block.vector
            def _(dve):
                V = nc.vector

                def add(i, t):
                    j = i * QT + t
                    if isinstance(i, int) and j == 0:
                        return
                    before = edge_feat[:, bass.ds((j - 1) * F, F)]
                    here = edge_feat[:, bass.ds(j * F, F)]
                    V.scalar_tensor_tensor(out=here, in0=before, scalar=same[:, bass.ds(j, 1)], in1=here,
                                           op0=ALU.mult, op1=ALU.add).then_inc(s_f, 1)
                    dve.wait_ge(s_f, j)
                dve.wait_ge(s_v, 1)
                for t in range(QT):
                    add(0, t)
                with dve.Fori(1, EG) as i:
                    dve.wait_ge(s_v, i + 1)
                    for t in range(QT):
                        add(i, t)
                dve.wait_ge(s_cy, 1)
                V.tensor_copy(carry[:, :], bank[0][0:EP, 0:F])

            @block.tensor
            def _(pe):
                pe.wait_ge(s_f, EJ - 1)
                nc.tensor.matmul(bank[0][0:EP, 0:F], carry_lhs[:, :], edge_feat[:, (EJ - 1) * F:EJ * F], start=True,
                                 stop=True).then_inc(s_cy, 1)

        take = carve()
        gbuf, dbuf = take(EP, U, QT * F), take(EP, U, QT * F)
        ring_g = Ring("g_stored")
        s_tot, s_bias, s_gain, s_gg, s_uu = (sem(n) for n in ("total", "bias_added", "gained", "g_ready", "u_ready"))
        norm_g = Norm("norm_g", EP, QT, lambda it: tiles(gbuf, it))
        norm_x = Norm("norm_x", EP, QT, lambda it: tiles(dbuf, it))

        with nc.Block() as block:
            @block.sync
            def _(sp):
                def body(step):
                    it = step.back(-1)
                    if it.on(EG):
                        after(sp, ring_out.of(it), ring_out.before(it))
                        sp.dma_start(tiles(dbuf, it), edge_rows(xd_dram, it.n * QT, QT)).then_inc(ring_in.of(it), 16)
                    it = step.back(2)
                    if it.on(EG):
                        sp.wait_ge(s_gg, it.n + 1)
                        sp.dma_start(edge_rows(g_dram, it.n * QT, QT), tiles(gbuf, it)).then_inc(ring_g.of(it), 16)
                    it = step.back(4)
                    if it.on(EG):
                        sp.wait_ge(norm_x.s_done_a, it.n + 1)
                        sp.dma_start(edge_rows(x1_dram, it.n * QT, QT), tiles(dbuf, it)).then_inc(ring_out.of(it), 16)
                sp.dma_start(tiles(dbuf, Item(0, 0)), edge_rows(xd_dram, 0, QT)).then_inc(ring_in.of(Item(0, 0)), 16)
                run_steps(sp, body, EG + 4, EG)
                ring_g.wait_all(sp, EG)
                ring_out.wait_all(sp, EG)

            @block.vector
            def _(dve):
                V = nc.vector

                def body(it):
                    if it.on(EG):
                        after(dve, ring_g.of(it), ring_g.before(it))
                        for t in range(QT):
                            j = it.n * QT + t
                            ins = V.scalar_tensor_tensor(out=tiles(gbuf, it)[:, t, :], in0=carry[:, :],
                                                         scalar=first[:, bass.ds(j, 1)],
                                                         in1=edge_feat[:, bass.ds(j * F, F)], op0=ALU.mult, op1=ALU.add)
                        ins.then_inc(s_tot, 1)
                    one, two = it.back(1), it.back(3)
                    if one.on(EG):
                        dve.wait_ge(s_bias, one.n + 1)
                        norm_g.dve_stats(dve, one)
                    if two.on(EG):
                        dve.wait_ge(s_uu, two.n + 1)
                        norm_x.dve_stats(dve, two)
                    if one.on(EG):
                        norm_g.dve_shift(dve, one)
                    if two.on(EG):
                        norm_x.dve_shift(dve, two)
                run_steps(dve, body, EG + 3, EG)

            @block.scalar
            def _(act):
                act.preload_act_table_set("natural_log_exp_and_others")

                def body(it):
                    one, two = it.back(1), it.back(3)
                    if one.on(EG):
                        norm_g.act_rstd(act, one)
                    if two.on(EG):
                        norm_x.act_rstd(act, two)
                    if one.on(EG):
                        norm_g.act_apply(act, one, range(QT))
                    if two.on(EG):
                        norm_x.act_apply(act, two, range(QT))
                run_steps(act, body, EG + 3, EG)

            @block.gpsimd
            def _(pool):
                G = nc.gpsimd

                def body(it):
                    if it.on(EG):
                        pool.wait_ge(s_tot, it.n + 1)
                        G.tensor_tensor(tiles(gbuf, it), tiles(gbuf, it), bcast(bc["bias"], EP, QT), ALU.add)\
                            .then_inc(s_bias, 1)
                    it = it.back(2)
                    if it.on(EG):
                        g, u = tiles(gbuf, it), tiles(dbuf, it)
                        pool.wait_ge(norm_g.s_done_a, it.n + 1)
                        G.tensor_tensor(g, g, bcast(bc["gamma"], EP, QT), ALU.mult).then_inc(s_gain, 1)
                        pool.wait_ge(s_gain, it.n + 1)
                        G.tensor_tensor(g, g, bcast(bc["beta"], EP, QT), ALU.add).then_inc(s_gg, 1)
                        pool.wait_ge(s_gg, it.n + 1)
                        pool.wait_ge(ring_in.of(it), ring_in.done(it))
                        G.tensor_tensor(u, u, g, ALU.add).then_inc(s_uu, 1)
                run_steps(pool, body, EG + 2, EG)

        ring_in.end_phase(EG)

        take = carve()
        sbuf = take(EP, U, QT * F)
        grow, drow = take(EP, 3, QT * F), take(EP, 3, QT * F)
        z6 = take(EP, 1, QT * F)
        xt6, mt6 = ([take(128, QT * EP) for _ in range(2)] for _ in range(2))
        junk6 = take(EP, QT * F // 2).bitcast(bf16).rearrange("p (k f) -> p k f", f=F)
        idx6 = sb("idx6", [EP, 3, 2 * QT], i32)
        norm_s = Norm("norm_s", EP, QT, lambda it: tiles(sbuf, it))
        msg = Layer("msg", EP, QT, lambda it: tiles(sbuf, it), lambda it: tiles(z6, it), xt6, junk6, [[2], [3]],
                    (w_ma, w_mb, bias_m, bc["mg"], bc["mbeta"]), m_of=lambda it: tiles(drow, it), mt=mt6,
                    gated=False)
        s_gin = [sem(f"gathered{n}") for n in range(3)]
        s_icp6, s_u6, s_w6, s_f6, s_cy6 = (sem(n) for n in (
            "idx6_copied", "m_u", "m_weighted", "m_summed", "carry6_ready"))
        with nc.Block() as block:
            @block.sync
            def _(sp):
                def body(step):
                    it = step.back(-1)
                    if it.on(EG):
                        after(sp, msg.s["transposed"], it.n - U + 1)
                        sp.dma_start(tiles(sbuf, it), edge_rows(xs_dram, it.n * QT, QT)).then_inc(ring_in.of(it), 16)
                sp.dma_start(tiles(sbuf, Item(0, 0)), edge_rows(xs_dram, 0, QT)).then_inc(ring_in.of(Item(0, 0)), 16)
                run_steps(sp, body, EG, EG)

            @block.gpsimd
            def _(pool):
                def body(it):
                    r3 = it.ring(3)
                    after(pool, msg.s["transposed"], it.n - 2)
                    after(pool, s_gin[r3], 16 * 2 * QT * it.uses(3))
                    cols = idx6[:, r3, :]
                    nc.gpsimd.tensor_copy(cols[:, 0:QT], g_idx[:, bass.ds(it.n * QT, QT)])
                    nc.gpsimd.tensor_copy(cols[:, QT:2 * QT], x1_idx[:, bass.ds(it.n * QT, QT)]).then_inc(s_icp6, 1)
                    pool.wait_ge(s_icp6, it.n + 1)
                    pool.sem_inc(s_go, 1)
                    for k in range(2 * QT):
                        rows, table = (grow, g_dram) if k < QT else (drow, x1_dram)
                        nc.gpsimd.indirect_dma_start(
                            out=rows[:, r3, (k % QT) * F:(k % QT + 1) * F], out_offset=None, in_=table,
                            in_offset=bass.IndirectOffsetOnAxis(ap=cols[:, k:k + 1], axis=0))\
                            .then_inc(s_gin[r3], 16)
                run_steps(pool, body, EG, EG)

            @block.vector
            def _(dve):
                V = nc.vector

                def body(it):
                    new, old = it.back(1), it.back(3)
                    if new.on(EG):
                        dve.wait_ge(ring_in.of(new), ring_in.done(new))
                        dve.wait_ge(s_gin[new.ring(3)], 16 * 2 * QT * (new.uses(3) + 1))
                        V.tensor_tensor(tiles(sbuf, new), tiles(sbuf, new), tiles(grow, new), ALU.add)\
                            .then_inc(s_u6, 1)
                        dve.wait_ge(s_u6, new.n + 1)
                        norm_s.dve_stats(dve, new)
                    if old.on(EG):
                        msg.dve_z(dve, old)
                        msg.shift(nc.vector, old)
                    if new.on(EG):
                        norm_s.dve_shift(dve, new)
                    if old.on(EG):
                        dve.wait_ge(msg.s["shifted"], old.n + 1)
                        z = tiles(z6, old)
                        for t in range(QT):
                            j = old.n * QT + t
                            to = edge_feat[:, 0:F] if old.known and j == 0 else z[:, t, :]
                            ins = V.tensor_scalar(to, z[:, t, :], 0.0, w_edge[:, bass.ds(j, 1)], ALU.max, ALU.mult)
                        ins.then_inc(s_w6, 1)
                        dve.wait_ge(s_w6, old.n + 1)
                        for t in range(QT):
                            j = old.n * QT + t
                            if old.known and j == 0:
                                continue
                            V.scalar_tensor_tensor(out=edge_feat[:, bass.ds(j * F, F)],
                                                   in0=edge_feat[:, bass.ds((j - 1) * F, F)],
                                                   scalar=same[:, bass.ds(j, 1)], in1=z[:, t, :],
                                                   op0=ALU.mult, op1=ALU.add).then_inc(s_f6, 1)
                            dve.wait_ge(s_f6, j)
                run_steps(dve, body, EG + 3, EG)
                dve.wait_ge(s_cy6, 1)
                V.tensor_copy(carry[:, :], bank[4][0:EP, 0:F])

            @block.scalar
            def _(act):
                act.preload_act_table_set("natural_log_exp_and_others")

                def body(it):
                    new, old = it.back(1), it.back(2)
                    if new.on(EG):
                        norm_s.act_rstd(act, new)
                    if old.on(EG):
                        msg.act_scales(act, old)
                    if new.on(EG):
                        norm_s.act_apply(act, new, range(QT))
                        msg.act_copy(act, new)
                run_steps(act, body, EG + 2, EG)

            @block.tensor
            def _(pe):
                def body(it):
                    it = it.back(1)
                    if it.on(EG):
                        pe.wait_ge(norm_s.s_done_a, it.n + 1)
                        msg.pe_transpose(pe, it)
                        msg.pe_products(pe, it)
                run_steps(pe, body, EG + 1, EG)
                pe.wait_ge(s_f6, EJ - 1)
                nc.tensor.matmul(bank[4][0:EP, 0:F], carry_lhs[:, :], edge_feat[:, (EJ - 1) * F:EJ * F], start=True,
                                 stop=True).then_inc(s_cy6, 1)

        ring_in.end_phase(EG)

        take = carve()
        ubuf, mbuf = take(EP, U, QT * F), take(EP, 3, QT * F)
        z7 = take(EP, 2, QT * F)
        xt7, mt7 = ([take(128, QT * EP) for _ in range(2)] for _ in range(2))
        junk7 = take(EP, QT * F // 2).bitcast(bf16).rearrange("p (k f) -> p k f", f=F)
        idx7 = sb("idx7", [EP, U, QT], i32)
        upd = Layer("upd", EP, QT, lambda it: tiles(ubuf, it), lambda it: tiles(z7, it), xt7, junk7, [[2, 3], [4, 5]],
                    (w_ut, w_ub, bias_u, bc["ug"], bc["ubeta"]), m_of=lambda it: tiles(mbuf, it), mt=mt7)
        ring_scatter = Ring("scattered", unit=16 * QT)
        s_icp7, s_tot7, s_m7 = (sem(n) for n in ("idx7_copied", "message_total", "message_mean"))
        with nc.Block() as block:
            @block.sync
            def _(sp):
                def body(step):
                    it = step.back(-1)
                    if it.on(EG):
                        after(sp, ring_scatter.of(it), ring_scatter.before(it))
                        sp.dma_start(tiles(ubuf, it), edge_rows(x1_dram, it.n * QT, QT)).then_inc(ring_in.of(it), 16)
                sp.dma_start(tiles(ubuf, Item(0, 0)), edge_rows(x1_dram, 0, QT)).then_inc(ring_in.of(Item(0, 0)), 16)
                run_steps(sp, body, EG, EG)

            @block.vector
            def _(dve):
                V = nc.vector

                def body(it):
                    if it.back(3).on(EG):
                        upd.dve_y(dve, it.back(3))
                        upd.dve_y_stats(dve, it.back(3))
                    if it.on(EG):
                        after(dve, upd.s["transposed"], it.n - 2)
                        for t in range(QT):
                            j = it.n * QT + t
                            ins = V.scalar_tensor_tensor(out=tiles(mbuf, it)[:, t, :], in0=carry[:, :],
                                                         scalar=first[:, bass.ds(j, 1)],
                                                         in1=edge_feat[:, bass.ds(j * F, F)], op0=ALU.mult, op1=ALU.add)
                        ins.then_inc(s_tot7, 1)
                    if it.back(3).on(EG):
                        upd.last.dve_shift(dve, it.back(3))
                    if it.back(2).on(EG):
                        upd.dve_z(dve, it.back(2))
                    if it.back(3).on(EG):
                        upd.last.dve_apply(dve, it.back(3), range(QT))
                run_steps(dve, body, EG + 3, EG)

            @block.scalar
            def _(act):
                act.preload_act_table_set("natural_log_exp_and_others")

                def body(it):
                    if it.back(1).on(EG):
                        upd.act_copy(act, it.back(1))
                    if it.back(3).on(EG):
                        upd.last.act_rstd(act, it.back(3))
                    if it.on(EG):
                        act.wait_ge(s_tot7, it.n + 1)
                        for t in range(QT):
                            m = tiles(mbuf, it)[:, t, :]
                            ins = nc.scalar.activation(m, m, ACT.Copy, scale=rcnt[:, bass.ds(it.n * QT + t, 1)])
                        ins.then_inc(s_m7, 1)
                    if it.back(1).on(EG):
                        upd.act_scales(act, it.back(1))
                    if it.back(2).on(EG):
                        upd.act_relu(act, it.back(2))
                run_steps(act, body, EG + 3, EG)

            @block.tensor
            def _(pe):
                def body(it):
                    it = it.back(1)
                    if it.on(EG):
                        pe.wait_ge(ring_in.of(it), ring_in.done(it))
                        pe.wait_ge(s_m7, it.n + 1)
                        upd.pe_transpose(pe, it)
                        upd.pe_products(pe, it)
                run_steps(pe, body, EG + 1, EG)

            @block.gpsimd
            def _(pool):
                def body(it):
                    if it.on(EG):
                        after(pool, ring_scatter.of(it), ring_scatter.before(it))
                        nc.gpsimd.tensor_copy(idx7[:, it.slot, :], out_idx[:, bass.ds(it.n * QT, QT)])\
                            .then_inc(s_icp7, 1)
                    if it.back(2).on(EG):
                        upd.shift(pool, it.back(2))
                    it = it.back(3)
                    if it.on(EG):
                        pool.wait_ge(s_icp7, it.n + 1)
                        pool.wait_ge(upd.last.s_done_v, it.n + 1)
                        pool.sem_inc(s_go, 1)
                        for k in range(QT):
                            nc.gpsimd.indirect_dma_start(
                                out=out, out_offset=bass.IndirectOffsetOnAxis(ap=idx7[:, it.slot, k:k + 1], axis=0),
                                in_=ubuf[:, it.slot, k * F:(k + 1) * F], in_offset=None, bounds_check=N - 1,
                                oob_is_err=False).then_inc(ring_scatter.of(it), 16)
                run_steps(pool, body, EG + 3, EG)
                ring_scatter.wait_all(pool, EG)


_INS = ['x', 'src', 'dst', 'edge_weight', 'L0_gnn_W', 'L0_gnn_attn_l', 'L0_gnn_attn_r', 'L0_gnn_bias', 'L0_gnn_gamma',
        'L0_gnn_beta', 'L1_gnn_msg_w', 'L1_gnn_msg_b', 'L1_gnn_msg_g', 'L1_gnn_msg_beta', 'L1_gnn_upd_w',
        'L1_gnn_upd_b', 'L1_gnn_upd_g', 'L1_gnn_upd_beta', 'L1_gnn_gate_w', 'L1_gnn_gate_b']


def kernel(**inputs):
    import numpy as np
    import concourse.bacc as bacc
    from concourse.bass_utils import run_bass_kernel_spmd

    nc = bacc.Bacc("TRN2", target_bir_lowering=False, num_devices=1)
    arrays, args = {}, []
    for name in _INS:
        a = np.ascontiguousarray(inputs[name])
        arrays["in_" + name] = a
        args.append(nc.dram_tensor("in_" + name, a.shape, mybir.dt.from_np(a.dtype), kind="ExternalInput").ap())
    shape = np.asarray(inputs['x']).shape
    args.append(nc.dram_tensor("out_rows", shape, mybir.dt.float32, kind="ExternalOutput").ap())
    gnn_resnorm_kernel(nc, *args)
    r = run_bass_kernel_spmd(nc, [arrays], core_ids=[0])
    return r.results[0]["out_rows"]
```

```python
import concourse.bass as bass
from concourse import mybir
from contextlib import ExitStack


def gnn_resnorm_kernel(nc, x, src, dst, edge_weight, gat_w, attn_l, attn_r, gat_bias, gat_gamma, gat_beta,
                       msg_w, msg_b, msg_g, msg_beta, upd_w, upd_b, upd_g, upd_beta, gate_w, gate_b, out):
    f32 = mybir.dt.float32
    i32 = mybir.dt.int32
    bf16 = mybir.dt.bfloat16
    ALU = mybir.AluOpType
    ACT = mybir.ActivationFunctionType
    X = mybir.AxisListType.X

    N, F = x.shape
    E = src.shape[0]
    HEADS, FO = attn_l.shape
    EP = 125
    EJ = E // EP
    assert E == EP * EJ and EJ % 8 == 0 and F == 128 and HEADS * FO == F
    NP = 128
    T = 8
    CHUNK = NP * T
    CHUNKS = -(-N // CHUNK)
    LAST_START = N - CHUNK
    QT = 4
    EG = EJ // QT
    EPS = 1e-5
    BIG = 1e30
    GATE_CAP = 1e8
    SKIP = 1 << 20
    U = 6
    OUT_SPLIT = 5

    xs_dram = nc.dram_tensor("xs_rows", (E, F), f32, kind="Internal").ap()
    xd_dram = nc.dram_tensor("xd_rows", (E, F), f32, kind="Internal").ap()
    g_dram = nc.dram_tensor("g_rows", (E + 1, F), f32, kind="Internal").ap()
    x1_dram = nc.dram_tensor("x1_rows", (E, F), f32, kind="Internal").ap()

    def edge_rows(table, j, k):
        return table[0:E, :].rearrange("(p j) f -> p j f", j=EJ)[:, bass.ds(j, k), :]

    def node_rows(table, start):
        return table[bass.ds(start, CHUNK), :].rearrange("(p k) f -> p k f", k=T)

    ctx = ExitStack()
    with ctx:
        def sb(name, shape, dt=f32):
            return ctx.enter_context(nc.sbuf_tensor(name, shape, dt))

        def pb(name, shape, dt=f32):
            return ctx.enter_context(nc.psum_tensor(name, shape, dt))

        def sem(name):
            return ctx.enter_context(nc.semaphore(name))

        edge_feat = sb("edge_feat", [EP, EJ * F])
        arena = sb("arena", [128, 12800])
        ident = sb("ident", [128, 128])
        ones = sb("ones", [128, 128])
        ones_bf = sb("ones_bf", [128, 128], bf16)
        eps_col = sb("eps_col", [128, 1])
        w_gat = sb("w_gat", [F, F + HEADS])
        w_ma, w_mb, w_ub = (sb(n, [F, F]) for n in ("w_ma", "w_mb", "w_ub"))
        w_ut = sb("w_ut", [F, F + 1])
        v_er = sb("v_er", [F, HEADS])
        bias_m, bias_u = sb("bias_m", [3, 4 * F], bf16), sb("bias_u", [3, 3 * (F + 1)], bf16)
        bc = {n: sb("bc_" + n, [128, F]) for n in ("al", "ar", "bias", "gamma", "beta", "mb", "mg", "mbeta",
                                                   "ub", "ug", "ubeta", "c")}
        gb_bc = sb("gb_bc", [128, 1])
        src_i, dst_i = sb("src_i", [EP, EJ], i32), sb("dst_i", [EP, EJ], i32)
        src_f, dst_f = sb("src_f", [EP, EJ]), sb("dst_f", [EP, EJ])
        w_edge = sb("w_edge", [EP, EJ])
        same = sb("same", [EP, EJ])
        first = sb("first", [EP, EJ])
        pen_f, pen_b = sb("pen_f", [EP, EJ]), sb("pen_b", [EP, EJ])
        same_n = sb("same_n", [EP, EJ])
        pen_first, pen_last = sb("pen_first", [EP, EJ]), sb("pen_last", [EP, EJ])
        in_last = sb("in_last", [EP, EJ])
        cross = sb("cross", [EP, 4, EP])
        cross_pen = sb("cross_pen", [EP, 4, EP])
        cross_sum = sb("cross_sum", [EP, 2, EP])
        carry_lhs = sb("carry_lhs", [EP, EP])
        nz = sb("nz", [EP, 1])
        alpha = sb("alpha", [EP, EJ * HEADS])
        rcnt = sb("rcnt", [EP, EJ])
        g_idx, x1_idx, out_idx = (sb(n, [EP, EJ], i32) for n in ("g_idx", "x1_idx", "out_idx"))
        carry = sb("carry", [EP, F])
        sc = [sb(f"sc{n}", [EP, EJ]) for n in range(6)]
        small = sb("small", [128, 16])

        bank = [pb(f"bank{n}", [128, 512]) for n in range(8)]

        class Chain:

            def __init__(self, eng, s, per_run, run):
                self.eng, self.s, self.per_run, self.base, self.k = eng, s, per_run, run * per_run, 0

            def __call__(self, ins):
                self.k += 1
                ins.then_inc(self.s, 1)
                self.eng.wait_ge(self.s, self.base + self.k)

            def end(self):
                assert self.k == self.per_run, (self.k, self.per_run)

        s_line = sem("vector_line")
        s_go = sem("rows_may_move")
        line = [0]

        def link(ins):
            line[0] += 1
            ins.then_inc(s_line, 1)
            nc.vector.wait_ge(s_line, line[0])

        def after(eng, s, count):
            if isinstance(count, int) and count <= 0:
                return
            eng.wait_ge(s, count)

        class Item:

            def __init__(self, block_, slot, n=None):
                self.block, self.slot = block_, slot
                self.n = block_ * U + slot if n is None else n
                self.known = isinstance(block_, int)

            def back(self, k):
                return Item(self.block + (self.slot - k) // U, (self.slot - k) % U, self.n - k)

            def ring(self, places):
                return self.slot % places

            def uses(self, places):
                return self.block * (U // places) + self.slot // places

            def on(self, count):
                return not self.known or 0 <= self.n < count

        class Ring:

            def __init__(self, name, unit=16):
                self.sems, self.base, self.unit = [sem(f"{name}{n}") for n in range(U)], [0] * U, unit

            def of(self, it):
                return self.sems[it.slot]

            def before(self, it):
                return self.base[it.slot] + self.unit * it.uses(U)

            def done(self, it):
                return self.base[it.slot] + self.unit * (it.uses(U) + 1)

            def wait_all(self, eng, items):
                for n in range(U):
                    eng.wait_ge(self.sems[n], self.base[n] + self.unit * len(range(n, items, U)))

            def end_phase(self, items):
                for n in range(U):
                    self.base[n] += self.unit * len(range(n, items, U))

        ring_in, ring_out = Ring("loaded"), Ring("stored")

        def run_steps(eng, body, steps, items):
            blocks = (items - 2) // U
            for i in range(U):
                body(Item(0, i))
            with eng.Fori(1, blocks) as b:
                for u in range(U):
                    body(Item(b, u))
            for i in range(blocks * U, steps):
                body(Item(i // U, i % U))

        def bcast(row, parts, k):
            return row[0:parts, :].rearrange("p (a f) -> p a f", a=1).to_broadcast([parts, k, F])

        SRC_PARTS = 5
        SRC_PART = E // SRC_PARTS
        assert EP % SRC_PARTS == 0
        s_srcs = [sem(f"sources_loaded{n}") for n in range(SRC_PARTS)]
        s_wc, s_ws = (sem(n) for n in ("w_ut_ready", "w_ut_sums"))
        s_ld, s_nx, s_pool0, s_p0, s_st, s_row0 = (sem(n) for n in (
            "setup_loaded", "next_cleared", "ident_ready", "setup_rows", "c_row_stored", "rows_read"))
        src_all = edge_feat[:, 0:E].bitcast(i32)
        dprev = sc[0][:, :].bitcast(i32)
        dnext = small[:, 8:9].bitcast(i32)
        n_loads = [0]
        with nc.Block() as block:
            @block.sync
            def _(sp):
                def load(dst_ap, src_ap):
                    n_loads[0] += 1
                    sp.dma_start(dst_ap, src_ap, allow_slow_non_contiguous=True).then_inc(s_ld, 16)

                load(dst_i[:, :], dst.rearrange("(p j) -> p j", j=EJ))
                load(src_i[:, :], src.rearrange("(p j) -> p j", j=EJ))
                for w, d in ((gat_w, w_gat), (msg_w[0:F, :], w_ma), (msg_w[F:2 * F, :], w_mb),
                             (upd_w[0:F, :], w_ut), (upd_w[F:2 * F, :], w_ub)):
                    load(d[:, 0:F], w)
                rows = (("al", attn_l.rearrange("h f -> (h f)")), ("ar", attn_r.rearrange("h f -> (h f)")),
                        ("bias", gat_bias), ("gamma", gat_gamma), ("beta", gat_beta), ("mb", msg_b), ("mg", msg_g),
                        ("mbeta", msg_beta), ("ub", upd_b), ("ug", upd_g), ("ubeta", upd_beta))
                for name, v in rows:
                    load(bc[name][:, :], v.partition_broadcast(128))
                load(w_ut[:, F:F + 1], gate_w)
                load(gb_bc[:, :], gate_b.partition_broadcast(128))
                load(w_edge[:, :], edge_weight.rearrange("(p j) -> p j", j=EJ))
                load(dprev[1:EP, :], dst[0:E - EJ].rearrange("(p j) -> p j", j=EJ))
                sp.wait_ge(s_nx, 1)
                load(dnext[0:EP - 1, :], dst[EJ:E].rearrange("(p j) -> p j", j=EJ)[:, 0:1])
                for q, s_part in enumerate(s_srcs):
                    sp.dma_start(src_all[:, q * SRC_PART:(q + 1) * SRC_PART],
                                 src[q * SRC_PART:(q + 1) * SRC_PART].partition_broadcast(EP)).then_inc(s_part, 16)
            LOADED = 16 * n_loads[0]

            @block.gpsimd
            def _(pool):
                nc.gpsimd.memset(ident[:, :], 0.0).then_inc(s_pool0, 1)
                pool.wait_ge(s_pool0, 1)
                nc.gpsimd.affine_select(out=ident[:, :], in_=ident[:, :], compare_op=ALU.not_equal, fill=1.0,
                                        base=0, pattern=[[-1, 128]], channel_multiplier=1).then_inc(s_pool0, 1)
                nc.gpsimd.iota(sc[1][:, :].bitcast(i32), pattern=[[1, EJ]], base=0,
                               channel_multiplier=EJ).then_inc(s_pool0, 1)
                pool.wait_ge(s_p0, 3)
                nc.gpsimd.affine_select(out=carry_lhs[:, :], in_=carry_lhs[:, :], compare_op=ALU.is_gt, fill=0.0,
                                        base=0, pattern=[[1, EP]], channel_multiplier=-1).then_inc(s_pool0, 1)

            @block.tensor
            def _(pe):
                pe.wait_ge(s_p0, 1)
                nc.tensor.matmul(bank[0][0:EP, 0:EP], ones[0:EP, 0:EP], arena[0:EP, 0:EP], start=True,
                                 stop=True).then_inc(s_row0, 1)
                pe.wait_ge(s_p0, 2)
                nc.tensor.matmul(bank[1][0:EP, 0:EP], ones[0:EP, 0:EP], arena[0:EP, 128:128 + EP], start=True,
                                 stop=True).then_inc(s_row0, 1)
                pe.wait_ge(s_wc, 1)
                nc.tensor.matmul(bank[2][:, 0:F + 1], ones[:, :], w_ut[:, :], start=True, stop=True).then_inc(s_ws, 1)

            @block.scalar
            def _(act):
                act.preload_act_table_set("natural_log_exp_and_others")
                act.wait_ge(s_p0, 4)
                nc.scalar.activation(small[:, 4:5], small[:, 3:4], ACT.Ln, bias=eps_col[:, :],
                                     scale=1.0 / F).then_inc(s_st, 1)
                act.wait_ge(s_st, 1)
                nc.scalar.activation(small[:, 5:6], small[:, 4:5], ACT.Exp, scale=-0.5).then_inc(s_st, 1)

            @block.vector
            def _(dve):
                V = nc.vector
                V.memset(ones[:, :], 1.0)
                V.memset(ones_bf[:, :], 1.0)
                V.memset(eps_col[:, :], EPS)
                link(V.memset(dprev[0:1, :], 0))
                V.memset(small[:, 8:9], -1.0).then_inc(s_nx, 1)
                dve.wait_ge(s_ld, LOADED)
                dve.wait_ge(s_pool0, 3)
                link(V.tensor_copy(src_f[:, :], src_i[:, :]))
                link(V.tensor_copy(dst_f[:, :], dst_i[:, :]))
                link(V.tensor_copy(sc[1][:, :], sc[1][:, :].bitcast(i32)))
                fd, ld = dst_f[:, 0:1], dst_f[:, EJ - 1:EJ]
                V.tensor_scalar(arena[0:EP, 0:EP], ident[0:EP, 0:EP], fd, None, ALU.mult).then_inc(s_p0, 1)
                V.tensor_scalar(arena[0:EP, 128:128 + EP], ident[0:EP, 0:EP], ld, None, ALU.mult).then_inc(s_p0, 1)
                for row, v in (("al", w_gat[:, F:F + HEADS]), ("ar", v_er[:, :])):
                    tmp = arena[:, 256:256 + F]
                    link(V.tensor_tensor(tmp, w_gat[:, 0:F], bc[row][:, :], ALU.mult))
                    link(V.tensor_reduce(v, tmp.rearrange("p (h f) -> p h f", h=HEADS), X, ALU.add))
                for w in (w_ut, w_ma, w_mb, w_ub):
                    link(V.tensor_reduce(small[:, 0:1], w[:, 0:F], X, ALU.add))
                    link(V.tensor_scalar(small[:, 1:2], small[:, 0:1], 1.0 / F, None, ALU.mult))
                    ins = V.tensor_scalar(w[:, 0:F], w[:, 0:F], small[:, 1:2], None, ALU.subtract)
                    if w is w_ut:
                        ins.then_inc(s_wc, 1)
                        dve.wait_ge(s_wc, 1)
                    else:
                        link(ins)
                dve.wait_ge(s_ws, 1)
                link(V.scalar_tensor_tensor(out=w_ut[:, :], in0=bank[2][:, 0:F + 1], scalar=-1.0 / F, in1=w_ut[:, :],
                                            op0=ALU.mult, op1=ALU.add))
                for row, width, parts_of in (("mb", F, bias_m), ("ub", F + 1, bias_u)):
                    full, rest = (arena[:, 512 + 256 * n:512 + 256 * n + width] for n in range(2))
                    link(V.tensor_reduce(small[:, 0:1], bc[row][:, :], X, ALU.add))
                    link(V.tensor_scalar(small[:, 1:2], small[:, 0:1], 1.0 / F, None, ALU.mult))
                    if width > F:
                        V.tensor_copy(full[:, F:F + 1], gb_bc[:, :])
                    link(V.tensor_scalar(full[:, 0:F], bc[row][:, :], small[:, 1:2], None, ALU.subtract))
                    half_row = arena[:, 1280:1280 + F].bitcast(bf16)[:, 0:width]
                    for n in range(3):
                        link(V.tensor_copy(half_row, full))
                        if n:
                            link(V.scalar_tensor_tensor(out=rest[0:3, :], in0=half_row[0:3, :],
                                                        scalar=ident[0:3, n:n + 1], in1=rest[0:3, :], op0=ALU.mult,
                                                        op1=ALU.add))
                        else:
                            link(V.tensor_scalar(rest[0:3, :], half_row[0:3, :], ident[0:3, 0:1], None, ALU.mult))
                        link(V.tensor_tensor(full, full, half_row, ALU.subtract))
                    for n in range(parts_of.shape[1] // width):
                        V.tensor_copy(parts_of[:, n * width:(n + 1) * width], rest[0:3, :])
                link(V.bn_stats(small[:, 9:15], bc["bias"][:, :]))
                st = small[:, 9:15]
                V.tensor_tensor(small[:, 0:1], st[:, 1:2], st[:, 4:5], ALU.add)
                V.tensor_tensor(small[:, 1:2], st[:, 1:2], st[:, 4:5], ALU.subtract)
                link(V.tensor_tensor(small[:, 2:3], st[:, 2:3], st[:, 5:6], ALU.add))
                link(V.tensor_tensor(small[:, 1:2], small[:, 1:2], small[:, 1:2], ALU.mult))
                dve.wait_ge(s_row0, 2)
                for n, (rows_, key) in enumerate(((0, fd), (1, fd), (0, ld), (1, ld))):
                    link(V.tensor_scalar(cross[:, n, :], bank[rows_][0:EP, 0:EP], key, None, ALU.is_equal))
                V.tensor_copy(carry_lhs[:, :], cross[:, 2, :]).then_inc(s_p0, 1)
                V.scalar_tensor_tensor(out=small[:, 3:4], in0=small[:, 1:2], scalar=float(F // 4),
                                       in1=small[:, 2:3], op0=ALU.mult, op1=ALU.add).then_inc(s_p0, 1)
                link(V.tensor_tensor(nz[:, :], fd, ld, ALU.not_equal))
                link(V.tensor_scalar(cross_pen[:, :, :], cross[:, :, :], -1.0, BIG, ALU.add, ALU.mult))
                link(V.tensor_scalar(cross_sum[:, 0, :], cross[:, 2, :], nz[:, :], None, ALU.mult))
                link(V.tensor_scalar(cross_sum[:, 1, :], cross[:, 3, :], nz[:, :], None, ALU.mult))
                link(V.memset(same[:, :], 0.0))
                link(V.memset(same_n[:, :], 0.0))
                link(V.tensor_tensor(same[:, 1:EJ], dst_f[:, 1:EJ], dst_f[:, 0:EJ - 1], ALU.is_equal))
                link(V.tensor_copy(same_n[:, 0:EJ - 1], same[:, 1:EJ]))
                link(V.tensor_scalar(first[:, :], dst_f[:, :], fd, None, ALU.is_equal))
                link(V.tensor_scalar(in_last[:, :], dst_f[:, :], ld, None, ALU.is_equal))
                for a, b in ((same, pen_f), (same_n, pen_b), (first, pen_first), (in_last, pen_last)):
                    link(V.tensor_scalar(b[:, :], a[:, :], -1.0, BIG, ALU.add, ALU.mult))
                last = sc[2]
                link(V.tensor_scalar(last[:, :], same_n[:, :], -1.0, 1.0, ALU.mult, ALU.add))
                link(V.tensor_copy(small[0:EP, 6:7], dnext[0:EP, :]))
                link(V.tensor_tensor(last[:, EJ - 1:EJ], small[0:EP, 6:7], ld, ALU.not_equal))
                link(V.scalar_tensor_tensor(out=sc[3][:, :], in0=dst_f[:, :], scalar=float(-SKIP), in1=last[:, :],
                                            op0=ALU.add, op1=ALU.mult))
                link(V.tensor_scalar(out_idx[:, :], sc[3][:, :], float(SKIP), None, ALU.add))
                dve.wait_ge(s_st, 2)
                link(V.scalar_tensor_tensor(out=small[:, 2:3], in0=small[:, 0:1], scalar=-0.5, in1=small[:, 5:6],
                                            op0=ALU.mult, op1=ALU.mult))
                link(V.tensor_scalar(bc["c"][:, :], bc["bias"][:, :], small[:, 5:6], small[:, 2:3], ALU.mult, ALU.add))
                link(V.tensor_tensor(bc["c"][:, :], bc["c"][:, :], bc["gamma"][:, :], ALU.mult))
                link(V.tensor_tensor(bc["c"][:, :], bc["c"][:, :], bc["beta"][:, :], ALU.add))

        above = arena[:, :].bitcast(bf16)[0:EP, 0:E].rearrange("k (j p) -> k j p", p=EP)
        step_hi, step_lo = (sb(n, [EP, EJ], bf16) for n in ("step_hi", "step_lo"))
        s_sp, s_sr, s_sc, s_ss, s_sb, s_cst = (sem(n) for n in (
            "search_ready", "row_fetched", "row_counted", "row_signed", "search_done",
            "c_stored"))
        junk_d, junk_a = (sb(n, [EP, 4, EJ], bf16) for n in ("junk_d", "junk_a"))
        qm = sc[4]
        cle, sgn = sc[2], sc[3]
        with nc.Block() as block:
            @block.vector
            def _(dve):
                V = nc.vector
                link(V.tensor_copy(sc[5][:, :], dprev[:, :]))
                link(V.tensor_tensor(sc[2][:, :], dst_f[:, :], sc[5][:, :], ALU.subtract))
                link(V.tensor_scalar(sc[3][:, :], sc[2][:, :], 1.0 / 512, float(3 << 22), ALU.mult, ALU.add))
                link(V.tensor_scalar(sc[3][:, :], sc[3][:, :], float(-(3 << 22)), 512.0, ALU.add, ALU.mult))
                link(V.tensor_copy(step_hi[:, :], sc[3][:, :]))
                link(V.tensor_tensor(step_lo[:, :], sc[2][:, :], sc[3][:, :], ALU.subtract))
                link(V.tensor_scalar(qm[:, :], src_f[:, :], -0.5, None, ALU.add))
                pw = EP // SRC_PARTS
                for q, s_part in enumerate(s_srcs):
                    dve.wait_ge(s_part, 16)
                    view = src_all[:, q * SRC_PART:(q + 1) * SRC_PART].rearrange("k (p j) -> k j p", j=EJ)
                    V.tensor_scalar(above[:, :, q * pw:(q + 1) * pw], view, dst_f[:, 0:1], None, ALU.is_ge)\
                        .then_inc(s_sp, 1)

                def count(b, u):
                    i = b * 4 + u
                    dve.wait_ge(s_sr, i + 1)
                    V.tensor_scalar(junk_d[:, u, :], bank[u][0:EP, 0:EJ], src_f[:, bass.ds(i, 1)],
                                    None, ALU.is_le, ALU.add, accum_out=cle[:, bass.ds(i, 1)]).then_inc(s_sc, 1)
                with dve.Fori(0, EJ // 4) as b:
                    for u in range(4):
                        count(b, u)
                dve.wait_ge(s_sc, EJ)
                dve.wait_ge(s_ss, EJ)
                dve.wait_ge(s_sb, EJ)
                part_no = sc[5]
                V.tensor_copy(part_no[:, :], bank[4][0:EP, 0:EJ])
                link(V.tensor_scalar(cle[:, :], cle[:, :], 1.0, None, ALU.mult))
                link(V.scalar_tensor_tensor(out=qm[:, :], in0=cle[:, :], scalar=2.0, in1=sgn[:, :], op0=ALU.mult,
                                            op1=ALU.subtract))
                link(V.tensor_scalar(qm[:, :], qm[:, :], float(EJ) + 0.5, None, ALU.is_gt))
                link(V.scalar_tensor_tensor(out=qm[:, :], in0=part_no[:, :], scalar=0.5, in1=qm[:, :], op0=ALU.is_gt,
                                            op1=ALU.mult))
                link(V.scalar_tensor_tensor(out=cle[:, :], in0=part_no[:, :], scalar=float(EJ), in1=cle[:, :],
                                            op0=ALU.mult, op1=ALU.add))
                link(V.scalar_tensor_tensor(out=cle[:, :], in0=cle[:, :], scalar=float(-EJ - 1 - E), in1=qm[:, :],
                                            op0=ALU.add, op1=ALU.mult))
                link(V.tensor_scalar(g_idx[:, :], cle[:, :], float(E), None, ALU.add))

            @block.scalar
            def _(act):
                act.preload_act_table_set("natural_log_exp_and_others")
                def signs(b, u):
                    i = b * 4 + u
                    act.wait_ge(s_sc, i + 1)
                    nc.scalar.activation(junk_a[:, u, :], bank[u][0:EP, 0:EJ], ACT.Sign, bias=qm[:, bass.ds(i, 1)],
                                         scale=-1.0, accum_out=sgn[:, bass.ds(i, 1)]).then_inc(s_ss, 1)
                act.wait_ge(s_sp, SRC_PARTS)
                with act.Fori(0, EJ // 4) as b:
                    for u in range(4):
                        signs(b, u)

            @block.tensor
            def _(pe):
                pe.wait_ge(s_sp, SRC_PARTS)

                def fetch(b, u, head):
                    i = b * 4 + u
                    if not head:
                        pe.wait_ge(s_ss, i - 3)
                    nc.tensor.matmul(bank[u][0:EP, 0:EJ], above[:, bass.ds(i, 1), :].rearrange("k a p -> k (a p)"),
                                     step_hi[:, :], start=True, stop=False)
                    nc.tensor.matmul(bank[u][0:EP, 0:EJ], above[:, bass.ds(i, 1), :].rearrange("k a p -> k (a p)"),
                                     step_lo[:, :], start=False, stop=True).then_inc(s_sr, 1)
                    nc.tensor.matmul(bank[4][0:EP, bass.ds(i, 1)],
                                     above[:, bass.ds(i, 1), :].rearrange("k a p -> k (a p)"),
                                     ones_bf[0:EP, 0:1], start=True, stop=True).then_inc(s_sb, 1)
                for u in range(4):
                    fetch(0, u, True)
                with pe.Fori(1, EJ // 4) as b:
                    for u in range(4):
                        fetch(b, u, False)

            @block.sync
            def _(sp):
                sp.dma_start(g_dram[E:E + 1, :], bc["c"][0:1, :]).then_inc(s_cst, 16)
                sp.wait_ge(s_cst, 16)

        class Norm:
            def __init__(self, tag, parts, sets, factor=False, centre=True):
                self.centre = centre
                self.parts, self.sets, self.at, k = parts, sets, [], 0
                for _, tiles_, _, _ in sets:
                    self.at.append(k)
                    k += tiles_
                self.st, self.sm, self.ln = sb(f"{tag}_st", [128, k, 6]), sb(f"{tag}_sm", [128, 4, k]), \
                    sb(f"{tag}_ln", [128, k])
                self.r, self.nb = sb(f"{tag}_r", [128, 2, k]), sb(f"{tag}_nb", [128, 2, k])
                self.factors = sb(f"{tag}_factors", [128, 2, k]) if factor else None
                self.first_step = min(lag for _, _, lag, _ in sets)
                self.s_stats, self.s_rstd, self.s_shift, self.s_links, self.s_alinks = (
                    sem(f"{tag}_{n}") for n in ("stats", "rstd", "shift", "vchain", "achain"))
                self.s_done_v, self.s_done_a = ([sem(f"{tag}_normed_{e}{n}") for n in range(len(sets))] for e in "va")

            def active(self, step):
                return [n for n, (_, _, lag, items) in enumerate(self.sets) if step.back(lag).on(items)]

            def on(self, step):
                return bool(self.active(step))

            def cut(self, step):
                a = self.active(step)
                return slice(self.at[a[0]], self.at[a[-1]] + self.sets[a[-1]][1])

            def count(self, step):
                return step.n - self.first_step + 1

            def dve_stats(self, dve, step):
                V, p, c = nc.vector, self.parts, self.cut(step)
                chain = Chain(dve, self.s_links, 3, self.count(step) - 1)
                for n in self.active(step):
                    x_of, k, lag, _ = self.sets[n]
                    for t in range(k):
                        ins = V.bn_stats(self.st[0:p, self.at[n] + t, :], x_of(step.back(lag))[:, t, :])
                chain(ins)
                after(dve, self.s_rstd, self.count(step) - 1)
                s, d, v, v128 = (self.sm[0:p, q, c] for q in range(4))
                st = self.st[0:p, c, :]
                if self.centre:
                    V.tensor_tensor(s, st[:, :, 1], st[:, :, 4], ALU.add)
                V.tensor_tensor(d, st[:, :, 1], st[:, :, 4], ALU.subtract)
                if self.factors is not None:
                    f = self.factors[0:p, step.back(self.sets[-1][2]).ring(2), c]
                    chain(V.scalar_tensor_tensor(out=v, in0=f, scalar=F * EPS, in1=st[:, :, 2], op0=ALU.mult,
                                                 op1=ALU.add))
                    V.tensor_tensor(v, v, st[:, :, 5], ALU.add)
                else:
                    chain(V.tensor_tensor(v, st[:, :, 2], st[:, :, 5], ALU.add))
                chain(V.tensor_tensor(d, d, d, ALU.mult))
                V.scalar_tensor_tensor(out=v128, in0=d, scalar=float(F // 4), in1=v, op0=ALU.mult, op1=ALU.add)\
                    .then_inc(self.s_stats, 1)
                chain.end()

            def act_rstd(self, act, step):
                p, c = self.parts, self.cut(step)
                chain = Chain(act, self.s_alinks, 1, self.count(step) - 1)
                act.wait_ge(self.s_stats, self.count(step))
                if self.factors is not None:
                    chain(nc.scalar.activation(self.ln[0:p, c], self.sm[0:p, 3, c], ACT.Ln, scale=1.0 / F))
                else:
                    chain(nc.scalar.activation(self.ln[0:p, c], self.sm[0:p, 3, c], ACT.Ln, bias=eps_col[0:p, :],
                                               scale=1.0 / F))
                nc.scalar.activation(self.r[0:p, step.ring(2), c], self.ln[0:p, c], ACT.Exp, scale=-0.5)\
                    .then_inc(self.s_rstd, 1)
                chain.end()

            def act_scale(self, act, step, n, tiles_):
                x_of, _, lag, items = self.sets[n]
                act.wait_ge(self.s_rstd, self.count(step))
                xb, p, par = x_of(step.back(lag)), self.parts, step.ring(2)
                for t in tiles_:
                    at = self.at[n] + t
                    ins = nc.scalar.activation(xb[:, t, :], xb[:, t, :], ACT.Copy, scale=self.r[0:p, par, at:at + 1])
                ins.then_inc(self.s_done_a[n], 1)

            def dve_shift(self, dve, step):
                p, c = self.parts, self.cut(step)
                dve.wait_ge(self.s_rstd, self.count(step))
                nc.vector.scalar_tensor_tensor(out=self.nb[0:p, step.ring(2), c], in0=self.sm[0:p, 0, c], scalar=-0.5,
                                               in1=self.r[0:p, step.ring(2), c], op0=ALU.mult, op1=ALU.mult)\
                    .then_inc(self.s_shift, 1)

            def dve_apply(self, dve, step, n, tiles_):
                x_of, _, lag, items = self.sets[n]
                if not step.back(lag).on(items):
                    return
                dve.wait_ge(self.s_shift, self.count(step))
                xb, p, par = x_of(step.back(lag)), self.parts, step.ring(2)
                for t in tiles_:
                    at = self.at[n] + t
                    ins = nc.vector.tensor_scalar(xb[:, t, :], xb[:, t, :], self.r[0:p, par, at:at + 1],
                                                  self.nb[0:p, par, at:at + 1], ALU.mult, ALU.add)
                ins.then_inc(self.s_done_v[n], 1)

            def act_apply(self, act, step, n, tiles_):
                x_of, _, lag, items = self.sets[n]
                if not step.back(lag).on(items):
                    return
                act.wait_ge(self.s_shift, self.count(step))
                xb, p, par = x_of(step.back(lag)), self.parts, step.ring(2)
                for t in tiles_:
                    at = self.at[n] + t
                    ins = nc.scalar.activation(xb[:, t, :], xb[:, t, :], ACT.Identity,
                                               scale=self.r[0:p, par, at:at + 1], bias=self.nb[0:p, par, at:at + 1])
                ins.then_inc(self.s_done_a[n], 1)

        class Layer:
            def __init__(self, tag, parts, k, x_of, z_of, xt, junk, banks, weights, m_of=None, mt=None, g2_of=None):
                self.wx, self.wm, self.bias3, self.gain, self.beta = weights
                self.gated = gated = g2_of is not None
                self.width, self.g2_of = F + 1 if gated else F, g2_of
                self.parts, self.k, self.groups, self.quad = parts, k, k // QT, QT * parts
                self.x_of, self.z_of, self.xt, self.junk, self.m_of, self.mt = x_of, z_of, xt, junk, m_of, mt
                self.banks, self.nb = banks, len(banks[0])
                self.per_bank = -(-k // self.nb)
                names = ["x_ready", "transposed", "copied", "products", "squared", "scales", "scaled", "shifted",
                         "chain_scales"] + (["relued", "chain_z", "y_done"] if gated else [])
                self.s = {n: sem(f"{tag}_{n}") for n in names}
                self.scal = sb(f"{tag}_scal", [128, 6, 2, k])

            SQ, LNH, RS, EX, KX, G = range(6)

            def q(self, n, it):
                return self.scal[0:self.parts, n, it.ring(2), :]

            def cuts(self):
                return [range(b * self.per_bank, min(self.k, (b + 1) * self.per_bank)) for b in range(self.nb)]

            def h(self, it, t, width=None):
                bank_no = self.banks[it.ring(len(self.banks))][t // self.per_bank]
                at = (t % self.per_bank) * self.width
                return bank[bank_no][0:self.parts, at:at + (width or F)]

            def gate_cols(self, it, b):
                n = len(self.cuts()[b])
                full = bank[self.banks[it.ring(len(self.banks))][b]][0:self.parts, 0:n * self.width]
                return full.rearrange("p (k w) -> p k w", w=self.width)[:, :, F]

            def pe_transpose(self, pe, it):
                s, p = self.s, self.parts
                for g in range(self.groups):
                    after(pe, s["copied"], self.groups * (it.n - 1) + g + 1)
                    for t in range(QT):
                        ins = nc.tensor.transpose(bank[g][:, t * p:(t + 1) * p], self.x_of(it)[:, g * QT + t, :],
                                                  ident[0:p, 0:p])
                    if self.m_of:
                        for t in range(QT):
                            ins = nc.tensor.transpose(bank[1][:, t * p:(t + 1) * p], self.m_of(it)[:, t, :],
                                                      ident[0:p, 0:p])
                    ins.then_inc(s["transposed"], 1)

            def act_copy(self, act, it):
                s, par = self.s, it.ring(2)
                after(act, s["products"], self.nb * (it.n - 1))
                for g in range(self.groups):
                    act.wait_ge(s["transposed"], self.groups * it.n + g + 1)
                    ins = nc.scalar.activation(self.xt[par][:, g * self.quad:(g + 1) * self.quad],
                                               bank[g][:, 0:self.quad], ACT.Copy)
                    if self.m_of:
                        ins = nc.scalar.activation(self.mt[par][:, :], bank[1][:, 0:self.quad], ACT.Copy)
                    ins.then_inc(s["copied"], 1)

            def pe_products(self, pe, it):
                s, p, par = self.s, self.parts, it.ring(2)
                for b, tiles_ in enumerate(self.cuts()):
                    pe.wait_ge(s["copied"], self.groups * it.n + tiles_[-1] // QT + 1)
                    after(pe, s["scaled"], self.nb * (it.n - len(self.banks)) + b + 1)
                    whole = bank[self.banks[it.ring(len(self.banks))][b]][0:p, 0:len(tiles_) * self.width]
                    nc.tensor.matmul(whole, ones_bf[0:3, 0:p], self.bias3[0:3, 0:len(tiles_) * self.width],
                                     start=True, stop=False)
                    for t in tiles_:
                        last = t == tiles_[-1]
                        ins = nc.tensor.matmul(self.h(it, t, self.width), self.xt[par][:, t * p:(t + 1) * p],
                                               self.wx[:, 0:self.width], start=False, stop=last and not self.m_of)
                        if self.m_of:
                            ins = nc.tensor.matmul(self.h(it, t), self.mt[par][:, t * p:(t + 1) * p], self.wm[:, :],
                                                   start=False, stop=last)
                    ins.then_inc(s["products"], 1)

            def act_scales(self, act, it):
                s, p = self.s, self.parts
                chain = Chain(act, s["chain_scales"], 2, it.n)
                for b, tiles_ in enumerate(self.cuts()):
                    act.wait_ge(s["products"], self.nb * it.n + b + 1)
                    if self.gated:
                        nc.scalar.activation(self.q(self.EX, it)[:, tiles_[0]:tiles_[-1] + 1], self.gate_cols(it, b),
                                             ACT.Exp, scale=-1.0)
                    for t in tiles_:
                        ins = nc.scalar.activation(self.junk[0:p, t, :], self.h(it, t), ACT.Square,
                                                   accum_out=self.q(self.SQ, it)[:, t:t + 1])
                chain(ins)
                chain(nc.scalar.activation(self.q(self.LNH, it), self.q(self.SQ, it), ACT.Ln, bias=eps_col[0:p, :],
                                           scale=1.0 / F))
                nc.scalar.activation(self.q(self.RS, it), self.q(self.LNH, it), ACT.Exp, scale=-0.5)\
                    .then_inc(s["scales"], 1)
                chain.end()

            def dve_z(self, dve, it):
                s, V = self.s, nc.vector
                dve.wait_ge(s["scales"], it.n + 1)
                if self.gated:
                    chain = Chain(dve, s["chain_z"], 1, it.n)
                    g, kx = self.q(self.G, it), self.q(self.KX, it)
                    chain(V.tensor_scalar(g, self.q(self.EX, it), GATE_CAP, 1.0, ALU.min, ALU.add))
                    V.tensor_tensor(self.g2_of(it), g, g, ALU.mult)
                    V.tensor_scalar(kx, g, 2.0, -1.0, ALU.mult, ALU.add)
                    chain.end()
                for tiles_ in self.cuts():
                    for t in tiles_:
                        ins = V.scalar_tensor_tensor(out=self.z_of(it)[:, t, :], in0=self.h(it, t),
                                                     scalar=self.q(self.RS, it)[:, t:t + 1],
                                                     in1=self.gain[0:self.parts, :], op0=ALU.mult, op1=ALU.mult)
                    ins.then_inc(s["scaled"], 1)

            def shift(self, eng, it):
                eng.wait_ge(self.s["scaled"], self.nb * (it.n + 1))
                eng.tensor_tensor(self.z_of(it), self.z_of(it), bcast(self.beta, self.parts, self.k), ALU.add)\
                    .then_inc(self.s["shifted"], 1)

            def act_relu(self, act, it):
                act.wait_ge(self.s["shifted"], it.n + 1)
                nc.scalar.activation(self.z_of(it), self.z_of(it), ACT.Relu).then_inc(self.s["relued"], 1)

            def dve_y(self, dve, it):
                s = self.s
                dve.wait_ge(s["relued"], it.n + 1)
                xb = self.x_of(it)
                for t in range(self.k):
                    ins = nc.vector.scalar_tensor_tensor(out=xb[:, t, :], in0=xb[:, t, :],
                                                         scalar=self.q(self.KX, it)[:, t:t + 1],
                                                         in1=self.z_of(it)[:, t, :], op0=ALU.mult, op1=ALU.add)
                ins.then_inc(s["y_done"], 1)
                dve.wait_ge(s["y_done"], it.n + 1)

        def carve():
            at = [0]

            def take(parts, *shape):
                size = 1
                for n in shape:
                    size *= n
                v = arena[0:parts, at[0]:at[0] + size]
                at[0] += size
                assert at[0] <= 12800
                return v if len(shape) == 1 else v.rearrange("p (a b) -> p a b", a=shape[0]) if len(shape) == 2 \
                    else v.rearrange("p (a b c) -> p a b c", a=shape[0], b=shape[1])
            return take

        def tiles(buf, it):
            return buf[:, it.ring(buf.shape[1]), :].rearrange("p (k f) -> p k f", f=F)

        take = carve()
        xbuf = take(128, U, T * F)
        z_dense = take(128, 2, T * F)
        xt_dense = [take(128, T * 128) for _ in range(2)]
        junk2 = take(128, T * F // 2).bitcast(bf16).rearrange("p (k f) -> p k f", f=F)
        rows2 = take(EP, 2, 4 * F)
        rows2t = take(128, 4 * EP)
        idx2 = sb("idx2", [EP, 2, 4], i32)
        scores = alpha

        norm1 = Norm("norm1", NP, [(lambda it: tiles(xbuf, it), T, 0, CHUNKS)], centre=False)
        norm2 = Norm("norm2", NP, [(lambda it: tiles(xbuf, it), T, 0, CHUNKS)], factor=True)
        dense = Layer("dense", NP, T, lambda it: tiles(xbuf, it), lambda it: tiles(z_dense, it), xt_dense, junk2,
                      [[2, 3, 4]], (w_ut, None, bias_u, bc["ug"], bc["ubeta"]),
                      g2_of=lambda it: norm2.factors[:, it.ring(2), :])
        s_rows = [sem(f"rows_in{n}") for n in range(2)]
        s_spill = [sem(f"rows_out{n}") for n in range(2)]
        s_cadd, s_icp, s_rt, s_rc, s_sf, s_fc = (sem(n) for n in (
            "c_added", "idx_copied", "rows_transposed", "rows_copied", "scored", "feat_copied"))
        PAIRS = EJ // 2
        STEPS2 = max(PAIRS + 1, CHUNKS + 4)

        def start_of(it):
            return LAST_START if it.known and it.n == CHUNKS - 1 else it.n * CHUNK

        with nc.Block() as block:
            @block.sync
            def _(sp):
                def body(step):
                    chunk = step.back(-1)
                    if chunk.on(CHUNKS):
                        after(sp, ring_out.of(chunk), ring_out.before(chunk))
                        sp.dma_start(tiles(xbuf, chunk), node_rows(x, start_of(chunk))).then_inc(ring_in.of(chunk), 16)
                    pair = step.back(1)
                    if pair.on(PAIRS):
                        p2 = pair.ring(2)
                        sp.wait_ge(s_rows[p2], 64 * (pair.uses(2) + 1))
                        sp.dma_start(edge_rows(xs_dram, pair.n * 2, 2), tiles(rows2, pair)[:, 0:2, :])\
                            .then_inc(s_spill[p2], 16)
                        sp.dma_start(edge_rows(xd_dram, pair.n * 2, 2), tiles(rows2, pair)[:, 2:4, :])\
                            .then_inc(s_spill[p2], 16)
                    chunk = step.back(4)
                    if chunk.on(CHUNKS):
                        sp.wait_ge(norm2.s_done_v[0], chunk.n + 1)
                        sp.wait_ge(norm2.s_done_a[0], chunk.n + 1)
                        if chunk.known and chunk.n == CHUNKS - 1:
                            before = chunk.back(1)
                            sp.wait_ge(ring_out.of(before), ring_out.done(before))
                        sp.dma_start(node_rows(out, start_of(chunk)), tiles(xbuf, chunk))\
                            .then_inc(ring_out.of(chunk), 16)

                sp.dma_start(tiles(xbuf, Item(0, 0)), node_rows(x, 0)).then_inc(ring_in.of(Item(0, 0)), 16)
                run_steps(sp, body, STEPS2, min(PAIRS, CHUNKS))
                ring_out.wait_all(sp, CHUNKS)
                for n in range(2):
                    sp.wait_ge(s_spill[n], 32 * (PAIRS // 2))

            @block.gpsimd
            def _(pool):
                def body(it):
                    chunk = it.back(-1)
                    if it.known and it.n == 0:
                        cadd(it)
                    if it.on(PAIRS):
                        p2 = it.ring(2)
                        after(pool, s_spill[p2], 32 * it.uses(2))
                        after(pool, s_rt, it.n - 1)
                        nc.gpsimd.tensor_copy(idx2[:, p2, 0:2], src_i[:, bass.ds(it.n * 2, 2)])
                        nc.gpsimd.tensor_copy(idx2[:, p2, 2:4], dst_i[:, bass.ds(it.n * 2, 2)]).then_inc(s_icp, 1)
                        pool.wait_ge(s_icp, it.n + 1)
                        pool.sem_inc(s_go, 1)
                        for k in range(4):
                            nc.gpsimd.indirect_dma_start(
                                out=rows2[:, p2, k * F:(k + 1) * F], out_offset=None, in_=x,
                                in_offset=bass.IndirectOffsetOnAxis(ap=idx2[:, p2, k:k + 1], axis=0))\
                                .then_inc(s_rows[p2], 16)
                    if chunk.on(CHUNKS):
                        cadd(chunk)
                    if it.back(2).on(CHUNKS):
                        dense.shift(pool, it.back(2))

                def cadd(chunk):
                    pool.wait_ge(ring_in.of(chunk), ring_in.done(chunk))
                    nc.gpsimd.tensor_tensor(tiles(xbuf, chunk), tiles(xbuf, chunk), bcast(bc["c"], NP, T), ALU.add)\
                        .then_inc(s_cadd, 1)
                run_steps(pool, body, STEPS2, min(PAIRS, CHUNKS))

            @block.vector
            def _(dve):
                def body(it):
                    if it.on(CHUNKS):
                        dve.wait_ge(s_cadd, it.n + 1)
                        norm1.dve_stats(dve, it)
                    if it.back(4).on(CHUNKS):
                        norm2.dve_shift(dve, it.back(4))
                    if it.back(2).on(CHUNKS):
                        dense.dve_z(dve, it.back(2))
                    if it.back(4).on(CHUNKS):
                        norm2.dve_apply(dve, it.back(4), 0, range(OUT_SPLIT, T))
                    if it.back(3).on(CHUNKS):
                        dense.dve_y(dve, it.back(3))
                    if it.back(3).on(CHUNKS):
                        norm2.dve_stats(dve, it.back(3))
                run_steps(dve, body, STEPS2, min(PAIRS, CHUNKS))

            @block.scalar
            def _(act):
                act.preload_act_table_set("natural_log_exp_and_others")

                def body(it):
                    chunk = it.back(1)
                    if chunk.on(CHUNKS):
                        dense.act_copy(act, chunk)
                    if it.back(4).on(CHUNKS):
                        norm2.act_apply(act, it.back(4), 0, range(OUT_SPLIT))
                    if chunk.on(PAIRS):
                        act.wait_ge(s_rt, chunk.n + 1)
                        after(act, s_sf, chunk.n)
                        nc.scalar.activation(rows2t[:, :], bank[6][:, 0:4 * EP], ACT.Copy).then_inc(s_rc, 1)
                    if it.on(CHUNKS):
                        norm1.act_rstd(act, it)
                    if chunk.on(CHUNKS):
                        dense.act_scales(act, chunk)
                    if it.on(CHUNKS):
                        norm1.act_scale(act, it, 0, range(T))
                    if it.back(3).on(CHUNKS):
                        norm2.act_rstd(act, it.back(3))
                    if it.back(2).on(CHUNKS):
                        dense.act_relu(act, it.back(2))
                    if chunk.on(PAIRS):
                        act.wait_ge(s_sf, chunk.n + 1)
                        got = bank[7][0:EP, 0:2 * (F + HEADS)].rearrange("p (k f) -> p k f", k=2)
                        nc.scalar.activation(
                            edge_feat[:, bass.ds(chunk.n * 2 * F, 2 * F)].rearrange("p (k f) -> p k f", k=2),
                            got[:, :, 0:F], ACT.Copy)
                        nc.scalar.activation(
                            scores[:, bass.ds(chunk.n * 2 * HEADS, 2 * HEADS)].rearrange("p (k f) -> p k f", k=2),
                            got[:, :, F:F + HEADS], ACT.Copy).then_inc(s_fc, 1)
                run_steps(act, body, STEPS2, min(PAIRS, CHUNKS))

            @block.tensor
            def _(pe):
                def body(it):
                    pair = it.back(1)
                    if it.back(1).on(CHUNKS):
                        pe.wait_ge(norm1.s_done_a[0], pair.n + 1)
                        dense.pe_transpose(pe, pair)
                    if pair.on(PAIRS):
                        pe.wait_ge(s_rows[pair.ring(2)], 64 * (pair.uses(2) + 1))
                        after(pe, s_rc, pair.n)
                        for k in range(4):
                            ins = nc.tensor.transpose(bank[6][:, k * EP:(k + 1) * EP],
                                                      tiles(rows2, pair)[:, k, :], ident[0:EP, 0:EP])
                        ins.then_inc(s_rt, 1)
                    if pair.on(CHUNKS):
                        dense.pe_products(pe, pair)
                    if pair.on(PAIRS):
                        pe.wait_ge(s_rc, pair.n + 1)
                        after(pe, s_fc, pair.n)
                        for k in range(2):
                            at = k * (F + HEADS)
                            nc.tensor.matmul(bank[7][0:EP, at:at + F + HEADS], rows2t[:, k * EP:(k + 1) * EP],
                                             w_gat[:, :], start=True, stop=False)
                            ins = nc.tensor.matmul(bank[7][0:EP, at + F:at + F + HEADS],
                                                   rows2t[:, (2 + k) * EP:(3 + k) * EP], v_er[:, :], start=False,
                                                   stop=True)
                        ins.then_inc(s_sf, 1)
                run_steps(pe, body, STEPS2, min(PAIRS, CHUNKS))

        ring_in.end_phase(CHUNKS)
        ring_out.end_phase(CHUNKS)

        take = carve()
        score, ex, den = (take(EP, HEADS + 1, EJ) for _ in range(3))
        run_f, run_all = take(EP, EJ), take(EP, EJ)
        diag = take(EP, 2, EP)
        junk3 = take(EP, EP)
        ends = take(EP, 2, 4)
        mx = take(EP, 8)
        s_dg, s_rows3, s_ex, s_en, s_tt = (sem(n) for n in (
            "ends_ready", "end_rows", "exps_ready", "sums_ready", "totals_ready"))
        with nc.Block() as block:
            @block.scalar
            def _(act):
                act.preload_act_table_set("natural_log_exp_and_others")
                act.wait_ge(s_ex, 1)
                nc.scalar.activation(ex[:, 0:HEADS, :], ex[:, 0:HEADS, :], ACT.Exp).then_inc(s_ex, 1)

            @block.tensor
            def _(pe):
                for n in range(HEADS + 1):
                    pe.wait_ge(s_dg, n + 1)
                    nc.tensor.matmul(bank[n][0:EP, 0:EP], ones[0:EP, 0:EP], diag[:, 0, :], start=True, stop=True)
                    nc.tensor.matmul(bank[n][0:EP, 128:128 + EP], ones[0:EP, 0:EP], diag[:, 1, :], start=True,
                                     stop=True).then_inc(s_rows3, 1)
                pe.wait_ge(s_en, 1)
                a, b = ends[:, 0, 0:HEADS + 1], ends[:, 1, 0:HEADS + 1]
                nc.tensor.matmul(bank[3][0:EP, 0:HEADS + 1], cross[:, 0, :], a, start=True, stop=False)
                nc.tensor.matmul(bank[3][0:EP, 0:HEADS + 1], cross_sum[:, 0, :], b, start=False, stop=True)
                nc.tensor.matmul(bank[3][0:EP, 8:9 + HEADS], cross[:, 1, :], a, start=True, stop=False)
                nc.tensor.matmul(bank[3][0:EP, 8:9 + HEADS], cross_sum[:, 1, :], b, start=False, stop=True)\
                    .then_inc(s_tt, 1)

            @block.vector
            def _(dve):
                V = nc.vector
                by_head = scores[:, :].rearrange("p (j h) -> p h j", h=HEADS)
                link(V.tensor_copy(score[:, 0:HEADS, :], by_head))
                link(V.scalar_tensor_tensor(out=score[:, 0:HEADS, :], in0=score[:, 0:HEADS, :], scalar=0.2,
                                            in1=score[:, 0:HEADS, :], op0=ALU.mult, op1=ALU.max))
                link(V.tensor_copy(score[:, HEADS, :], sc[1][:, :]))
                for n in range(HEADS + 1):
                    link(V.tensor_tensor_scan(run_f[:, :], pen_f[:, :], score[:, n, :], -BIG, ALU.add, ALU.max))
                    link(V.tensor_tensor_scan(run_all[:, ::-1], pen_b[:, ::-1], run_f[:, ::-1], -BIG, ALU.add, ALU.max))
                    link(V.tensor_scalar(diag[:, 0, :], ident[0:EP, 0:EP], run_all[:, 0:1], None, ALU.mult))
                    V.tensor_scalar(diag[:, 1, :], ident[0:EP, 0:EP], run_all[:, EJ - 1:EJ], None, ALU.mult)\
                        .then_inc(s_dg, 1)
                    dve.wait_ge(s_rows3, n + 1)
                    for q in range(4):
                        row = bank[n][0:EP, 128 * (q % 2):128 * (q % 2) + EP]
                        link(V.tensor_tensor_reduce(out=junk3[:, :], in0=cross_pen[:, q, :], in1=row, scale=1.0,
                                                    scalar=-BIG, op0=ALU.add, op1=ALU.max, accum_out=mx[:, q:q + 1]))
                    V.tensor_tensor(mx[:, 4:5], mx[:, 0:1], mx[:, 1:2], ALU.max)
                    link(V.tensor_tensor(mx[:, 5:6], mx[:, 2:3], mx[:, 3:4], ALU.max))
                    link(V.scalar_tensor_tensor(out=den[:, n, :], in0=pen_first[:, :], scalar=mx[:, 4:5],
                                                in1=run_all[:, :], op0=ALU.add, op1=ALU.max))
                    link(V.scalar_tensor_tensor(out=den[:, n, :], in0=pen_last[:, :], scalar=mx[:, 5:6],
                                                in1=den[:, n, :], op0=ALU.add, op1=ALU.max))
                V.tensor_copy(x1_idx[:, :], den[:, HEADS, :])
                V.tensor_tensor(ex[:, 0:HEADS, :], score[:, 0:HEADS, :], den[:, 0:HEADS, :], ALU.subtract)\
                    .then_inc(s_ex, 1)
                link(V.memset(ex[:, HEADS, :], 1.0))
                dve.wait_ge(s_ex, 2)
                for n in range(HEADS + 1):
                    link(V.tensor_tensor_scan(run_f[:, :], same[:, :], ex[:, n, :], 0.0, ALU.mult, ALU.add))
                    link(V.tensor_tensor_scan(den[:, n, ::-1], same_n[:, ::-1], run_f[:, ::-1], 0.0, ALU.mult, ALU.max))
                V.tensor_copy(ends[:, 0, 0:HEADS + 1], den[:, :, 0])
                V.tensor_copy(ends[:, 1, 0:HEADS + 1], den[:, :, EJ - 1]).then_inc(s_en, 1)
                dve.wait_ge(s_tt, 1)
                link(V.tensor_copy(mx[:, 0:3], bank[3][0:EP, 0:3]))
                link(V.tensor_copy(mx[:, 4:7], bank[3][0:EP, 8:11]))
                for n in range(HEADS + 1):
                    link(V.scalar_tensor_tensor(out=den[:, n, :], in0=first[:, :], scalar=mx[:, n:n + 1],
                                                in1=den[:, n, :], op0=ALU.mult, op1=ALU.max))
                    link(V.scalar_tensor_tensor(out=den[:, n, :], in0=in_last[:, :], scalar=mx[:, 4 + n:5 + n],
                                                in1=den[:, n, :], op0=ALU.mult, op1=ALU.max))
                link(V.tensor_scalar(den[:, HEADS, :], den[:, HEADS, :], 1e-8, None, ALU.add))
                link(V.reciprocal(den[:, :, :], den[:, :, :]))
                V.tensor_copy(rcnt[:, :], den[:, HEADS, :])
                link(V.tensor_tensor(alpha[:, :].rearrange("p (j h) -> p h j", h=HEADS), ex[:, 0:HEADS, :],
                                     den[:, 0:HEADS, :], ALU.mult))

        FC = 16
        BY_VECTOR = (0, 3, 6)
        by_feature = edge_feat[:, :].rearrange("p (j f) -> p f j", f=F)
        s_v, s_vd, s_f, s_cy = (sem(n) for n in ("weighted", "weighted_here", "summed", "carry_ready"))

        def weigh(eng, c):
            v = by_feature[:, c * FC:(c + 1) * FC, :]
            head = c * FC // FO
            w = alpha[:, :].rearrange("p (j h) -> p h j", h=HEADS)[:, head:head + 1, :]
            return eng.tensor_tensor(v, v, w.to_broadcast([EP, FC, EJ]), ALU.mult)

        def sum_runs(dve, s_done, c):
            with dve.Fori(0, FC // 4) as b:
                for u in range(4):
                    v = by_feature[:, bass.ds(b * 4 + (c * FC + u), 1), :].rearrange("p a j -> p (a j)")
                    nc.vector.tensor_tensor_scan(v, same[:, :], v, 0.0, ALU.mult, ALU.add).then_inc(s_done, 1)

        with nc.Block() as block:
            @block.gpsimd
            def _(pool):
                for c in range(F // FC):
                    if c not in BY_VECTOR:
                        weigh(nc.gpsimd, c).then_inc(s_v, 1)

            @block.vector
            def _(dve):
                for n, c in enumerate(BY_VECTOR):
                    weigh(nc.vector, c).then_inc(s_vd, 1)
                    dve.wait_ge(s_vd, n + 1)
                    sum_runs(dve, s_f, c)
                    for other in range(c + 1, (BY_VECTOR + (F // FC,))[n + 1]):
                        dve.wait_ge(s_v, other - n)
                        sum_runs(dve, s_f, other)
                dve.wait_ge(s_cy, 1)
                nc.vector.tensor_copy(carry[:, :], bank[0][0:EP, 0:F])

            @block.tensor
            def _(pe):
                pe.wait_ge(s_f, F)
                nc.tensor.matmul(bank[0][0:EP, 0:F], carry_lhs[:, :], edge_feat[:, (EJ - 1) * F:EJ * F], start=True,
                                 stop=True).then_inc(s_cy, 1)

        take = carve()
        gbuf, dbuf = take(EP, U, QT * F), take(EP, U, QT * F)
        ring_g = Ring("g_stored")
        s_tot, s_bias, s_gain, s_gg, s_uu = (sem(n) for n in ("total", "bias_added", "gained", "g_ready", "u_ready"))
        norm5 = Norm("norm5", EP, [(lambda it: tiles(gbuf, it), QT, 1, EG), (lambda it: tiles(dbuf, it), QT, 3, EG)])

        with nc.Block() as block:
            @block.sync
            def _(sp):
                def body(step):
                    it = step.back(-1)
                    if it.on(EG):
                        after(sp, ring_out.of(it), ring_out.before(it))
                        sp.dma_start(tiles(dbuf, it), edge_rows(xd_dram, it.n * QT, QT)).then_inc(ring_in.of(it), 16)
                    it = step.back(2)
                    if it.on(EG):
                        sp.wait_ge(s_gg, it.n + 1)
                        sp.dma_start(edge_rows(g_dram, it.n * QT, QT), tiles(gbuf, it)).then_inc(ring_g.of(it), 16)
                    it = step.back(4)
                    if it.on(EG):
                        sp.wait_ge(norm5.s_done_a[1], it.n + 1)
                        sp.dma_start(edge_rows(x1_dram, it.n * QT, QT), tiles(dbuf, it)).then_inc(ring_out.of(it), 16)
                sp.dma_start(tiles(dbuf, Item(0, 0)), edge_rows(xd_dram, 0, QT)).then_inc(ring_in.of(Item(0, 0)), 16)
                run_steps(sp, body, EG + 4, EG)
                ring_g.wait_all(sp, EG)
                ring_out.wait_all(sp, EG)

            @block.vector
            def _(dve):
                V = nc.vector

                def body(it):
                    if it.back(1).on(EG):
                        dve.wait_ge(s_bias, it.back(1).n + 1)
                    if it.back(3).on(EG):
                        dve.wait_ge(s_uu, it.back(3).n + 1)
                    if norm5.on(it):
                        norm5.dve_stats(dve, it)
                    if it.on(EG):
                        after(dve, ring_g.of(it), ring_g.before(it))
                        for t in range(QT):
                            j = it.n * QT + t
                            ins = V.scalar_tensor_tensor(out=tiles(gbuf, it)[:, t, :], in0=carry[:, :],
                                                         scalar=first[:, bass.ds(j, 1)],
                                                         in1=edge_feat[:, bass.ds(j * F, F)], op0=ALU.mult, op1=ALU.add)
                        ins.then_inc(s_tot, 1)
                    if norm5.on(it):
                        norm5.dve_shift(dve, it)
                    if it.on(EG):
                        dve.wait_ge(s_tot, it.n + 1)
                        V.tensor_tensor(tiles(gbuf, it), tiles(gbuf, it), bcast(bc["bias"], EP, QT), ALU.add)\
                            .then_inc(s_bias, 1)
                run_steps(dve, body, EG + 3, EG)

            @block.scalar
            def _(act):
                act.preload_act_table_set("natural_log_exp_and_others")

                def body(it):
                    if norm5.on(it):
                        norm5.act_rstd(act, it)
                    norm5.act_apply(act, it, 0, range(QT))
                    norm5.act_apply(act, it, 1, range(QT))
                run_steps(act, body, EG + 3, EG)

            @block.gpsimd
            def _(pool):
                G = nc.gpsimd

                def body(it):
                    it = it.back(2)
                    if it.on(EG):
                        g, u = tiles(gbuf, it), tiles(dbuf, it)
                        pool.wait_ge(norm5.s_done_a[0], it.n + 1)
                        G.tensor_tensor(g, g, bcast(bc["gamma"], EP, QT), ALU.mult).then_inc(s_gain, 1)
                        pool.wait_ge(s_gain, it.n + 1)
                        G.tensor_tensor(g, g, bcast(bc["beta"], EP, QT), ALU.add).then_inc(s_gg, 1)
                        pool.wait_ge(s_gg, it.n + 1)
                        pool.wait_ge(ring_in.of(it), ring_in.done(it))
                        G.tensor_tensor(u, u, g, ALU.add).then_inc(s_uu, 1)
                run_steps(pool, body, EG + 2, EG)

        ring_in.end_phase(EG)

        take = carve()
        sbuf = take(EP, U, QT * F)
        grow, drow = take(EP, 3, QT * F), take(EP, 3, QT * F)
        z6 = take(EP, 2, QT * F)
        xt6, mt6 = ([take(128, QT * EP) for _ in range(2)] for _ in range(2))
        junk6 = take(EP, QT * F // 2).bitcast(bf16).rearrange("p (k f) -> p k f", f=F)
        idx6 = sb("idx6", [EP, 3, 2 * QT], i32)
        norm_s = Norm("norm_s", EP, [(lambda it: tiles(sbuf, it), QT, 0, EG)])
        msg = Layer("msg", EP, QT, lambda it: tiles(sbuf, it), lambda it: tiles(z6, it), xt6, junk6, [[2], [3]],
                    (w_ma, w_mb, bias_m, bc["mg"], bc["mbeta"]), m_of=lambda it: tiles(drow, it), mt=mt6)
        s_gin = [sem(f"gathered{n}") for n in range(3)]
        s_icp6, s_u6, s_w6, s_f6, s_cy6 = (sem(n) for n in (
            "idx6_copied", "m_u", "m_weighted", "m_summed", "carry6_ready"))
        with nc.Block() as block:
            @block.sync
            def _(sp):
                def body(step):
                    it = step.back(-1)
                    if it.on(EG):
                        after(sp, msg.s["transposed"], it.n - U + 1)
                        sp.dma_start(tiles(sbuf, it), edge_rows(xs_dram, it.n * QT, QT)).then_inc(ring_in.of(it), 16)
                sp.dma_start(tiles(sbuf, Item(0, 0)), edge_rows(xs_dram, 0, QT)).then_inc(ring_in.of(Item(0, 0)), 16)
                run_steps(sp, body, EG, EG)

            @block.gpsimd
            def _(pool):
                def body(it):
                    r3 = it.ring(3)
                    after(pool, msg.s["transposed"], it.n - 2)
                    after(pool, s_gin[r3], 16 * 2 * QT * it.uses(3))
                    cols = idx6[:, r3, :]
                    nc.gpsimd.tensor_copy(cols[:, 0:QT], g_idx[:, bass.ds(it.n * QT, QT)])
                    nc.gpsimd.tensor_copy(cols[:, QT:2 * QT], x1_idx[:, bass.ds(it.n * QT, QT)]).then_inc(s_icp6, 1)
                    pool.wait_ge(s_icp6, it.n + 1)
                    pool.sem_inc(s_go, 1)
                    for k in range(2 * QT):
                        rows, table = (grow, g_dram) if k < QT else (drow, x1_dram)
                        nc.gpsimd.indirect_dma_start(
                            out=rows[:, r3, (k % QT) * F:(k % QT + 1) * F], out_offset=None, in_=table,
                            in_offset=bass.IndirectOffsetOnAxis(ap=cols[:, k:k + 1], axis=0))\
                            .then_inc(s_gin[r3], 16)
                run_steps(pool, body, EG, EG)

            @block.vector
            def _(dve):
                V = nc.vector

                def body(it):
                    new, old = it.back(1), it.back(3)
                    if new.on(EG):
                        dve.wait_ge(ring_in.of(new), ring_in.done(new))
                        dve.wait_ge(s_gin[new.ring(3)], 16 * 2 * QT * (new.uses(3) + 1))
                        V.tensor_tensor(tiles(sbuf, new), tiles(sbuf, new), tiles(grow, new), ALU.add)\
                            .then_inc(s_u6, 1)
                        dve.wait_ge(s_u6, new.n + 1)
                        norm_s.dve_stats(dve, new)
                    if old.on(EG):
                        msg.dve_z(dve, old)
                        msg.shift(nc.vector, old)
                    if new.on(EG):
                        norm_s.dve_shift(dve, new)
                    if old.on(EG):
                        dve.wait_ge(msg.s["shifted"], old.n + 1)
                        z = tiles(z6, old)

                        def weigh_message(t):
                            V.tensor_scalar(z[:, t, :], z[:, t, :], 0.0, w_edge[:, bass.ds(old.n * QT + t, 1)],
                                            ALU.max, ALU.mult).then_inc(s_w6, 1)

                        def add_message(t):
                            j = old.n * QT + t
                            dve.wait_ge(s_w6, j + 1)
                            after(dve, s_f6, j)
                            here = edge_feat[:, bass.ds(j * F, F)]
                            if old.known and j == 0:
                                ins = V.tensor_copy(here, z[:, t, :])
                            else:
                                ins = V.scalar_tensor_tensor(out=here, in0=edge_feat[:, bass.ds((j - 1) * F, F)],
                                                             scalar=same[:, bass.ds(j, 1)], in1=z[:, t, :],
                                                             op0=ALU.mult, op1=ALU.add)
                            ins.then_inc(s_f6, 1)

                        weigh_message(0)
                        for t in range(QT):
                            if t + 1 < QT:
                                weigh_message(t + 1)
                            add_message(t)
                run_steps(dve, body, EG + 3, EG)
                dve.wait_ge(s_cy6, 1)
                V.tensor_copy(carry[:, :], bank[4][0:EP, 0:F])

            @block.scalar
            def _(act):
                act.preload_act_table_set("natural_log_exp_and_others")

                def body(it):
                    new, old = it.back(1), it.back(2)
                    if new.on(EG):
                        norm_s.act_rstd(act, new)
                        norm_s.act_apply(act, new, 0, range(QT))
                    if old.on(EG):
                        msg.act_scales(act, old)
                    if new.on(EG):
                        msg.act_copy(act, new)
                run_steps(act, body, EG + 2, EG)

            @block.tensor
            def _(pe):
                def body(it):
                    it = it.back(1)
                    if it.on(EG):
                        pe.wait_ge(norm_s.s_done_a[0], it.n + 1)
                        msg.pe_transpose(pe, it)
                        msg.pe_products(pe, it)
                run_steps(pe, body, EG + 1, EG)
                pe.wait_ge(s_f6, EJ)
                nc.tensor.matmul(bank[4][0:EP, 0:F], carry_lhs[:, :], edge_feat[:, (EJ - 1) * F:EJ * F], start=True,
                                 stop=True).then_inc(s_cy6, 1)

        ring_in.end_phase(EG)

        take = carve()
        ubuf, mbuf = take(EP, U, QT * F), take(EP, 3, QT * F)
        z7 = take(EP, 2, QT * F)
        xt7, mt7 = ([take(128, QT * EP) for _ in range(2)] for _ in range(2))
        junk7 = take(EP, QT * F // 2).bitcast(bf16).rearrange("p (k f) -> p k f", f=F)
        idx7 = sb("idx7", [EP, U, QT], i32)
        norm7 = Norm("norm7", EP, [(lambda it: tiles(ubuf, it), QT, 0, EG)], factor=True)
        upd = Layer("upd", EP, QT, lambda it: tiles(ubuf, it), lambda it: tiles(z7, it), xt7, junk7, [[2, 3], [4, 5]],
                    (w_ut, w_ub, bias_u, bc["ug"], bc["ubeta"]), m_of=lambda it: tiles(mbuf, it), mt=mt7,
                    g2_of=lambda it: norm7.factors[0:EP, it.ring(2), :])
        ring_scatter = Ring("scattered", unit=16 * QT)
        s_icp7, s_tot7, s_m7 = (sem(n) for n in ("idx7_copied", "message_total", "message_mean"))
        with nc.Block() as block:
            @block.sync
            def _(sp):
                def body(step):
                    it = step.back(-1)
                    if it.on(EG):
                        after(sp, ring_scatter.of(it), ring_scatter.before(it))
                        sp.dma_start(tiles(ubuf, it), edge_rows(x1_dram, it.n * QT, QT)).then_inc(ring_in.of(it), 16)
                sp.dma_start(tiles(ubuf, Item(0, 0)), edge_rows(x1_dram, 0, QT)).then_inc(ring_in.of(Item(0, 0)), 16)
                run_steps(sp, body, EG, EG)

            @block.vector
            def _(dve):
                V = nc.vector

                def body(it):
                    if it.on(EG):
                        after(dve, upd.s["transposed"], it.n - 2)
                        for t in range(QT):
                            j = it.n * QT + t
                            ins = V.scalar_tensor_tensor(out=tiles(mbuf, it)[:, t, :], in0=carry[:, :],
                                                         scalar=first[:, bass.ds(j, 1)],
                                                         in1=edge_feat[:, bass.ds(j * F, F)], op0=ALU.mult, op1=ALU.add)
                        ins.then_inc(s_tot7, 1)
                    if it.back(4).on(EG):
                        norm7.dve_shift(dve, it.back(4))
                    if it.back(2).on(EG):
                        upd.dve_z(dve, it.back(2))
                    if it.back(4).on(EG):
                        norm7.dve_apply(dve, it.back(4), 0, range(QT // 2, QT))
                    if it.back(3).on(EG):
                        upd.dve_y(dve, it.back(3))
                        norm7.dve_stats(dve, it.back(3))
                run_steps(dve, body, EG + 4, EG)

            @block.scalar
            def _(act):
                act.preload_act_table_set("natural_log_exp_and_others")

                def body(it):
                    if it.back(1).on(EG):
                        upd.act_copy(act, it.back(1))
                    if it.back(4).on(EG):
                        norm7.act_apply(act, it.back(4), 0, range(QT // 2))
                    if it.on(EG):
                        act.wait_ge(s_tot7, it.n + 1)
                        for t in range(QT):
                            m = tiles(mbuf, it)[:, t, :]
                            ins = nc.scalar.activation(m, m, ACT.Copy, scale=rcnt[:, bass.ds(it.n * QT + t, 1)])
                        ins.then_inc(s_m7, 1)
                    if it.back(1).on(EG):
                        upd.act_scales(act, it.back(1))
                    if it.back(2).on(EG):
                        upd.act_relu(act, it.back(2))
                    if it.back(3).on(EG):
                        norm7.act_rstd(act, it.back(3))
                run_steps(act, body, EG + 4, EG)

            @block.tensor
            def _(pe):
                def body(it):
                    it = it.back(1)
                    if it.on(EG):
                        pe.wait_ge(ring_in.of(it), ring_in.done(it))
                        pe.wait_ge(s_m7, it.n + 1)
                        upd.pe_transpose(pe, it)
                        upd.pe_products(pe, it)
                run_steps(pe, body, EG + 1, EG)

            @block.gpsimd
            def _(pool):
                def body(it):
                    if it.on(EG):
                        after(pool, ring_scatter.of(it), ring_scatter.before(it))
                        nc.gpsimd.tensor_copy(idx7[:, it.slot, :], out_idx[:, bass.ds(it.n * QT, QT)])\
                            .then_inc(s_icp7, 1)
                    if it.back(2).on(EG):
                        upd.shift(pool, it.back(2))
                    it = it.back(4)
                    if it.on(EG):
                        pool.wait_ge(s_icp7, it.n + 1)
                        pool.wait_ge(norm7.s_done_v[0], it.n + 1)
                        pool.wait_ge(norm7.s_done_a[0], it.n + 1)
                        pool.sem_inc(s_go, 1)
                        for k in range(QT):
                            nc.gpsimd.indirect_dma_start(
                                out=out, out_offset=bass.IndirectOffsetOnAxis(ap=idx7[:, it.slot, k:k + 1], axis=0),
                                in_=ubuf[:, it.slot, k * F:(k + 1) * F], in_offset=None, bounds_check=N - 1,
                                oob_is_err=False).then_inc(ring_scatter.of(it), 16)
                run_steps(pool, body, EG + 4, EG)
                ring_scatter.wait_all(pool, EG)


_INS = ['x', 'src', 'dst', 'edge_weight', 'L0_gnn_W', 'L0_gnn_attn_l', 'L0_gnn_attn_r', 'L0_gnn_bias', 'L0_gnn_gamma',
        'L0_gnn_beta', 'L1_gnn_msg_w', 'L1_gnn_msg_b', 'L1_gnn_msg_g', 'L1_gnn_msg_beta', 'L1_gnn_upd_w',
        'L1_gnn_upd_b', 'L1_gnn_upd_g', 'L1_gnn_upd_beta', 'L1_gnn_gate_w', 'L1_gnn_gate_b']


def kernel(**inputs):
    import numpy as np
    import concourse.bacc as bacc
    from concourse.bass_utils import run_bass_kernel_spmd

    nc = bacc.Bacc("TRN2", target_bir_lowering=False, num_devices=1)
    arrays, args = {}, []
    for name in _INS:
        a = np.ascontiguousarray(inputs[name])
        arrays["in_" + name] = a
        args.append(nc.dram_tensor("in_" + name, a.shape, mybir.dt.from_np(a.dtype), kind="ExternalInput").ap())
    shape = np.asarray(inputs['x']).shape
    args.append(nc.dram_tensor("out_rows", shape, mybir.dt.float32, kind="ExternalOutput").ap())
    gnn_resnorm_kernel(nc, *args)
    r = run_bass_kernel_spmd(nc, [arrays], core_ids=[0])
    return r.results[0]["out_rows"]
```
